# Optimizing a Trainium2 kernel written in Bass

```python
import numpy as np
import jax
import jax.numpy as jnp

def _softmax(x, axis=-1):
    return jax.nn.softmax(x, axis=axis)

def _gelu(x):
    return jax.nn.gelu(x, approximate=True)

def _silu(x):
    return jax.nn.silu(x)

def _sigmoid(x):
    return jax.nn.sigmoid(x)

def _layernorm(x, axis=-1, eps=1e-05):
    m = jnp.mean(x, axis=axis, keepdims=True)
    v = jnp.var(x, axis=axis, keepdims=True)
    return (x - m) / jnp.sqrt(v + eps)

def _scatter_add(tgt, idx, src, axis=0):
    return tgt.at[idx].add(src)

def _segment_sum(src, seg, n):
    return jax.ops.segment_sum(src, seg, n)
kernel_name = 'mk_seq_preln_d1_jaxref_r8_a874c9'

def setup_inputs(seed: int=0):
    np.random.seed(seed)
    _w = jnp.asarray

    def _L0_attn_setup():
        import jax, jax.numpy as jnp
        import numpy as np
        B, T, C = (4, 512, 128)
        H = 16
        D = C // H
        W_SCALE = 0.02
        key = jax.random.key(seed)
        ks = jax.random.split(key, 9)
        inp = {'x': jax.random.normal(ks[0], (B, T, C), dtype=jnp.float32)}
        for i, nm in enumerate(['q', 'k', 'v', 'o']):
            inp[f'W{nm}'] = jax.random.normal(ks[1 + i], (C, C), dtype=jnp.float32) * W_SCALE
            inp[f'b{nm}'] = jnp.zeros((C,), dtype=jnp.float32)
        return inp
    _L0_attn_in = _L0_attn_setup()

    def _L0_ffn_setup():
        import jax, jax.numpy as jnp
        import numpy as np
        DIM = 128
        DEPTH = 6
        HEADS = 16
        DIM_HEAD = 64
        WINDOW = 32
        INNER = HEADS * DIM_HEAD
        DIM_INNER = int(DIM * 4 * 2 / 3)
        QK_SCALE = 8.0

        def shift_tokens(t):
            a, s = jnp.split(t, 2, -1)
            s = jnp.pad(s, ((0, 0), (1, 0), (0, 0)))[:, :-1]
            return jnp.concatenate([a, s], -1)

        def l2norm(t):
            return t / jnp.maximum(jnp.linalg.norm(t, axis=-1, keepdims=True), 1e-12)

        def rotate_half(x):
            x1, x2 = jnp.split(x, 2, -1)
            return jnp.concatenate([-x2, x1], -1)

        def rotary_tables(n):
            half = jnp.arange(0, DIM_HEAD, 2, dtype=jnp.float32)
            inv_freq = 1.0 / 10000.0 ** (half / DIM_HEAD)
            t = jnp.arange(n, dtype=jnp.float32)
            freqs = t[:, None] * inv_freq[None, :]
            freqs = jnp.concatenate([freqs, freqs], -1)
            base_scale = (half + 0.4 * DIM_HEAD) / (1.4 * DIM_HEAD)
            power = (t - n // 2) / (WINDOW // 2)
            scale = base_scale[None, :] ** power[:, None]
            scale = jnp.concatenate([scale, scale], -1)
            return (freqs, scale)

        def local_attention(q, k, v):
            b, h, n, d = q.shape
            w = WINDOW
            nw = n // w
            bq = q.reshape(b, h, nw, w, d)
            bk = k.reshape(b, h, nw, w, d)
            bv = v.reshape(b, h, nw, w, d)

            def look(t):
                p = jnp.pad(t, ((0, 0), (0, 0), (1, 0), (0, 0), (0, 0)))
                return jnp.concatenate([p[:, :, :nw], p[:, :, 1:]], axis=3)
            bk2, bv2 = (look(bk), look(bv))
            seq = jnp.arange(n).reshape(nw, w)
            seq_p = jnp.pad(seq, ((1, 0), (0, 0)), constant_values=-1)
            jt = jnp.concatenate([seq_p[:nw], seq_p[1:]], axis=1)
            it = seq[:, :, None]
            jb = jt[:, None, :]
            mask = (it < jb) | (it > jb + w) | (jb == -1)
            sim = jnp.einsum('bhwie,bhwje->bhwij', bq, bk2) * QK_SCALE
            sim = jnp.where(mask, -jnp.finfo(sim.dtype).max, sim)
            attn = jax.nn.softmax(sim, -1)
            out = jnp.einsum('bhwij,bhwje->bhwie', attn, bv2)
            return out.reshape(b, h, n, d)

        def attn_layer(x, Wqkv, qs, ksc, Wo):
            b, n, _ = x.shape
            qkv = x @ Wqkv
            q, k, v = jnp.split(qkv, 3, -1)
            sh = lambda t: t.reshape(b, n, HEADS, DIM_HEAD).transpose(0, 2, 1, 3)
            q, k, v = (sh(q), sh(k), sh(v))
            q = l2norm(q) * qs
            k = l2norm(k) * ksc
            freqs, scale = rotary_tables(n)
            cos, sin = (jnp.cos(freqs), jnp.sin(freqs))
            q = q * cos * scale + rotate_half(q) * sin * scale
            inv = 1.0 / scale
            k = k * cos * inv + rotate_half(k) * sin * inv
            out = local_attention(q, k, v)
            out = out.transpose(0, 2, 1, 3).reshape(b, n, INNER)
            return out @ Wo

        def ffn_layer(x, g, bln, W1, b1, W2, b2):
            mu = x.mean(-1, keepdims=True)
            var = ((x - mu) ** 2).mean(-1, keepdims=True)
            xn = (x - mu) / jnp.sqrt(var + 1e-05) * g + bln
            hg = xn @ W1 + b1
            a, gate = jnp.split(hg, 2, -1)
            return a * jax.nn.gelu(gate, approximate=False) @ W2 + b2
        key = jax.random.key(seed)
        ks = jax.random.split(key, 8)
        B, N = (2, 256)
        init = lambda k, shape: jax.random.normal(k, shape, jnp.float32) * 0.02
        return {'x': jax.random.normal(ks[0], (B, N, DIM), jnp.float32), 'Wqkv': init(ks[1], (DEPTH, DIM, 3 * INNER)), 'q_scale': jnp.ones((DEPTH, DIM_HEAD), jnp.float32), 'k_scale': jnp.ones((DEPTH, DIM_HEAD), jnp.float32), 'Wo': init(ks[2], (DEPTH, INNER, DIM)), 'ln_g': jnp.ones((DEPTH, DIM), jnp.float32), 'ln_b': jnp.zeros((DEPTH, DIM), jnp.float32), 'W1': init(ks[3], (DEPTH, DIM, 2 * DIM_INNER)), 'b1': jnp.zeros((DEPTH, 2 * DIM_INNER), jnp.float32), 'W2': init(ks[4], (DEPTH, DIM_INNER, DIM)), 'b2': jnp.zeros((DEPTH, DIM), jnp.float32)}
    _L0_ffn_in = _L0_ffn_setup()
    _d = {'L0_attn_x': _L0_attn_in['x'], 'L0_attn_Wq': _L0_attn_in['Wq'], 'L0_attn_bq': _L0_attn_in['bq'], 'L0_attn_Wk': _L0_attn_in['Wk'], 'L0_attn_bk': _L0_attn_in['bk'], 'L0_attn_Wv': _L0_attn_in['Wv'], 'L0_attn_bv': _L0_attn_in['bv'], 'L0_attn_Wo': _L0_attn_in['Wo'], 'L0_attn_bo': _L0_attn_in['bo'], 'L0_ffn_Wqkv': _L0_ffn_in['Wqkv'], 'L0_ffn_q_scale': _L0_ffn_in['q_scale'], 'L0_ffn_k_scale': _L0_ffn_in['k_scale'], 'L0_ffn_Wo': _L0_ffn_in['Wo'], 'L0_ffn_ln_g': _L0_ffn_in['ln_g'], 'L0_ffn_ln_b': _L0_ffn_in['ln_b'], 'L0_ffn_W1': _L0_ffn_in['W1'], 'L0_ffn_b1': _L0_ffn_in['b1'], 'L0_ffn_W2': _L0_ffn_in['W2'], 'L0_ffn_b2': _L0_ffn_in['b2']}
    _x0 = _d['L0_attn_x']
    _d['L0_attn_x'] = jax.random.normal(jax.random.fold_in(jax.random.key(seed), 1), (4, 1024, 128), dtype=_x0.dtype)
    del _x0
    return _d

def reference(L0_attn_x, L0_attn_Wq, L0_attn_bq, L0_attn_Wk, L0_attn_bk, L0_attn_Wv, L0_attn_bv, L0_attn_Wo, L0_attn_bo, L0_ffn_Wqkv, L0_ffn_q_scale, L0_ffn_k_scale, L0_ffn_Wo, L0_ffn_ln_g, L0_ffn_ln_b, L0_ffn_W1, L0_ffn_b1, L0_ffn_W2, L0_ffn_b2):

    def _L0_attn_ref(x, Wq, bq, Wk, bk, Wv, bv, Wo, bo):
        import jax, jax.numpy as jnp
        import numpy as np
        B, T, C = (4, 512, 128)
        H = 16
        D = C // H
        W_SCALE = 0.02
        Bx, Tx, Cx = x.shape
        q = (x @ Wq.T + bq).reshape(Bx, Tx, H, D)
        k = (x @ Wk.T + bk).reshape(Bx, Tx, H, D)
        v = (x @ Wv.T + bv).reshape(Bx, Tx, H, D)
        q = jax.nn.elu(q) + 1.0
        k = jax.nn.elu(k) + 1.0
        kv = jnp.einsum('bthd,bthe->bhde', k, v)
        denom = jnp.einsum('bthd,bhd->bth', q, k.sum(axis=1))
        num = jnp.einsum('bthd,bhde->bthe', q, kv)
        out = num / jnp.clip(denom, 1e-06, None)[..., None]
        out = out.reshape(Bx, Tx, Cx)
        return out @ Wo.T + bo

    def _L0_ffn_ref(x, Wqkv, q_scale, k_scale, Wo, ln_g, ln_b, W1, b1, W2, b2):
        import jax, jax.numpy as jnp
        import numpy as np
        DIM = 128
        DEPTH = 6
        HEADS = 16
        DIM_HEAD = 64
        WINDOW = 32
        INNER = HEADS * DIM_HEAD
        DIM_INNER = int(DIM * 4 * 2 / 3)
        QK_SCALE = 8.0

        def shift_tokens(t):
            a, s = jnp.split(t, 2, -1)
            s = jnp.pad(s, ((0, 0), (1, 0), (0, 0)))[:, :-1]
            return jnp.concatenate([a, s], -1)

        def l2norm(t):
            return t / jnp.maximum(jnp.linalg.norm(t, axis=-1, keepdims=True), 1e-12)

        def rotate_half(x):
            x1, x2 = jnp.split(x, 2, -1)
            return jnp.concatenate([-x2, x1], -1)

        def rotary_tables(n):
            half = jnp.arange(0, DIM_HEAD, 2, dtype=jnp.float32)
            inv_freq = 1.0 / 10000.0 ** (half / DIM_HEAD)
            t = jnp.arange(n, dtype=jnp.float32)
            freqs = t[:, None] * inv_freq[None, :]
            freqs = jnp.concatenate([freqs, freqs], -1)
            base_scale = (half + 0.4 * DIM_HEAD) / (1.4 * DIM_HEAD)
            power = (t - n // 2) / (WINDOW // 2)
            scale = base_scale[None, :] ** power[:, None]
            scale = jnp.concatenate([scale, scale], -1)
            return (freqs, scale)

        def local_attention(q, k, v):
            b, h, n, d = q.shape
            w = WINDOW
            nw = n // w
            bq = q.reshape(b, h, nw, w, d)
            bk = k.reshape(b, h, nw, w, d)
            bv = v.reshape(b, h, nw, w, d)

            def look(t):
                p = jnp.pad(t, ((0, 0), (0, 0), (1, 0), (0, 0), (0, 0)))
                return jnp.concatenate([p[:, :, :nw], p[:, :, 1:]], axis=3)
            bk2, bv2 = (look(bk), look(bv))
            seq = jnp.arange(n).reshape(nw, w)
            seq_p = jnp.pad(seq, ((1, 0), (0, 0)), constant_values=-1)
            jt = jnp.concatenate([seq_p[:nw], seq_p[1:]], axis=1)
            it = seq[:, :, None]
            jb = jt[:, None, :]
            mask = (it < jb) | (it > jb + w) | (jb == -1)
            sim = jnp.einsum('bhwie,bhwje->bhwij', bq, bk2) * QK_SCALE
            sim = jnp.where(mask, -jnp.finfo(sim.dtype).max, sim)
            attn = jax.nn.softmax(sim, -1)
            out = jnp.einsum('bhwij,bhwje->bhwie', attn, bv2)
            return out.reshape(b, h, n, d)

        def attn_layer(x, Wqkv, qs, ksc, Wo):
            b, n, _ = x.shape
            qkv = x @ Wqkv
            q, k, v = jnp.split(qkv, 3, -1)
            sh = lambda t: t.reshape(b, n, HEADS, DIM_HEAD).transpose(0, 2, 1, 3)
            q, k, v = (sh(q), sh(k), sh(v))
            q = l2norm(q) * qs
            k = l2norm(k) * ksc
            freqs, scale = rotary_tables(n)
            cos, sin = (jnp.cos(freqs), jnp.sin(freqs))
            q = q * cos * scale + rotate_half(q) * sin * scale
            inv = 1.0 / scale
            k = k * cos * inv + rotate_half(k) * sin * inv
            out = local_attention(q, k, v)
            out = out.transpose(0, 2, 1, 3).reshape(b, n, INNER)
            return out @ Wo

        def ffn_layer(x, g, bln, W1, b1, W2, b2):
            mu = x.mean(-1, keepdims=True)
            var = ((x - mu) ** 2).mean(-1, keepdims=True)
            xn = (x - mu) / jnp.sqrt(var + 1e-05) * g + bln
            hg = xn @ W1 + b1
            a, gate = jnp.split(hg, 2, -1)
            return a * jax.nn.gelu(gate, approximate=False) @ W2 + b2
        for i in range(DEPTH):
            x = attn_layer(shift_tokens(x), Wqkv[i], q_scale[i], k_scale[i], Wo[i]) + x
            x = ffn_layer(shift_tokens(x), ln_g[i], ln_b[i], W1[i], b1[i], W2[i], b2[i]) + x
        return x
    x = L0_attn_x
    x = x + _L0_attn_ref(_layernorm(x, axis=-1), L0_attn_Wq, L0_attn_bq, L0_attn_Wk, L0_attn_bk, L0_attn_Wv, L0_attn_bv, L0_attn_Wo, L0_attn_bo)
    x = x + _L0_ffn_ref(_layernorm(x, axis=-1), L0_ffn_Wqkv, L0_ffn_q_scale, L0_ffn_k_scale, L0_ffn_Wo, L0_ffn_ln_g, L0_ffn_ln_b, L0_ffn_W1, L0_ffn_b1, L0_ffn_W2, L0_ffn_b2)
    return x

_drawn_inputs = setup_inputs


def setup_inputs(seed=0):
    import zlib

    import numpy as np

    out = dict(_drawn_inputs(seed))
    spreads = {'L0_attn_bq': (0.0, 2.0),
     'L0_attn_bk': (0.0, 2.0),
     'L0_attn_bv': (0.0, 0.371),
     'L0_attn_bo': (0.0, 0.1),
     'L0_ffn_q_scale': (1.0, 0.6),
     'L0_ffn_k_scale': (1.0, 0.6),
     'L0_ffn_ln_g': (1.0, 0.6),
     'L0_ffn_ln_b': (0.0, 0.8),
     'L0_ffn_b1': (0.0, 0.8),
     'L0_ffn_b2': (0.0, 0.1)}
    factors = {'L0_attn_Wq': 36.224,
     'L0_attn_Wk': 22.848,
     'L0_attn_Wv': 8.0,
     'L0_ffn_W1': 3.626,
     'L0_ffn_W2': 3.575}
    for name, (base, spread) in spreads.items():
        noise = np.random.default_rng([zlib.crc32(name.encode()), seed]).standard_normal(out[name].shape)
        drawn = base * np.exp(spread * noise) if base else spread * noise
        out[name] = jnp.asarray(drawn.astype(out[name].dtype))
    for name, factor in factors.items():
        out[name] = (out[name] * factor).astype(out[name].dtype)
    return out
```

```python
from contextlib import ExitStack

import numpy as np

import concourse.bass as bass
from concourse import mybir

F32 = mybir.dt.float32
I32 = mybir.dt.int32
BF16 = mybir.dt.bfloat16
ACT = mybir.ActivationFunctionType
ALU = mybir.AluOpType
AX = mybir.AxisListType.X

P = 128
B, N, C = 4, 1024, 128
TPB = N // P
NT = B * TPB
DEPTH, H, D, WIN = 6, 16, 64, 32
PAIRS = H // 2
QUADS = H // 4
NW = P // WIN
INNER = H * D
F = int(C * 4 * 2 / 3)
FB = [(0, 128), (128, 128), (256, F - 256)]
FT = 4
NG = NT // FT
H0, D0 = 16, 8
EPS = 1e-5
NEG = -1e30
RING = WIN + 2 * P
RSQRT_MAGIC = 1597463007.0
RSQRT_OPS = 12
NORM_STEPS = RSQRT_OPS + 2
LN_STEPS = RSQRT_OPS + 4


def rotary_constants():
    f = np.float32
    half = np.arange(0, D, 2, dtype=f)
    inv_freq = f(1.0) / np.power(f(10000.0), half / f(D), dtype=f)
    t = np.arange(N, dtype=f)
    freqs = np.concatenate([t[:, None] * inv_freq[None]] * 2, -1)
    base = (half + f(0.4 * D)) / f(1.4 * D)
    power = (t - N // 2) / f(WIN // 2)
    scale = np.power(base[None], power[:, None], dtype=f)
    scale = np.concatenate([scale, scale], -1)
    inv = f(1.0) / scale
    sign = np.where(np.arange(D) < D // 2, f(1), f(-1))[None]
    cos, sin = np.cos(freqs), np.sin(freqs) * sign
    qk_scale = f(8.0)
    tab = np.stack([cos * scale * qk_scale, sin * scale * qk_scale, cos * inv, sin * inv])
    return tab.reshape(4, TPB, P, D).transpose(2, 0, 1, 3).reshape(P, -1).astype(f)


def constants():
    f = np.float32
    parts = {"ident": np.eye(P, dtype=f)}
    parts["shift"] = np.eye(P, k=1, dtype=f)
    carry = np.zeros((P, P), f)
    carry[P - 1, 0] = 1
    parts["carry"] = carry
    r, c = np.arange(P)[:, None] % WIN, np.arange(WIN)[None]
    mask = np.concatenate([np.where(r > c, f(NEG), f(0)), np.where(c > r, f(NEG), f(0))], 1)
    first = mask.copy()
    first[0:WIN, 0:WIN] = NEG
    parts["mask"] = np.concatenate([first] + [mask] * (TPB // 2 - 1), 1)
    parts["keep"] = np.tile((np.arange(TPB // 2) > 0).astype(f)[None], (P, 1))
    h = np.arange(P) // D0
    parts["blocks"] = (h[:, None] == h[None]).astype(f)
    parts["heads"] = (h[:, None] == np.arange(H0)[None]).astype(f)
    parts["rotary"] = rotary_constants()
    at, n = {}, 0
    for k, v in parts.items():
        at[k] = (n, v.shape[1])
        n += v.shape[1]
    return np.concatenate(list(parts.values()), 1), at


def build(nc, consts, at, x, Wq, bq, Wk, bk, Wv, bv, Wo, bo, Wqkv, q_scale, k_scale, Wout,
          ln_g, ln_b, W1, b1, W2, b2, out):
    ctx = ExitStack()
    with ctx:
        def sb(name, shape, dt=F32):
            return ctx.enter_context(nc.sbuf_tensor(name, shape, dt))

        def sem(name):
            return ctx.enter_context(nc.semaphore(name))

        q_ps = ctx.enter_context(nc.psum_tensor("q_ps", [P, INNER], F32))
        k_ps = ctx.enter_context(nc.psum_tensor("k_ps", [P, INNER], F32))
        s_ps = ctx.enter_context(nc.psum_tensor("s_ps", [P, 2, 512], F32))
        ring = ctx.enter_context(nc.psum_tensor("ring", [P, 2, 512], F32))

        cst = sb("cst", [P, consts.shape[1]])

        def const(name):
            a, n = at[name]
            return cst[:, a:a + n]

        ident = const("ident")
        ident_bf = sb("ident_bf", [P, P], BF16)
        mask_bf = sb("mask_bf", [P, at["mask"][1]], BF16)
        rotary0 = const("rotary").rearrange("p (f j d) -> p f j d", f=4, j=TPB)
        x_tok = sb("x_tok", [P, (B * (TPB + 1) + 1) * C])
        x_keep = sb("x_keep", [P, NT, C])

        w0 = sb("w0", [P, 4, C])
        w0T = sb("w0T", [P, 4, C])
        bq_col = sb("bq_col", [P, 1])
        bkv_row = sb("bkv_row", [P, 2 * C])
        bo_row = sb("bo_row", [P, C])
        wqk = sb("wqk", [P, 2 * INNER])
        wv = sb("wv", [P, INNER])
        wvT = sb("wvT", [P, PAIRS, C])
        wo_pad = sb("wo_pad", [P, PAIRS, 2, C])
        wvo = sb("wvo", [P, 4, QUADS, C])
        qk_scales = sb("qk_scales", [P, 2, D])
        rotary = sb("rotary", [P, 4, TPB * D])
        w1 = sb("w1", [P, 2 * F])
        w2 = sb("w2", [P, 3, C])
        b1_col = sb("b1_col", [P, 2, 3])
        ln_col = sb("ln_col", [P, 2])
        b2_row = sb("b2_row", [P, C])

        xs = sb("xs", [P, C])
        xsT = sb("xsT", [P, 2, P])
        squares = sb("squares", [P, 2 * INNER])
        by_cos = sb("by_cos", [P, 2, INNER])
        by_sin = sb("by_sin", [P, 2, INNER])
        qk_rot = sb("qk_rot", [P, 2, INNER])
        sumsq = sb("sumsq", [P, 2 * H])
        rs_t = sb("rs_t", [P, 2 * H])
        rs_h = sb("rs_h", [P, 2 * H])
        rnorm = sb("rnorm", [P, 2, 2 * H])
        qT = sb("qT", [P, PAIRS, P])
        kT = sb("kT", [P, PAIRS, 2, RING])
        smax = sb("smax", [P, H])
        nbias = sb("nbias", [P, H])
        probs = sb("probs", [P, 2, QUADS, 2, 4, WIN])
        psum_row = sb("psum_row", [P, H])
        rrow = sb("rrow", [P, H])
        pT = sb("pT", [P, QUADS, 2, P])
        vo = sb("vo", [P, 2 * NW, QUADS * C])
        xs4 = sb("xs4", [P, FT, C])
        xn4 = sb("xn4", [P, FT, C])
        ln_rs = sb("ln_rs", [P, 5, FT])
        xnT = sb("xnT", [P, 2, FT * P])
        xb = sb("xb", [P, 2, FT, C])
        gate = sb("gate", [P, 3, FT * P])
        hid = sb("hid", [P, 3, FT * P])
        def tiles4(ap):
            return ap.rearrange("p (t c) -> p t c", t=FT)

        q0, q0e = squares[:, 0:512], squares[:, 512:1024]
        k0, k0e = tiles4(squares[:, 1024:1536]), tiles4(squares[:, 1536:2048])
        qfT = by_cos[:, 0, :]
        kf, o0 = tiles4(by_cos[:, 1, 0:512]), tiles4(by_cos[:, 1, 512:1024])
        o0T = by_sin[:, 0, 0:512]
        v1 = tiles4(by_sin[:, 1, 0:FT * (C + 4)])
        kv_bd = sb("kv_bd", [P, C + H0])
        den = sb("den", [P, FT, H0])

        cst_in, x_in, w0_in, wqk_in, wv_in, wo_in, sc_in, w1_in, w2_in, b1_in, ln_in, b2_in = [
            sem(n) for n in ("cst_in", "x_in", "w0_in", "wqk_in", "wv_in", "wo_in", "sc_in", "w1_in",
                             "w2_in", "b1_in", "ln_in", "b2_in")]
        out_done = sem("out_done")
        zeroed = sem("zeroed")
        consts_ready = sem("consts_ready")
        w0T_ps_ready, w0T_ready = sem("w0T_ps_ready"), sem("w0T_ready")
        f_step, f_xn, f_xnT_ps, f_xnT = [sem(n) for n in ("f_step", "f_xn", "f_xnT_ps", "f_xnT")]
        f_proj, f_min, f_exp, f_feat, f_kv, f_bd, f_num, f_den = [
            sem(n) for n in ("f_proj", "f_min", "f_exp", "f_feat", "f_kv", "f_bd", "f_num", "f_den")]
        f_o, f_oT_ps, f_oT, f_y, f_xb, f_x1, h_step = [
            sem(n) for n in ("f_o", "f_oT_ps", "f_oT", "f_y", "f_xb", "f_x1", "h_step")]
        x_ready = sem("x_ready")
        x_mid = sem("x_mid")
        wvT_ps, wvT_ready, wvo_ps, wvo_ready = [sem(n) for n in ("wvT_ps", "wvT_ready", "wvo_ps", "wvo_ready")]
        tables_ready = sem("tables_ready")
        shift_ps, xs_ready, xsT_ps, xsT_ready = [sem(n) for n in ("shift_ps", "xs_ready", "xsT_ps", "xsT_ready")]
        q_ready, k_ready, q_squared, k_squared, q_read, k_read = [
            sem(n) for n in ("q_ready", "k_ready", "q_squared", "k_squared", "q_read", "k_read")]
        norm_step, q_rotated, k_added, k_rotated = [
            sem(n) for n in ("norm_step", "q_rotated", "k_added", "k_rotated")]
        qT_ps, qT_ready, kT_ps, kT_low, kT_high, carried = [
            sem(n) for n in ("qT_ps", "qT_ready", "kT_ps", "kT_low", "kT_high", "carried")]
        s_ready, max_done, bias_ready, exp_done, rrow_ready, p_normed = [
            sem(n) for n in ("s_ready", "max_done", "bias_ready", "exp_done", "rrow_ready", "p_normed")]
        pT_ps, pT_ready, vo_ps, vo_ready, o_ps = [sem(n) for n in ("pT_ps", "pT_ready", "vo_ps", "vo_ready", "o_ps")]
        g_shift, g_xs, g_step, g_xn, g_xnT_ps, g_xnT, g_xb = [
            sem(n) for n in ("g_shift", "g_xs", "g_step", "g_xn", "g_xnT_ps", "g_xnT", "g_xb")]
        g_up, g_gelu, g_hid, g_down = [sem(n) for n in ("g_up", "g_gelu", "g_hid", "g_down")]
        final_ready = sem("final_ready")

        block = ctx.enter_context(nc.Block())

        def slot(i):
            return i + (i >> 3) + 1

        low_rows, high_rows = slice(0, D), slice(D, P)

        def x_cols(i, tiles=1, lo=0, n=C):
            view = x_tok[:, bass.ds((slot(i)) * C, tiles * C)]
            return view.rearrange("p (t c) -> p t c", c=C)[:, :, lo:lo + n] if tiles > 1 or n < C else view

        up_banks = [(q_ps[:, 0:512], q_ps[:, 512:1024]), (k_ps[:, 0:512], k_ps[:, 512:1024]),
                    (s_ps[:, 0, :], s_ps[:, 1, :])]
        wvo_banks = [k_ps[:, 0:512], k_ps[:, 512:1024], s_ps[:, 0, :], s_ps[:, 1, :]]

        def heads(ap, n=H):
            return ap.rearrange("p (h d) -> p h d", h=n)

        RING_USES = ("shift", "qT0", "kT0", "qT1", "kT1", "pT0", "pT1", "o", "vo0", "vo1", "vo2", "vo3", "xsT")

        def ring_bank(k_par, use):
            return (len(RING_USES) * k_par + RING_USES.index(use)) % 2

        def schedule(loop, step):
            for k in (-1, 0, 1):
                step(k, k % 2, None)
            with loop(0, (NT - 4) // 2) as it:
                for r in range(2):
                    step(2 + 2 * it + r, r, it)
            for k in range(NT - 2, NT + 2):
                step(k, k % 2, None)

        def stages(k, it):
            if it is not None:
                return True, True, True, True
            return 0 <= k + 1 < NT, 0 <= k < NT, 0 <= k - 1 < NT, 0 <= k - 2 < NT

        @block.tensor
        def _(pe):
            mm = nc.tensor.matmul

            pe.wait_ge(cst_in, 16)
            pe.wait_ge(w0_in, 128)
            for i in range(4):
                last = nc.tensor.transpose(ring[:, 0, i * C:(i + 1) * C], w0[:, i, :], ident)
            last.then_inc(w0T_ps_ready, 1)
            pe.wait_ge(w0T_ready, 1)

            with pe.Fori(0, B) as b:
                for gg in range(2):
                    G = 2 * b + gg
                    pe.wait_ge(f_xn, G + 1)
                    for t in range(FT):
                        last = nc.tensor.transpose(ring[:, 0, t * P:(t + 1) * P], xn4[:, t, :], ident)
                    last.then_inc(f_xnT_ps, 1)
                    pe.wait_ge(f_xnT, G + 1)
                    pe.wait_ge(f_feat, G)
                    mm(q_ps[:, 0:512], w0T[:, 0, :], xnT[:, 0, :], start=True, stop=True)
                    for t in range(FT):
                        last = mm(k_ps[:, t * 256:(t + 1) * 256], xnT[:, 0, t * P:(t + 1) * P],
                                  w0T[:, 1:3, :], start=True, stop=True)
                    last.then_inc(f_proj, 1)
                    if gg == 0:
                        pe.wait_ge(f_bd, b)
                    pe.wait_ge(f_feat, G + 1)
                    for t in range(FT):
                        last = mm(s_ps[:, 0, 0:C + 2], kf[:, t, :], v1[:, t, 0:C + 2],
                                  start=(gg == 0 and t == 0), stop=(gg == 1 and t == FT - 1))
                    last.then_inc(f_kv, 1)
                pe.wait_ge(f_bd, b + 1)
                for gg in range(2):
                    G = 2 * b + gg
                    pe.wait_ge(f_o, G)
                    for t in range(FT):
                        bank = q_ps[:, 512:1024] if t < 2 else s_ps[:, 1, :]
                        a = (t % 2) * (C + H0)
                        last = mm(bank[:, a:a + C + H0], qfT[:, (gg * FT + t) * P:(gg * FT + t + 1) * P],
                                  kv_bd[:, :], start=True, stop=True)
                    last.then_inc(f_num, 1)
                    pe.wait_ge(f_o, G + 1)
                    for t in range(FT):
                        last = nc.tensor.transpose(ring[:, 1, t * P:(t + 1) * P], o0[:, t, :], ident)
                    last.then_inc(f_oT_ps, 1)
                    pe.wait_ge(f_oT, G + 1)
                    for t in range(FT):
                        last = mm(ring[:, 0, t * C:(t + 1) * C], o0T[:, t * P:(t + 1) * P], w0T[:, 3, :],
                                  start=True, stop=True)
                    last.then_inc(f_y, 1)
                    pe.wait_ge(f_x1, G + 1)

            with pe.Fori(0, DEPTH) as l:
                pe.wait_ge(x_ready, NT * l + NT)
                pe.wait_ge(wv_in, 16 * l + 16)
                for p in range(PAIRS):
                    last = nc.tensor.transpose(q_ps[:, p * C:(p + 1) * C], wv[:, p * C:(p + 1) * C], ident)
                last.then_inc(wvT_ps, 1)
                pe.wait_ge(wvT_ready, l + 1)
                pe.wait_ge(wo_in, 32 * l + 32)
                for p in range(PAIRS):
                    if p >= 4:
                        pe.wait_ge(wvo_ready, PAIRS * l + p - 3)
                    mm(wvo_banks[p % 4][:, 0:2 * C], wvT[:, p, :], wo_pad[:, p, :, :],
                       start=True, stop=True).then_inc(wvo_ps, 1)
                pe.wait_ge(wvo_ready, PAIRS * l + PAIRS)
                pe.wait_ge(wqk_in, 16 * l + 16)

                freed = {
                    "shift": [(xs_ready, 1, 2)], "xsT": [(xsT_ready, 1, 2)],
                    "qT0": [(qT_ready, 2, -1)], "qT1": [(qT_ready, 2, 0)],
                    "kT0": [(kT_low, 2, -1), (kT_high, 2, -1)], "kT1": [(kT_low, 2, 0), (kT_high, 2, 0)],
                    "pT0": [(pT_ready, 2, -3)], "pT1": [(pT_ready, 2, -2)], "o": [(x_mid, 1, -1)],
                } | {f"vo{w}": [(vo_ready, NW, w + 1 - NW)] for w in range(NW)}
                last_use = [None, None]
                steps = [0]

                def bank(par, use, T):
                    s = ring_bank(par, use)
                    if last_use[s]:
                        name, then = last_use[s]
                        for done, times, plus in freed[name]:
                            pe.wait_ge(done, times * (T - (steps[0] - then)) + plus)
                    last_use[s] = use, steps[0]
                    return ring[:, s, :]

                def step(k, par, it):
                    X, Pj, M, O = stages(k, it)
                    a, m, o = par, 1 - par, par
                    T = NT * l + k
                    steps[0] += 1

                    if X:
                        r = bank(par, "shift", T)
                        pe.wait_ge(x_ready, T + 2)
                        mm(r[:, 0:C], const("shift"), x_cols(k + 1), start=True, stop=False)
                        mm(r[:, 0:C], const("carry"), x_tok[:, bass.ds((slot(k + 1) - 1) * C, C)],
                           start=False, stop=True).then_inc(shift_ps, 1)

                    def transposed(which, half, name, ready, signal):
                        r = bank(par, name, T)
                        pe.wait_ge(ready, T)
                        for p in range(4):
                            c = (4 * half + p) * P
                            last = nc.tensor.transpose(r[:, p * P:(p + 1) * P], qk_rot[:, which, c:c + P], ident)
                        last.then_inc(signal, 1)

                    def project(ps, n, w):
                        return mm(ps[:, n * 512:(n + 1) * 512], xsT[:, a, :],
                                  wqk[:, w * INNER + n * 512:w * INNER + (n + 1) * 512], start=True, stop=True)

                    if M:
                        transposed(0, 0, "qT0", q_rotated, qT_ps)
                    if Pj:
                        pe.wait_ge(xsT_ready, T + 1)
                        pe.wait_ge(q_read, T)
                        project(q_ps, 0, 0)
                    if M:
                        transposed(1, 0, "kT0", k_rotated, kT_ps)
                    if Pj:
                        project(q_ps, 1, 0).then_inc(q_ready, 1)
                    if M:
                        transposed(0, 1, "qT1", q_rotated, qT_ps)
                    if Pj:
                        pe.wait_ge(k_read, T)
                        project(k_ps, 0, 1)
                    if M:
                        transposed(1, 1, "kT1", k_rotated, kT_ps)
                    if Pj:
                        project(k_ps, 1, 1).then_inc(k_ready, 1)

                    def probs_transposed(half):
                        r = bank(par, f"pT{half}", T)
                        pe.wait_ge(p_normed, 2 * T - 3 + half)
                        for n in range(4):
                            quad, side = 2 * half + n // 2, n % 2
                            last = nc.tensor.transpose(r[:, n * P:(n + 1) * P],
                                                       probs[:, o, quad, side, :, :].rearrange("p h c -> p (h c)"),
                                                       ident)
                        last.then_inc(pT_ps, 1)

                    def scores(half):
                        pe.wait_ge(qT_ready, 2 * T - 1 + half)
                        pe.wait_ge(kT_low, 2 * T - 1 + half)
                        pe.wait_ge(kT_high, 2 * T - 1 + half)
                        pe.wait_ge(exp_done, 2 * (T - 1))
                        if m == 0:
                            couple = k // 2 if it is None else it + 1
                            variant = couple & (TPB // 2 - 1)
                            pe.wait_ge(carried, NT // 2 * l + couple + 1)
                        else:
                            variant = 1
                        mask = mask_bf[:, bass.ds(variant * 2 * WIN, 2 * WIN)]
                        mm(s_ps[:, half, :], ident_bf[:, :], mask.unsqueeze(1).broadcast_to([P, 8, 2 * WIN]),
                           start=True, stop=False, skip_group_check=True)
                        for p in range(4):
                            for w in range(NW):
                                c = P * m + WIN * w
                                last = mm(s_ps[WIN * w:WIN * (w + 1), half, p * P:(p + 1) * P],
                                          qT[:, 4 * half + p, WIN * w:WIN * (w + 1)],
                                          kT[:, 4 * half + p, :, c:c + 2 * WIN],
                                          start=False, stop=True, skip_group_check=True)
                        last.then_inc(s_ready, 1)

                    if O:
                        probs_transposed(0)
                    if M:
                        scores(0)
                    if O:
                        probs_transposed(1)
                    if M:
                        scores(1)
                    if O:
                        r = bank(par, "o", T)
                        pe.wait_ge(pT_ready, 2 * (T - 1))
                        pe.wait_ge(vo_ready, NW * (T - 1))
                        for n in range(2 * QUADS):
                            quad, side = n // 2, n % 2
                            for w in range(NW):
                                at_w = (NW * o + w - 1 + side) % (2 * NW)
                                last = mm(r[WIN * w:WIN * (w + 1), 0:C], pT[:, quad, side, WIN * w:WIN * (w + 1)],
                                          vo[:, at_w, quad * C:(quad + 1) * C],
                                          start=(n == 0), stop=(n == 2 * QUADS - 1))
                        last.then_inc(o_ps, 1)
                    if M:
                        for w in range(NW):
                            r = bank(par, f"vo{w}", T)
                            for mh in range(4):
                                last = mm(r[WIN * mh:WIN * (mh + 1), :], xsT[:, m, WIN * w:WIN * (w + 1)],
                                          wvo[:, mh, :, :], start=True, stop=True)
                            last.then_inc(vo_ps, 1)
                    if X:
                        r = bank(par, "xsT", T)
                        pe.wait_ge(xs_ready, T + 2)
                        nc.tensor.transpose(r[:, 0:P], xs[:, :], ident).then_inc(xsT_ps, 1)
                schedule(pe.Fori, step)

                pe.wait_ge(x_mid, NT * l + NT)
                pe.wait_ge(w1_in, 16 * l + 16)
                pe.wait_ge(w2_in, 32 * l + 32)

                def shift4(u, U):
                    pe.wait_ge(g_xnT, U)
                    mm(ring[:, 0, :], const("shift"), x_cols(u * FT, FT).rearrange("p t c -> p (t c)"),
                       start=True, stop=False)
                    mm(ring[:, 0, :], const("carry"), x_tok[:, bass.ds((slot(u * FT) - 1) * C, FT * C)],
                       start=False, stop=True).then_inc(g_shift, 1)

                def transpose4(U):
                    pe.wait_ge(g_xn, U + 1)
                    for t in range(FT):
                        last = nc.tensor.transpose(ring[:, 0, t * P:(t + 1) * P], xn4[:, t, :], ident)
                    last.then_inc(g_xnT_ps, 1)

                def up(U, par):
                    pe.wait_ge(g_xnT, U + 1)
                    pe.wait_ge(g_hid, 3 * U)
                    for i, (c, n) in enumerate(FB):
                        for j, off in ((1, F + c), (0, c)):
                            mm(up_banks[i][j][0:n, :], w1[:, off:off + n], xnT[:, par, :],
                               start=True, stop=True).then_inc(g_up, 1)

                def down(U):
                    pe.wait_ge(g_hid, 3 * U + 3)
                    pe.wait_ge(x_ready, FT * U + NT)
                    for t in range(FT):
                        for i in range(3):
                            last = mm(ring[:, 1, t * C:(t + 1) * C], hid[:, i, t * P:(t + 1) * P], w2[:, i, :],
                                      start=(i == 0), stop=(i == 2))
                    last.then_inc(g_down, 1)

                def both(u, par):
                    U = NG * l + u
                    shift4(u, U)
                    up(U - 1, 1 - par)
                    transpose4(U)
                    down(U - 1)

                shift4(0, NG * l)
                transpose4(NG * l)
                with pe.Fori(0, (NG - 2) // 2) as it:
                    both(2 * it + 1, 1)
                    both(2 * it + 2, 0)
                both(NG - 1, 1)
                up(NG * l + NG - 1, 1)
                down(NG * l + NG - 1)

        @block.vector
        def _(dve):
            v = nc.vector

            def rsqrt(y, src, t, h, first, done, base):
                ops = [
                    first,
                    lambda: v.tensor_scalar(t.bitcast(I32), src.bitcast(I32), 1, None, ALU.logical_shift_right),
                    lambda: v.tensor_scalar(y.bitcast(I32), t.bitcast(I32), -1.0, RSQRT_MAGIC, ALU.mult, ALU.add),
                ]
                for _ in range(3):
                    ops += [
                        lambda: v.tensor_tensor(t, y, y, ALU.mult),
                        lambda: v.scalar_tensor_tensor(h, t, -0.5, src, ALU.mult, ALU.mult),
                        lambda: v.scalar_tensor_tensor(y, h, 1.5, y, ALU.add, ALU.mult),
                    ]
                assert len(ops) == RSQRT_OPS
                for i, op in enumerate(ops):
                    dve.wait_ge(done, base + i)
                    op().then_inc(done, 1)

            def layernorm4(src, dst, G, step, free):
                n = LN_STEPS
                rows, var, rstd, t, h = (ln_rs[:, i, :] for i in range(5))

                def wide(ap):
                    return ap.unsqueeze(2).broadcast_to([P, FT, C])

                v.tensor_reduce(rows, src, AX, ALU.add).then_inc(step, 1)
                dve.wait_ge(free, G)
                dve.wait_ge(step, n * G + 1)
                v.scalar_tensor_tensor(xs4[:, :, :], wide(rows), -1.0 / C, src, ALU.mult, ALU.add).then_inc(step, 1)
                dve.wait_ge(step, n * G + 2)
                v.tensor_tensor(xn4[:, :, :], xs4[:, :, :], xs4[:, :, :], ALU.mult).then_inc(step, 1)
                dve.wait_ge(step, n * G + 3)
                v.tensor_reduce(var, xn4[:, :, :], AX, ALU.add).then_inc(step, 1)
                rsqrt(rstd, var, t, h, lambda: v.tensor_scalar(var, var, 1.0 / C, EPS, ALU.mult, ALU.add),
                      step, n * G + 4)
                dve.wait_ge(step, n * G + n)
                return v.tensor_tensor(dst, xs4[:, :, :], wide(rstd), ALU.mult)

            dve.wait_ge(cst_in, 16)
            v.tensor_copy(ident_bf[:, :], ident).then_inc(consts_ready, 1)
            v.tensor_copy(mask_bf[:, :], const("mask")).then_inc(consts_ready, 1)
            v.memset(x_tok[:, :], 0.0).then_inc(zeroed, 1)
            v.memset(v1[:, :, C:C + 4], 1.0)
            v.memset(kT[:, :, :, :], 0.0).then_inc(zeroed, 1)
            v.memset(wo_pad[0:D, :, 1, :], 0.0)
            v.memset(wo_pad[D:P, :, 0, :], 0.0)
            v.memset(hid[:, 2, :], 0.0)
            v.memset(w2[:, 2, :], 0.0).then_inc(zeroed, 1)
            v.memset(vo[:, 2 * NW - 1, :], 0.0).then_inc(zeroed, 1)
            dve.wait_ge(zeroed, 4)
            dve.wait_ge(x_in, 64)
            dve.wait_ge(w0_in, 128)

            with dve.Fori(0, B) as b:
                for gg in range(2):
                    G = 2 * b + gg
                    src = x_keep[:, bass.ds(G * FT, FT), :]
                    layernorm4(src, xn4[:, :, :], G, f_step, f_xnT_ps).then_inc(f_xn, 1)
                    dve.wait_ge(f_proj, G + 1)
                    dve.wait_ge(f_kv, G)
                    v.tensor_scalar(q0[:, :], q_ps[:, 0:512], bq_col[:, :], None, ALU.add).then_inc(f_min, 1)
                    kv_ps = k_ps[:, :].rearrange("p (t c) -> p t c", t=FT)
                    v.tensor_tensor(k0[:, :, :], kv_ps[:, :, 0:C],
                                    bkv_row[:, 0:C].unsqueeze(1).broadcast_to([P, FT, C]), ALU.add).then_inc(f_min, 1)
                    v.tensor_tensor(v1[:, :, 0:C], kv_ps[:, :, C:2 * C],
                                    bkv_row[:, C:2 * C].unsqueeze(1).broadcast_to([P, FT, C]), ALU.add)
                    dve.wait_ge(f_min, 4 * G + 1)
                    v.tensor_scalar(q0e[:, :], q0[:, :], 0.0, None, ALU.min).then_inc(f_min, 1)
                    dve.wait_ge(f_min, 4 * G + 2)
                    v.tensor_scalar(k0e[:, :, :], k0[:, :, :], 0.0, None, ALU.min).then_inc(f_min, 1)
                    dve.wait_ge(f_exp, 2 * G + 1)
                    if gg == 0:
                        dve.wait_ge(f_num, G)
                    v.scalar_tensor_tensor(qfT[:, gg * 512:(gg + 1) * 512], q0[:, :], 0.0, q0e[:, :],
                                           ALU.max, ALU.add)
                    dve.wait_ge(f_exp, 2 * G + 2)
                    v.scalar_tensor_tensor(kf[:, :, :], k0[:, :, :], 0.0, k0e[:, :, :],
                                           ALU.max, ALU.add).then_inc(f_feat, 1)
                dve.wait_ge(f_kv, 2 * b + 2)
                dve.wait_ge(f_num, 2 * b)
                v.tensor_tensor(kv_bd[:, 0:C], s_ps[:, 0, 0:C], const("blocks"), ALU.mult)
                v.tensor_tensor(kv_bd[:, C:C + H0], s_ps[:, 0, C:C + 1].broadcast_to([P, H0]), const("heads"),
                                ALU.mult).then_inc(f_bd, 1)
                for gg in range(2):
                    G = 2 * b + gg
                    tiles = x_keep[:, bass.ds(G * FT, FT), :]
                    dve.wait_ge(f_num, G + 1)
                    halves = [ps.rearrange("p (t c) -> p t c", t=2)
                              for ps in (q_ps[:, 512:512 + 2 * (C + H0)], s_ps[:, 1, 0:2 * (C + H0)])]
                    for n in range(2):
                        v.tensor_scalar(den[:, 2 * n:2 * n + 2, :], halves[n][:, :, C:C + H0], 1e-6, None,
                                        ALU.max).then_inc(f_den, 1)
                    dve.wait_ge(f_den, 3 * G + 2)
                    v.reciprocal(den[:, :, :], den[:, :, :]).then_inc(f_den, 1)
                    dve.wait_ge(f_den, 3 * G + 3)
                    dve.wait_ge(f_oT_ps, G)
                    for n in range(2):
                        for t in range(2):
                            i = 2 * n + t
                            last = v.tensor_tensor(heads(o0[:, i, :], H0), heads(halves[n][:, t, 0:C], H0),
                                                   den[:, i, :].unsqueeze(2).broadcast_to([P, H0, D0]), ALU.mult)
                    last.then_inc(f_o, 1)
                    dve.wait_ge(f_y, G + 1)
                    dve.wait_ge(f_xb, G + 1)
                    y = tiles4(ring[:, 0, :])
                    v.tensor_tensor(xb[:, 1, :, :], y, xb[:, 0, :, :], ALU.add)
                    v.tensor_tensor(tiles, y, xb[:, 0, :, :], ALU.add).then_inc(f_x1, 1)
                    dve.wait_ge(f_x1, G + 1)
                    layernorm4(xb[:, 1, :, :], x_cols(G * FT, FT), G, h_step, f_xnT_ps).then_inc(x_ready, FT)

            with dve.Fori(0, DEPTH) as l:
                dve.wait_ge(tables_ready, l + 1)

                def step(k, par, it):
                    X, Pj, M, O = stages(k, it)
                    a, m = par, 1 - par
                    T = NT * l + k
                    off = WIN + P * m

                    def q_evacuated(half):
                        dve.wait_ge(qT_ps, 2 * T - 1 + half)
                        v.tensor_copy(qT[:, 4 * half:4 * half + 4, :],
                                      ring[:, ring_bank(par, f"qT{half}"), :].rearrange("p (n t) -> p n t", n=4)
                                      ).then_inc(qT_ready, 1)

                    def k_evacuated(half):
                        dve.wait_ge(kT_ps, 2 * T - 1 + half)
                        bank = ring[high_rows, ring_bank(par, f"kT{half}"), :]
                        v.tensor_copy(kT[high_rows, 4 * half:4 * half + 4, 1, off:off + P],
                                      bank.rearrange("p (n t) -> p n t", n=4)).then_inc(kT_high, 1)

                    def row_reciprocals(t, half):
                        dve.wait_ge(exp_done, 2 * t + 1 + half)
                        if half:
                            dve.wait_ge(p_normed, 2 * t)
                        else:
                            dve.wait_ge(p_normed, 2 * t)
                        h = slice(8 * half, 8 * half + 8)
                        v.reciprocal(rrow[:, h], psum_row[:, h]).then_inc(rrow_ready, 1)

                    def rotate(n, ps, squared, free, signal):
                        dve.wait_ge(squared, T + 1)
                        dve.wait_ge(free, T)
                        j = (k & (TPB - 1)) if it is not None else k % TPB
                        for part, buf in ((0, by_cos), (1, by_sin)):
                            tab = rotary[:, 2 * n + part, bass.ds(j * D, D)]
                            last = v.tensor_tensor(heads(buf[:, n, :]), heads(ps[:, :]),
                                                   tab.unsqueeze(1).broadcast_to([P, H, D]), ALU.mult)
                        last.then_inc(signal, 1)

                    def softmax_bias(half):
                        h = slice(8 * half, 8 * half + 8)
                        dve.wait_ge(s_ready, 2 * T - 1 + half)
                        v.tensor_reduce(smax[:, h], heads(s_ps[:, half, :], 8), AX, ALU.max).then_inc(max_done, 1)
                        dve.wait_ge(max_done, 2 * T - 1 + half)
                        dve.wait_ge(norm_step, NORM_STEPS * T)
                        v.scalar_tensor_tensor(nbias[:, h], smax[:, h], -1.0, rnorm[:, m, h], ALU.mult,
                                               ALU.mult).then_inc(bias_ready, 1)

                    if M:
                        if m == 0:
                            n = (k // 2 if it is None else it + 1) & (TPB // 2 - 1)
                            dve.wait_ge(kT_low, 2 * T - 2)
                            dve.wait_ge(kT_high, 2 * T - 2)
                            keep = const("keep")[:, bass.ds(n, 1)].unsqueeze(2).broadcast_to([P, H, WIN])
                            v.tensor_tensor(kT[:, :, :, 0:WIN].rearrange("p a b c -> p (a b) c"),
                                            kT[:, :, :, RING - WIN:RING].rearrange("p a b c -> p (a b) c"),
                                            keep, ALU.mult).then_inc(carried, 1)
                        q_evacuated(0)
                        k_evacuated(0)
                    if O:
                        row_reciprocals(T - 2, 1)
                    if M:
                        q_evacuated(1)
                        k_evacuated(1)
                    if Pj:
                        rotate(0, q_ps, q_squared, q_rotated, q_read)
                    if M:
                        softmax_bias(0)
                        softmax_bias(1)
                    if Pj:
                        rotate(1, k_ps, k_squared, k_added, k_read)
                    if O:
                        dve.wait_ge(o_ps, T - 1)
                        xc = x_cols(k - 2)
                        v.tensor_tensor(xc, ring[:, ring_bank(par, "o"), 0:C], xc, ALU.add).then_inc(x_mid, 1)
                    if Pj:
                        for n in range(2):
                            v.tensor_reduce(sumsq[:, n * H:(n + 1) * H],
                                            heads(squares[:, n * INNER:(n + 1) * INNER]), AX,
                                            ALU.add).then_inc(norm_step, 1)
                        rsqrt(rnorm[:, a, :], sumsq[:, :], rs_t[:, :], rs_h[:, :],
                              lambda: v.tensor_scalar(sumsq[:, :], sumsq[:, :], 1e-24, None, ALU.max),
                              norm_step, NORM_STEPS * T + 2)
                    if M:
                        row_reciprocals(T - 1, 0)

                schedule(dve.Fori, step)

                dve.wait_ge(b1_in, 96 * l + 96)

                def normed(U):
                    dve.wait_ge(g_xs, U + 1)
                    layernorm4(xs4[:, :, :], xn4[:, :, :], U, g_step, g_xnT_ps).then_inc(g_xn, 1)

                def hidden(U, u, par):
                    dve.wait_ge(g_down, U)
                    for i, (c, n) in enumerate(FB):
                        dve.wait_ge(g_up, 6 * U + 2 * i + 2)
                        dve.wait_ge(g_gelu, 3 * U + i + 1)
                        v.scalar_tensor_tensor(hid[0:n, i, :], up_banks[i][0][0:n, :], b1_col[0:n, 0, i:i + 1],
                                               gate[0:n, i, :], ALU.add, ALU.mult).then_inc(g_hid, 1)
                    dve.wait_ge(g_down, U + 1)
                    dve.wait_ge(g_xb, U + 1)
                    v.tensor_tensor(x_cols(u * FT, FT), ring[:, 1, :].rearrange("p (t c) -> p t c", t=FT),
                                    xb[:, par, :, :], ALU.add).then_inc(x_ready, FT)

                def both(u, par):
                    normed(NG * l + u)
                    hidden(NG * l + u - 1, u - 1, 1 - par)

                normed(NG * l)
                with dve.Fori(0, (NG - 2) // 2) as it:
                    both(2 * it + 1, 1)
                    both(2 * it + 2, 0)
                both(NG - 1, 1)
                hidden(NG * l + NG - 1, NG - 1, 1)

            dve.wait_ge(x_ready, NT * (DEPTH + 1))
            for b in range(B):
                tiles = x_keep[:, b * TPB:(b + 1) * TPB, :]
                v.tensor_tensor(tiles, tiles, x_cols(b * TPB, TPB), ALU.add).then_inc(final_ready, 1)

        @block.scalar
        def _(act):
            def copy(out_, in_):
                return nc.scalar.activation(out_, in_, ACT.Copy)

            act.wait_ge(w0T_ps_ready, 1)
            copy(w0T[:, :, :].rearrange("p a c -> p (a c)"), ring[:, 0, :]).then_inc(w0T_ready, 1)

            with act.Fori(0, B) as b:
                for gg in range(2):
                    G = 2 * b + gg
                    act.wait_ge(f_xnT_ps, G + 1)
                    act.wait_ge(f_proj, G)
                    copy(xnT[:, 0, :], ring[:, 0, :]).then_inc(f_xnT, 1)
                    act.wait_ge(f_min, 4 * G + 3)
                    nc.scalar.activation(q0e[:, :], q0e[:, :], ACT.Exp).then_inc(f_exp, 1)
                    act.wait_ge(f_min, 4 * G + 4)
                    nc.scalar.activation(k0e[:, :, :], k0e[:, :, :], ACT.Exp).then_inc(f_exp, 1)
                for gg in range(2):
                    G = 2 * b + gg
                    act.wait_ge(f_oT_ps, G + 1)
                    act.wait_ge(f_y, G)
                    copy(o0T[:, :], ring[:, 1, :]).then_inc(f_oT, 1)

            with act.Fori(0, DEPTH) as l:
                act.wait_ge(wvT_ps, l + 1)
                copy(wvT[:, :, :].rearrange("p a c -> p (a c)"), q_ps[:, :]).then_inc(wvT_ready, 1)
                for p in range(PAIRS):
                    act.wait_ge(wvo_ps, PAIRS * l + p + 1)
                    copy(wvo[:, 2 * (p % 2):2 * (p % 2) + 2, p // 2, :],
                         wvo_banks[p % 4][:, 0:2 * C].rearrange("p (a c) -> p a c", a=2)).then_inc(wvo_ready, 1)

                def step(k, par, it):
                    X, Pj, M, O = stages(k, it)
                    m, o = 1 - par, par
                    T = NT * l + k
                    off = WIN + P * m

                    def from_ring(use, rows=slice(0, P), n=512):
                        return ring[rows, ring_bank(par, use), 0:n]

                    def k_evacuated(half):
                        act.wait_ge(kT_ps, 2 * T - 1 + half)
                        copy(kT[low_rows, 4 * half:4 * half + 4, 0, off:off + P],
                             from_ring(f"kT{half}", low_rows).rearrange("p (n t) -> p n t", n=4)).then_inc(kT_low, 1)

                    def square(n, ps, ready, signal):
                        act.wait_ge(ready, T + 1)
                        act.wait_ge(norm_step, NORM_STEPS * T)
                        nc.scalar.activation(squares[:, n * INNER:(n + 1) * INNER], ps[:, :],
                                             ACT.Square).then_inc(signal, 1)

                    def p_evacuated(half):
                        act.wait_ge(pT_ps, 2 * T - 3 + half)
                        copy(pT[:, 2 * half:2 * half + 2, :, :].rearrange("p a b c -> p (a b c)"),
                             from_ring(f"pT{half}")).then_inc(pT_ready, 1)

                    def exponentials(h0, h1):
                        for h in range(h0, h1):
                            c = h % 8 * 2 * WIN
                            last = nc.scalar.activation(
                                probs[:, m, h // 4, :, h % 4, :],
                                s_ps[:, h // 8, c:c + 2 * WIN].rearrange("p (s c) -> p s c", s=2), ACT.Exp,
                                scale=rnorm[:, m, h:h + 1], bias=nbias[:, h:h + 1],
                                accum_out=psum_row[:, h:h + 1])
                        return last

                    def vo_evacuated(w):
                        act.wait_ge(vo_ps, NW * (T - 1) + w + 1)
                        copy(vo[:, NW * m + w, :], from_ring(f"vo{w}")).then_inc(vo_ready, 1)

                    if X:
                        act.wait_ge(shift_ps, T + 2)
                        act.wait_ge(xsT_ps, T + 1)
                        copy(xs[:, C // 2:C], ring[:, ring_bank(par, "shift"), C // 2:C])
                        copy(xs[:, 0:C // 2], x_tok[:, bass.ds(slot(k + 1) * C, C // 2)]).then_inc(xs_ready, 1)
                    if M:
                        k_evacuated(0)
                    if Pj:
                        square(0, q_ps, q_ready, q_squared)
                    if M:
                        k_evacuated(1)
                    if O:
                        p_evacuated(0)
                    if Pj:
                        square(1, k_ps, k_ready, k_squared)
                    if O:
                        p_evacuated(1)
                    if M:
                        act.wait_ge(bias_ready, 2 * T - 1)
                        exponentials(0, 8).then_inc(exp_done, 1)
                        vo_evacuated(0)
                        act.wait_ge(bias_ready, 2 * T)
                        exponentials(8, 12)
                        vo_evacuated(1)
                        exponentials(12, 16).then_inc(exp_done, 1)
                        vo_evacuated(2)
                        vo_evacuated(3)
                    if X:
                        act.wait_ge(xsT_ps, T + 2)
                        copy(xsT[:, m, :], from_ring("xsT", n=P)).then_inc(xsT_ready, 1)

                schedule(act.Fori, step)

                act.wait_ge(ln_in, 32 * l + 32)
                act.wait_ge(b1_in, 96 * l + 96)

                def shifted(u, U):
                    act.wait_ge(g_shift, U + 1)
                    act.wait_ge(g_xn, U)
                    bank = ring[:, 0, :].rearrange("p (t c) -> p t c", t=FT)
                    copy(xs4[:, :, C // 2:C], bank[:, :, C // 2:C])
                    copy(xs4[:, :, 0:C // 2], x_cols(u * FT, FT, 0, C // 2)).then_inc(g_xs, 1)

                def transposed(U, par):
                    act.wait_ge(g_xnT_ps, U + 1)
                    nc.scalar.activation(xnT[:, par, :], ring[:, 0, :], ACT.Identity, scale=ln_col[:, 0:1],
                                         bias=ln_col[:, 1:2]).then_inc(g_xnT, 1)

                def gelus(U):
                    act.wait_ge(g_hid, 3 * U)
                    for i, (c, n) in enumerate(FB):
                        act.wait_ge(g_up, 6 * U + 2 * i + 1)
                        nc.scalar.activation(gate[0:n, i, :], up_banks[i][1][0:n, :], ACT.Gelu,
                                             bias=b1_col[0:n, 1, i:i + 1]).then_inc(g_gelu, 1)

                def both(u, par):
                    U = NG * l + u
                    shifted(u, U)
                    gelus(U - 1)
                    transposed(U, par)

                shifted(0, NG * l)
                transposed(NG * l, 0)
                with act.Fori(0, (NG - 2) // 2) as it:
                    both(2 * it + 1, 1)
                    both(2 * it + 2, 0)
                both(NG - 1, 1)
                gelus(NG * l + NG - 1)

        @block.gpsimd
        def _(pool):
            g = nc.gpsimd

            pool.wait_ge(x_in, 64)
            pool.wait_ge(w0_in, 128)
            with pool.Fori(0, NG) as G:
                pool.wait_ge(f_x1, G)
                g.tensor_tensor(xb[:, 0, :, :], x_keep[:, bass.ds(G * FT, FT), :],
                                bo_row[:, :].unsqueeze(1).broadcast_to([P, FT, C]), ALU.add).then_inc(f_xb, 1)

            with pool.Fori(0, DEPTH) as l:
                pool.wait_ge(sc_in, 32 * l + 32)
                pool.wait_ge(k_read, NT * l)
                for n in range(4):
                    last = g.tensor_tensor(rotary[:, n, :].rearrange("p (j d) -> p j d", j=TPB), rotary0[:, n],
                                           qk_scales[:, n // 2, :].unsqueeze(1).broadcast_to([P, TPB, D]), ALU.mult)
                last.then_inc(tables_ready, 1)

                def step(k, par, it):
                    X, Pj, M, O = stages(k, it)
                    T = NT * l + k

                    def normalise(t, half, slot_par):
                        pool.wait_ge(rrow_ready, 2 * t + half + 1)
                        for quad in (2 * half, 2 * half + 1):
                            p = probs[:, slot_par, quad]
                            r = rrow[:, 4 * quad:4 * quad + 4].unsqueeze(1).unsqueeze(3).broadcast_to([P, 2, 4, WIN])
                            last = g.tensor_tensor(p, p, r, ALU.mult)
                        last.then_inc(p_normed, 1)

                    def add_rotated(n, signal):
                        d, cs, sn = heads(qk_rot[:, n, :]), heads(by_cos[:, n, :]), heads(by_sin[:, n, :])
                        lo, hi = slice(0, D // 2), slice(D // 2, D)
                        g.tensor_tensor(d[:, :, lo], cs[:, :, lo], sn[:, :, hi], ALU.add)
                        g.tensor_tensor(d[:, :, hi], cs[:, :, hi], sn[:, :, lo], ALU.add).then_inc(signal, 1)

                    if O:
                        normalise(T - 2, 1, par)
                    if Pj:
                        pool.wait_ge(q_read, T + 1)
                        pool.wait_ge(qT_ps, 2 * T)
                        add_rotated(0, q_rotated)
                        pool.wait_ge(k_read, T + 1)
                        pool.wait_ge(kT_ps, 2 * T)
                        add_rotated(1, k_added)
                        pool.wait_ge(k_added, T + 1)
                        pool.wait_ge(norm_step, NORM_STEPS * (T + 1))
                        kk = heads(qk_rot[:, 1, :])
                        g.tensor_tensor(kk, kk, rnorm[:, par, H:2 * H].unsqueeze(2).broadcast_to([P, H, D]),
                                        ALU.mult).then_inc(k_rotated, 1)
                    if M:
                        normalise(T - 1, 0, 1 - par)

                schedule(pool.Fori, step)

                def biased(u, par):
                    pool.wait_ge(b2_in, 16 * l + 16)
                    pool.wait_ge(x_mid, NT * l + FT * u + FT)
                    pool.wait_ge(x_ready, FT * (NG * l + u - 1) + NT)
                    g.tensor_tensor(xb[:, par, :, :], x_cols(u * FT, FT),
                                    b2_row[:, :].unsqueeze(1).broadcast_to([P, FT, C]), ALU.add).then_inc(g_xb, 1)

                with pool.Fori(0, NG // 2) as it:
                    biased(2 * it, 0)
                    biased(2 * it + 1, 1)

        @block.sync
        def _(sp):
            def load(dst, src, done):
                sp.dma_start(dst, src).then_inc(done, 16)

            def col(ap):
                return ap.rearrange("(p a) -> p a", a=1)

            def row(ap):
                return ap.partition_broadcast(P)

            load(cst[:, :], consts, cst_in)
            for i, w in enumerate((Wq, Wk, Wv, Wo)):
                load(w0[:, i, :], w, w0_in)
            load(bq_col[:, :], col(bq), w0_in)
            load(bkv_row[:, 0:C], row(bk), w0_in)
            load(bkv_row[:, C:2 * C], row(bv), w0_in)
            load(bo_row[:, :], row(bo), w0_in)
            for b in range(B):
                load(x_keep[:, b * TPB:(b + 1) * TPB, :], x[b].rearrange("(t p) c -> p t c", p=P), x_in)
            sp.wait_ge(zeroed, 4)
            with sp.Fori(0, DEPTH) as l:
                layer = bass.ds(l, 1)
                sp.wait_ge(vo_ps, NW * NT * l)
                w = Wqkv[layer, :, :].rearrange("l c n -> (l c) n")
                load(wqk[:, :], w[:, 0:2 * INNER], wqk_in)
                load(wv[:, :], w[:, 2 * INNER:3 * INNER], wv_in)
                wo = Wout[layer, :, :].rearrange("l (q a d) c -> (l a) d q c", a=2, d=D)
                load(wo_pad[low_rows, :, 0, :], wo[0], wo_in)
                load(wo_pad[high_rows, :, 1, :], wo[1], wo_in)
                sp.wait_ge(tables_ready, l)
                load(qk_scales[:, 0, :], row(q_scale[layer, :].rearrange("l d -> (l d)")), sc_in)
                load(qk_scales[:, 1, :], row(k_scale[layer, :].rearrange("l d -> (l d)")), sc_in)
                sp.wait_ge(x_ready, NT * l + NT)
                load(w1[:, :], W1[layer, :, :].rearrange("l c n -> (l c) n"), w1_in)
                wd = W2[layer, :, :].rearrange("l n c -> (l n) c")
                load(w2[:, 0:2, :], wd[0:2 * P, :].rearrange("(i p) c -> p i c", p=P), w2_in)
                load(w2[0:F - 2 * P, 2, :], wd[2 * P:F, :], w2_in)
                bias = b1[layer, :].rearrange("l n -> (l n)")
                for j in range(2):
                    for i, (c, n) in enumerate(FB):
                        load(b1_col[0:n, j, i:i + 1], col(bias[j * F + c:j * F + c + n]), b1_in)
                load(ln_col[:, 0:1], col(ln_g[layer, :].rearrange("l n -> (l n)")), ln_in)
                load(ln_col[:, 1:2], col(ln_b[layer, :].rearrange("l n -> (l n)")), ln_in)
                load(b2_row[:, :], row(b2[layer, :].rearrange("l n -> (l n)")), b2_in)
            for b in range(B):
                sp.wait_ge(final_ready, b + 1)
                sp.dma_start(out[b].rearrange("(t p) c -> p t c", p=P),
                             x_keep[:, b * TPB:(b + 1) * TPB, :]).then_inc(out_done, 16)
            sp.wait_ge(out_done, 16 * B)


_INS = ["L0_attn_x", "L0_attn_Wq", "L0_attn_bq", "L0_attn_Wk", "L0_attn_bk", "L0_attn_Wv", "L0_attn_bv",
        "L0_attn_Wo", "L0_attn_bo", "L0_ffn_Wqkv", "L0_ffn_q_scale", "L0_ffn_k_scale", "L0_ffn_Wo",
        "L0_ffn_ln_g", "L0_ffn_ln_b", "L0_ffn_W1", "L0_ffn_b1", "L0_ffn_W2", "L0_ffn_b2"]


def kernel(**inputs):
    import concourse.bacc as bacc
    from concourse.bass_utils import run_bass_kernel_spmd

    nc = bacc.Bacc("TRN2", target_bir_lowering=False, num_devices=1)
    table, at = constants()
    arrays = {"consts": table}
    for name in _INS:
        arrays[name] = np.ascontiguousarray(inputs[name])
    args = [nc.dram_tensor(n, a.shape, mybir.dt.from_np(a.dtype), kind="ExternalInput").ap()
            for n, a in arrays.items()]
    out = nc.dram_tensor("out", (B, N, C), F32, kind="ExternalOutput").ap()
    build(nc, args[0], at, *args[1:], out)
    r = run_bass_kernel_spmd(nc, [arrays], core_ids=[0])
    return r.results[0]["out"]
```

```python
from contextlib import ExitStack

import numpy as np

import concourse.bass as bass
from concourse import mybir

F32 = mybir.dt.float32
F32R = mybir.dt.float32r
I32 = mybir.dt.int32
BF16 = mybir.dt.bfloat16
ACT = mybir.ActivationFunctionType
ALU = mybir.AluOpType
AX = mybir.AxisListType.X

P = 128
B, N, C = 4, 1024, 128
TPB = N // P
NT = B * TPB
DEPTH, H, D, WIN = 6, 16, 64, 32
PAIRS = H // 2
WVO_ROUNDS = PAIRS // 2
QUADS = H // 4
NW = P // WIN
INNER = H * D
F = int(C * 4 * 2 / 3)
FB = [(0, 128), (128, 128), (256, F - 256)]
FT = 4
NG = NT // FT
H0, D0 = 16, 8
EPS = 1e-5
NEG = -1e30
CREDIT = 2
RING_BANKS = 4
RING = WIN + 2 * P
RSQRT_MAGIC = 1597463007.0
RSQRT_OPS = 12
LN_STEPS = RSQRT_OPS + 4


def rotary_constants():
    f = np.float32
    half = np.arange(0, D, 2, dtype=f)
    inv_freq = f(1.0) / np.power(f(10000.0), half / f(D), dtype=f)
    t = np.arange(N, dtype=f)
    freqs = np.concatenate([t[:, None] * inv_freq[None]] * 2, -1)
    base = (half + f(0.4 * D)) / f(1.4 * D)
    power = (t - N // 2) / f(WIN // 2)
    scale = np.power(base[None], power[:, None], dtype=f)
    scale = np.concatenate([scale, scale], -1)
    inv = f(1.0) / scale
    sign = np.where(np.arange(D) < D // 2, f(1), f(-1))[None]
    cos, sin = np.cos(freqs), np.sin(freqs) * sign
    qk_scale = f(8.0)
    tab = np.stack([cos * scale * qk_scale, sin * scale * qk_scale, cos * inv, sin * inv])
    return tab.reshape(4, TPB, P, D).transpose(2, 0, 1, 3).reshape(P, -1).astype(f)


def constants():
    f = np.float32
    parts = {"ident": np.eye(P, dtype=f)}
    parts["shift"] = np.eye(P, k=1, dtype=f)
    carry = np.zeros((P, P), f)
    carry[P - 1, 0] = 1
    parts["carry"] = carry
    r, c = np.arange(P)[:, None] % WIN, np.arange(WIN)[None]
    mask = np.concatenate([np.where(r > c, f(NEG), f(0)), np.where(c > r, f(NEG), f(0))], 1)
    first = mask.copy()
    first[0:WIN, 0:WIN] = NEG
    parts["mask"] = np.concatenate([first] + [mask] * (TPB // 2 - 1), 1)
    parts["keep"] = np.tile((np.arange(TPB // 2) > 0).astype(f)[None], (P, 1))
    h = np.arange(P) // D0
    parts["blocks"] = (h[:, None] == h[None]).astype(f)
    parts["heads"] = (h[:, None] == np.arange(H0)[None]).astype(f)
    parts["rotary"] = rotary_constants()
    at, n = {}, 0
    for k, v in parts.items():
        at[k] = (n, v.shape[1])
        n += v.shape[1]
    return np.concatenate(list(parts.values()), 1), at


def build(nc, consts, at, x, Wq, bq, Wk, bk, Wv, bv, Wo, bo, Wqkv, q_scale, k_scale, Wout,
          ln_g, ln_b, W1, b1, W2, b2, out):
    ctx = ExitStack()
    with ctx:
        def sb(name, shape, dt=F32):
            return ctx.enter_context(nc.sbuf_tensor(name, shape, dt))

        def sem(name):
            return ctx.enter_context(nc.semaphore(name))

        qk_ps = ctx.enter_context(nc.psum_tensor("qk_ps", [P, INNER], F32))
        s_ps = ctx.enter_context(nc.psum_tensor("s_ps", [P, 2, 512], F32))
        ring = ctx.enter_context(nc.psum_tensor("ring", [P, RING_BANKS, 512], F32))
        q_ps = qk_ps
        k_ps = ring[:, 2:4, :].rearrange("p a c -> p (a c)")

        cst = sb("cst", [P, consts.shape[1]])

        def const(name):
            a, n = at[name]
            return cst[:, a:a + n]

        ident = const("ident")
        ident_bf = sb("ident_bf", [P, P], BF16)
        mask_bf = sb("mask_bf", [P, at["mask"][1]], BF16)
        rotary0 = const("rotary").rearrange("p (f j d) -> p f j d", f=4, j=TPB)
        x_tok = sb("x_tok", [P, (B * (TPB + 1) + 1) * C])
        x_keep = sb("x_keep", [P, NT, C])

        w0 = sb("w0", [P, 4, C])
        w0T = sb("w0T", [P, 4, C])
        bq_col = sb("bq_col", [P, 1])
        bkv_row = sb("bkv_row", [P, 2 * C])
        bo_row = sb("bo_row", [P, C])
        wqk_hi = sb("wqk_hi", [P, 2 * INNER], F32R)
        wqk_lo = sb("wqk_lo", [P, 2 * INNER], F32R)
        wv = sb("wv", [P, INNER])
        wvT = sb("wvT", [P, PAIRS, C])
        wo_pad = sb("wo_pad", [P, PAIRS, 2, C])
        wvo = sb("wvo", [P, 4, QUADS, C])
        qk_scales = sb("qk_scales", [P, 2, D])
        rotary = [sb(f"rotary{n}", [P, TPB * D]) for n in range(4)]
        w1 = sb("w1", [P, 2 * F])
        w2 = sb("w2", [P, 3, C])
        b1_col = sb("b1_col", [P, 2, 3])
        ln_col = sb("ln_col", [P, 2])
        b2_row = sb("b2_row", [P, C])

        xs = sb("xs", [P, C])
        xsT = sb("xsT", [P, 2, P])
        xsT_hi = sb("xsT_hi", [P, 2, P], F32R)
        xsT_lo = sb("xsT_lo", [P, 2, P], F32R)
        squares = sb("squares", [P, 2 * INNER])
        by_cos = sb("by_cos", [P, 2, INNER])
        by_sin = sb("by_sin", [P, 2, INNER])
        qk_rot = sb("qk_rot", [P, 2, INNER])
        wqk = qk_rot[:, :, :].rearrange("p a n -> p (a n)")
        sumsq = sb("sumsq", [P, 2 * H])
        rs_t = sb("rs_t", [P, 2 * H])
        rs_h = sb("rs_h", [P, 2 * H])
        rnorm = sb("rnorm", [P, 2, 2 * H])
        qT = sb("qT", [P, PAIRS, P])
        kT = sb("kT", [P, PAIRS, 2, RING])
        smax = sb("smax", [P, H])
        nbias = sb("nbias", [P, H])
        probs = sb("probs", [P, 2, QUADS, 2, 4, WIN])
        psum_row = sb("psum_row", [P, H])
        rrow = sb("rrow", [P, H])
        pT = sb("pT", [P, QUADS, 2, P])
        vo = sb("vo", [P, 2 * NW, QUADS * C])
        xs4 = sb("xs4", [P, FT, C])
        xn4 = sb("xn4", [P, FT, C])
        ln_rs = sb("ln_rs", [P, 5, FT])
        xnT = sb("xnT", [P, FT * P])
        xb = sb("xb", [P, 2, FT, C])
        gate = by_sin[:, :, :].rearrange("p a n -> p (a n)")[:, 0:3 * FT * P].rearrange("p (a n) -> p a n", a=3)
        hid = sb("hid", [P, 3, FT * P])
        def tiles4(ap):
            return ap.rearrange("p (t c) -> p t c", t=FT)

        q0, q0e = squares[:, 0:512], squares[:, 512:1024]
        k0, k0e = tiles4(squares[:, 1024:1536]), tiles4(squares[:, 1536:2048])
        qfT = by_cos[:, 0, :]
        kf, o0 = tiles4(by_cos[:, 1, 0:512]), tiles4(by_cos[:, 1, 512:1024])
        o0T = by_sin[:, 0, 0:512]
        v1 = tiles4(by_sin[:, 1, 0:FT * (C + 4)])
        spare = probs[:, :, :, :, :, :].rearrange("p a b c d e -> p (a b c d e)")
        kv_bd = spare[:, 0:C + H0]
        den = spare[:, C + H0:C + H0 + FT * H0].rearrange("p (t h) -> p t h", t=FT)

        cst_in, x_in, w0_in, wqk_in, wv_in, wo_in, sc_in, w1_in, w2_in, b1_in, ln_in, b2_in = [
            sem(n) for n in ("cst_in", "x_in", "w0_in", "wqk_in", "wv_in", "wo_in", "sc_in", "w1_in",
                             "w2_in", "b1_in", "ln_in", "b2_in")]
        out_done = sem("out_done")
        zeroed = sem("zeroed")
        consts_ready = sem("consts_ready")
        w0T_ps_ready, w0T_ready = sem("w0T_ps_ready"), sem("w0T_ready")
        f_step, f_xn, f_xnT_ps, f_xnT = [sem(n) for n in ("f_step", "f_xn", "f_xnT_ps", "f_xnT")]
        f_proj, f_min, f_exp, f_feat, f_kv, f_bd, f_num, f_den = [
            sem(n) for n in ("f_proj", "f_min", "f_exp", "f_feat", "f_kv", "f_bd", "f_num", "f_den")]
        f_o, f_oT_ps, f_oT, f_y, f_xb, f_x1, h_step = [
            sem(n) for n in ("f_o", "f_oT_ps", "f_oT", "f_y", "f_xb", "f_x1", "h_step")]
        x_ready = sem("x_ready")
        counts_tiles = []

        def tile_sem(name, n=None):
            sems = [sem(name if n is None else f"{name}{i}") for i in range(n or 1)]
            counts_tiles.extend(sems)
            return sems[0] if n is None else sems

        x_mid = tile_sem("x_mid")
        wvT_ps, wvT_ready, wvo_ps, wvo_ready = [sem(n) for n in ("wvT_ps", "wvT_ready", "wvo_ps", "wvo_ready")]
        tables_ready = sem("tables_ready")
        wq_hi_ready, wq_ready = sem("wq_hi_ready"), sem("wq_ready")
        shift_ps, xs_ready, xsT_ps, xsT_ready, xsT_hi_ready, xsT_lo_ready = [
            tile_sem(n) for n in ("shift_ps", "xs_ready", "xsT_ps", "xsT_ready", "xsT_hi_ready", "xsT_lo_ready")]
        projected, squared, summed, read, added = [
            {qk: tile_sem(f"{qk}_{n}") for qk in "qk"} for n in ("projected", "squared", "summed", "read", "added")]
        norm_step = sem("norm_step")
        k_rotated = tile_sem("k_rotated")
        qT_ps, qT_ready, kT_ps = [tile_sem(n, 2) for n in ("qT_ps", "qT_ready", "kT_ps")]
        kT_ready = {rows: tile_sem(f"kT_{rows}", 2) for rows in ("low", "high")}
        carried = sem("carried")
        s_ready, max_done, bias_ready, exp_done, rrow_ready, p_normed = [
            tile_sem(n, 2) for n in ("s_ready", "max_done", "bias_ready", "exp_done", "rrow_ready", "p_normed")]
        pT_ps, pT_ready = [tile_sem(n, 2) for n in ("pT_ps", "pT_ready")]
        vo_ps, vo_ready = [tile_sem(n, NW) for n in ("vo_ps", "vo_ready")]
        o_ps = tile_sem("o_ps")
        g_shift, g_xs, g_step, g_xn, g_xnT_ps, g_xnT, g_xb = [
            sem(n) for n in ("g_shift", "g_xs", "g_step", "g_xn", "g_xnT_ps", "g_xnT", "g_xb")]
        g_up, g_gelu, g_hid, g_down = [sem(n) for n in ("g_up", "g_gelu", "g_hid", "g_down")]
        final_ready = sem("final_ready")

        block = ctx.enter_context(nc.Block())

        def slot(i):
            return i + (i >> 3) + 1

        low_rows, high_rows = slice(0, D), slice(D, P)

        def x_cols(i, tiles=1, lo=0, n=C):
            view = x_tok[:, bass.ds((slot(i)) * C, tiles * C)]
            return view.rearrange("p (t c) -> p t c", c=C)[:, :, lo:lo + n] if tiles > 1 or n < C else view

        up_banks = [(q_ps[:, 0:512], q_ps[:, 512:1024]), (k_ps[:, 0:512], k_ps[:, 512:1024]),
                    (s_ps[:, 0, :], s_ps[:, 1, :])]

        def heads(ap, n=H):
            return ap.rearrange("p (h d) -> p h d", h=n)

        RING_USES = (("vo2", 8), ("qT0", 8), ("vo0", 8), ("pT0", 9), ("vo1", 8), ("qT1", 8), ("kT0", 8), ("kT1", 8), ("vo3", 8), ("pT1", 9), ("shift", 6), ("xsT", 6), ("pad", 0), ("o", 9))
        ring_names = [name for name, _ in RING_USES]

        def ring_bank(tile_par, use):
            i = ring_names.index(use)
            return (len(RING_USES) * ((tile_par + RING_USES[i][1]) % 2) + i) % RING_BANKS

        def use_before(i):
            j = i - RING_BANKS
            if ring_names[j] == "pad":
                j -= RING_BANKS
            return *RING_USES[j], int(j < 0)

        def schedule(loop, step, depth, after_loop=None):
            turns = (NT - depth) // 2
            for k in range(depth):
                step(k, k % 2, None)
            with loop(0, turns) as it:
                for r in range(2):
                    step(depth + r, (depth + r) % 2, it)
            k = depth + 2 * turns
            if after_loop:
                after_loop(k)
            for k in range(k, NT + depth):
                step(k, k % 2, None)

        def tile_numbers(l, k, it):
            if it is None:
                return k, NT * l + k
            return 2 * it + k, (NT * l + 2 * it) + k

        def there(k, it, s):
            return it is not None or 0 <= k - s < NT

        def done(T):
            return T + 1 + CREDIT

        def ahead(engine, value):
            engine.compute_val(value)
            return value

        @block.tensor
        def _(pe):
            mm = nc.tensor.matmul

            pe.wait_ge(cst_in, 16)
            pe.wait_ge(w0_in, 128)
            for i in range(4):
                last = nc.tensor.transpose(ring[:, 0, i * C:(i + 1) * C], w0[:, i, :], ident)
            last.then_inc(w0T_ps_ready, 1)
            pe.wait_ge(w0T_ready, 1)

            def wv_transposed(half, layer):
                pe.wait_ge(wv_in, 16 * layer + 16)
                for p in range(4 * half, 4 * half + 4):
                    last = nc.tensor.transpose(ring[:, 0, (p % 4) * C:(p % 4 + 1) * C], wv[:, p * C:(p + 1) * C], ident)
                last.then_inc(wvT_ps, 1)

            def wvo_product(r, layer):
                if r == 0:
                    pe.wait_ge(wo_in, 32 * layer + 32)
                    pe.wait_ge(wvT_ready, 2 * layer + 2)
                else:
                    pe.wait_ge(wvo_ready, WVO_ROUNDS * layer + r)
                for p in (2 * r, 2 * r + 1):
                    last = mm(ring[:, 0, (p % 2) * 2 * C:(p % 2 + 1) * 2 * C], wvT[:, p, :], wo_pad[:, p, :, :],
                              start=True, stop=True)
                last.then_inc(wvo_ps, 1)

            wv_transposed(0, 0)
            pe.wait_ge(wvT_ready, 1)
            wv_transposed(1, 0)
            for r in range(WVO_ROUNDS):
                wvo_product(r, 0)
            pe.wait_ge(wvo_ready, WVO_ROUNDS)

            with pe.Fori(0, B) as b:
                for gg in range(2):
                    G = 2 * b + gg
                    pe.wait_ge(f_xn, G + 1)
                    for t in range(FT):
                        last = nc.tensor.transpose(ring[:, 0, t * P:(t + 1) * P], xn4[:, t, :], ident)
                    last.then_inc(f_xnT_ps, 1)
                    pe.wait_ge(f_xnT, G + 1)
                    pe.wait_ge(f_feat, G)
                    mm(q_ps[:, 0:512], w0T[:, 0, :], xnT[:, :], start=True, stop=True)
                    for t in range(FT):
                        last = mm(k_ps[:, t * 256:(t + 1) * 256], xnT[:, t * P:(t + 1) * P],
                                  w0T[:, 1:3, :], start=True, stop=True)
                    last.then_inc(f_proj, 1)
                    if gg == 0:
                        pe.wait_ge(f_bd, b)
                    pe.wait_ge(f_feat, G + 1)
                    for t in range(FT):
                        last = mm(s_ps[:, 0, 0:C + 2], kf[:, t, :], v1[:, t, 0:C + 2],
                                  start=(gg == 0 and t == 0), stop=(gg == 1 and t == FT - 1))
                    last.then_inc(f_kv, 1)
                pe.wait_ge(f_bd, b + 1)
                for gg in range(2):
                    G = 2 * b + gg
                    pe.wait_ge(f_o, G)
                    for t in range(FT):
                        bank = q_ps[:, 512:1024] if t < 2 else s_ps[:, 1, :]
                        a = (t % 2) * (C + H0)
                        last = mm(bank[:, a:a + C + H0], qfT[:, (gg * FT + t) * P:(gg * FT + t + 1) * P],
                                  kv_bd[:, :], start=True, stop=True)
                    last.then_inc(f_num, 1)
                    pe.wait_ge(f_o, G + 1)
                    for t in range(FT):
                        last = nc.tensor.transpose(ring[:, 1, t * P:(t + 1) * P], o0[:, t, :], ident)
                    last.then_inc(f_oT_ps, 1)
                    pe.wait_ge(f_oT, G + 1)
                    for t in range(FT):
                        last = mm(ring[:, 0, t * C:(t + 1) * C], o0T[:, t * P:(t + 1) * P], w0T[:, 3, :],
                                  start=True, stop=True)
                    last.then_inc(f_y, 1)
                    pe.wait_ge(f_x1, G + 1)

            with pe.Fori(0, DEPTH) as l:
                pe.wait_ge(x_ready, NT * l + NT)
                pe.wait_ge(wvo_ready, WVO_ROUNDS * l + WVO_ROUNDS)
                pe.wait_ge(wq_ready, l + 1)

                def freed(use, T):
                    if use == "shift":
                        pe.wait_ge(xs_ready, done(T))
                    elif use == "xsT":
                        pe.wait_ge(xsT_ready, done(T))
                        pe.wait_ge(xsT_hi_ready, done(T))
                    elif use == "o":
                        pe.wait_ge(x_mid, done(T))
                    elif use[0] == "q":
                        pe.wait_ge(qT_ready[int(use[2])], done(T))
                    elif use[0] == "k":
                        pe.wait_ge(kT_ready["low"][int(use[2])], done(T))
                        pe.wait_ge(kT_ready["high"][int(use[2])], done(T))
                    elif use[0] == "p":
                        pe.wait_ge(pT_ready[int(use[2])], done(T))
                    else:
                        pe.wait_ge(vo_ready[int(use[2])], done(T))

                last_use = [None] * RING_BANKS

                def after_loop(k):
                    for step_before in (k - 2, k - 1):
                        for name, s in RING_USES:
                            if name != "pad":
                                last_use[ring_bank((step_before - s) % 2, name)] = name, NT * l + step_before - s

                def step(k, par, it):
                    t0, T0 = tile_numbers(l, k, it)

                    def bank(use, s):
                        i = ring_names.index(use)
                        b = ring_bank((par - s) % 2, use)
                        if it is not None:
                            name, s2, ago = use_before(i)
                            freed(name, T0 - s2 - ago)
                            if ago and par == 1 and last_use[b][0] != name:
                                freed(*last_use[b])
                        else:
                            if last_use[b]:
                                freed(*last_use[b])
                            last_use[b] = use, T0 - s
                        return ring[:, b, :]

                    def shifted(s):
                        if not there(k, it, s):
                            return
                        t, T = t0 - s, T0 - s
                        first = ahead(pe, (slot(t) - 1) * C)
                        r = bank("shift", s)
                        pe.wait_ge(x_ready, T + 1)
                        mm(r[:, 0:C], const("shift"), x_tok[:, bass.ds(first + C, C)], start=True, stop=False)
                        mm(r[:, 0:C], const("carry"), x_tok[:, bass.ds(first, C)],
                           start=False, stop=True).then_inc(shift_ps, 1)

                    def xs_transposed(s):
                        if not there(k, it, s):
                            return
                        T = T0 - s
                        r = bank("xsT", s)
                        pe.wait_ge(xs_ready, done(T))
                        nc.tensor.transpose(r[:, 0:P], xs[:, :], ident).then_inc(xsT_ps, 1)

                    def project(qk, n, s):
                        if not there(k, it, s):
                            return
                        T, a = T0 - s, (par - s) % 2
                        pe.wait_ge(xsT_hi_ready, done(T))
                        pe.wait_ge(xsT_lo_ready, done(T))
                        pe.wait_ge(read["k" if qk == "q" else "q"], done(T - 1 if qk == "q" else T))
                        cols = slice(INNER * (qk == "k") + n * 512, INNER * (qk == "k") + (n + 1) * 512)
                        half = qk_ps[:, n * 512:(n + 1) * 512]
                        mm(half, xsT_hi[:, a, :], wqk_hi[:, cols], start=True, stop=False)
                        mm(half, xsT_hi[:, a, :], wqk_lo[:, cols], start=False, stop=False)
                        last = mm(half, xsT_lo[:, a, :], wqk_hi[:, cols], start=False, stop=True)
                        if n == 1:
                            last.then_inc(projected[qk], 1)

                    def transposed(qk, half, s):
                        if not there(k, it, s):
                            return
                        T = T0 - s
                        r = bank(f"{qk}T{half}", s)
                        pe.wait_ge(k_rotated if qk == "k" else added["q"], done(T))
                        for p in range(4):
                            c = (4 * half + p) * P
                            last = nc.tensor.transpose(r[:, p * P:(p + 1) * P],
                                                       qk_rot[:, 1 if qk == "k" else 0, c:c + P], ident)
                        last.then_inc((kT_ps if qk == "k" else qT_ps)[half], 1)

                    def probs_transposed(half, s):
                        if not there(k, it, s):
                            return
                        T, a = T0 - s, (par - s) % 2
                        r = bank(f"pT{half}", s)
                        pe.wait_ge(p_normed[half], done(T))
                        for n in range(4):
                            quad, side = 2 * half + n // 2, n % 2
                            last = nc.tensor.transpose(r[:, n * P:(n + 1) * P],
                                                       probs[:, a, quad, side, :, :].rearrange("p h c -> p (h c)"),
                                                       ident)
                        last.then_inc(pT_ps[half], 1)

                    def scores(half, s):
                        if not there(k, it, s):
                            return
                        t, T, a = t0 - s, T0 - s, (par - s) % 2
                        if a == 0:
                            variant = (t >> 1) & (TPB // 2 - 1)
                            pe.wait_ge(carried, NT // 2 * l + (t >> 1) + 1)
                        else:
                            variant = 1
                        pe.wait_ge(exp_done[half], done(T - 1))
                        pe.wait_ge(qT_ready[half], done(T))
                        pe.wait_ge(kT_ready["low"][half], done(T))
                        pe.wait_ge(kT_ready["high"][half], done(T))
                        mask = mask_bf[:, bass.ds(variant * 2 * WIN, 2 * WIN)]
                        mm(s_ps[:, half, :], ident_bf[:, :], mask.unsqueeze(1).broadcast_to([P, 8, 2 * WIN]),
                           start=True, stop=False, skip_group_check=True)
                        for p in range(4):
                            for w in range(NW):
                                c = P * a + WIN * w
                                last = mm(s_ps[WIN * w:WIN * (w + 1), half, p * P:(p + 1) * P],
                                          qT[:, 4 * half + p, WIN * w:WIN * (w + 1)],
                                          kT[:, 4 * half + p, :, c:c + 2 * WIN],
                                          start=False, stop=True, skip_group_check=True)
                        last.then_inc(s_ready[half], 1)

                    def values(w, s):
                        if not there(k, it, s):
                            return
                        T, a = T0 - s, (par - s) % 2
                        r = bank(f"vo{w}", s)
                        pe.wait_ge(xsT_ready, done(T))
                        for mh in range(4):
                            last = mm(r[WIN * mh:WIN * (mh + 1), :], xsT[:, a, WIN * w:WIN * (w + 1)],
                                      wvo[:, mh, :, :], start=True, stop=True)
                        last.then_inc(vo_ps[w], 1)

                    def output(s):
                        if not there(k, it, s):
                            return
                        T, a = T0 - s, (par - s) % 2
                        r = bank("o", s)
                        for w in range(NW):
                            pe.wait_ge(vo_ready[w], done(T))
                        for half in range(2):
                            pe.wait_ge(pT_ready[half], done(T))
                        for n in range(2 * QUADS):
                            quad, side = n // 2, n % 2
                            for w in range(NW):
                                at_w = (NW * a + w - 1 + side) % (2 * NW)
                                last = mm(r[WIN * w:WIN * (w + 1), 0:C], pT[:, quad, side, WIN * w:WIN * (w + 1)],
                                          vo[:, at_w, quad * C:(quad + 1) * C],
                                          start=(n == 0), stop=(n == 2 * QUADS - 1))
                        last.then_inc(o_ps, 1)

                    values(2, 8)
                    transposed("q", 0, 8)
                    values(0, 8)
                    probs_transposed(0, 9)
                    values(1, 8)
                    transposed("q", 1, 8)
                    transposed("k", 0, 8)
                    project("k", 0, 7)
                    project("k", 1, 7)
                    transposed("k", 1, 8)
                    values(3, 8)
                    scores(0, 8)
                    probs_transposed(1, 9)
                    shifted(6)
                    scores(1, 8)
                    xs_transposed(6)
                    output(9)
                    project("q", 0, 6)
                    project("q", 1, 6)

                schedule(pe.Fori, step, 9, after_loop)

                pe.wait_ge(x_mid, done(NT * l + NT - 1))
                pe.wait_ge(w1_in, 16 * l + 16)
                pe.wait_ge(w2_in, 32 * l + 32)

                def shift4(u):
                    U = NG * l + u
                    if isinstance(u, int):
                        pe.wait_ge(g_xs, U)
                    else:
                        pe.wait_ge(g_xnT, U - 1)
                    here = x_cols(u * FT, FT).rearrange("p t c -> p (t c)")
                    mm(ring[:, 0, :], const("shift"), here, start=True, stop=False)
                    mm(ring[:, 0, :], const("carry"), x_tok[:, bass.ds((slot(u * FT) - 1) * C, FT * C)],
                       start=False, stop=True).then_inc(g_shift, 1)

                def transpose4(u):
                    U = NG * l + u
                    pe.wait_ge(g_xn, U + 1)
                    if not (isinstance(u, int) and u == NG - 1):
                        pe.wait_ge(g_xs, U + 2)
                    for t in range(FT):
                        last = nc.tensor.transpose(ring[:, 0, t * P:(t + 1) * P], xn4[:, t, :], ident)
                    last.then_inc(g_xnT_ps, 1)

                def up(u, i):
                    U = NG * l + u
                    if i == 0:
                        pe.wait_ge(g_xnT, U + 1)
                        pe.wait_ge(g_hid, 3 * U)
                    c, n = FB[i]
                    for j, off in ((1, F + c), (0, c)):
                        mm(up_banks[i][j][0:n, :], w1[:, off:off + n], xnT[:, :],
                           start=True, stop=True).then_inc(g_up, 1)

                def down(u):
                    U = NG * l + u
                    pe.wait_ge(x_ready, FT * U + NT)
                    pe.wait_ge(g_hid, 3 * U + 3)
                    for t in range(FT):
                        for i in range(3):
                            last = mm(ring[:, 1, t * C:(t + 1) * C], hid[:, i, t * P:(t + 1) * P], w2[:, i, :],
                                      start=(i == 0), stop=(i == 2))
                    last.then_inc(g_down, 1)

                shift4(0)
                shift4(1)
                transpose4(0)
                with pe.Fori(0, NG - 2) as u:
                    for i in range(3):
                        up(u, i)
                    shift4(u + 2)
                    transpose4(u + 1)
                    down(u)
                for i in range(3):
                    up(NG - 2, i)
                transpose4(NG - 1)
                down(NG - 2)
                pe.wait_ge(g_xnT, NG * l + NG)
                wv_transposed(0, l + 1)
                up(NG - 1, 0)
                pe.wait_ge(wvT_ready, 2 * l + 3)
                wv_transposed(1, l + 1)
                up(NG - 1, 1)
                wvo_product(0, l + 1)
                up(NG - 1, 2)
                wvo_product(1, l + 1)
                down(NG - 1)
                for r in range(2, WVO_ROUNDS):
                    wvo_product(r, l + 1)

        @block.vector
        def _(dve):
            v = nc.vector

            def rsqrt(y, src, t, h, first, steps, base, first_waits=True):
                ops = [
                    first,
                    lambda: v.tensor_scalar(t.bitcast(I32), src.bitcast(I32), 1, None, ALU.logical_shift_right),
                    lambda: v.tensor_scalar(y.bitcast(I32), t.bitcast(I32), -1.0, RSQRT_MAGIC, ALU.mult, ALU.add),
                ]
                for _ in range(3):
                    ops += [
                        lambda: v.tensor_tensor(t, y, y, ALU.mult),
                        lambda: v.scalar_tensor_tensor(h, t, -0.5, src, ALU.mult, ALU.mult),
                        lambda: v.scalar_tensor_tensor(y, h, 1.5, y, ALU.add, ALU.mult),
                    ]
                assert len(ops) == RSQRT_OPS

                def op(i):
                    if i or first_waits:
                        dve.wait_ge(steps, base + i)
                    ops[i]().then_inc(steps, 1)
                return op

            rows, var, rstd, ln_t, ln_h = (ln_rs[:, i, :] for i in range(5))

            def wide(ap):
                return ap.unsqueeze(2).broadcast_to([P, FT, C])

            def centred(src, G, step):
                v.tensor_reduce(rows, src, AX, ALU.add).then_inc(step, 1)
                dve.wait_ge(step, LN_STEPS * G + 1)
                v.scalar_tensor_tensor(xs4[:, :, :], wide(rows), -1.0 / C, src, ALU.mult, ALU.add).then_inc(step, 1)

            def squared4(scratch, G, step):
                dve.wait_ge(step, LN_STEPS * G + 2)
                v.tensor_tensor(scratch, xs4[:, :, :], xs4[:, :, :], ALU.mult).then_inc(step, 1)

            def variance(scratch, G, step):
                dve.wait_ge(step, LN_STEPS * G + 3)
                v.tensor_reduce(var, scratch, AX, ALU.add).then_inc(step, 1)

            def inverse_deviation(G, step, i0, i1):
                op = rsqrt(rstd, var, ln_t, ln_h, lambda: v.tensor_scalar(var, var, 1.0 / C, EPS, ALU.mult, ALU.add),
                           step, LN_STEPS * G + 4)
                for i in range(i0, i1):
                    op(i)

            def scaled(dst, G, step):
                dve.wait_ge(step, LN_STEPS * G + LN_STEPS)
                return v.tensor_tensor(dst, xs4[:, :, :], wide(rstd), ALU.mult)

            def layernorm4(src, dst, G, step, free):
                centred(src, G, step)
                dve.wait_ge(free, G)
                squared4(xn4[:, :, :], G, step)
                variance(xn4[:, :, :], G, step)
                inverse_deviation(G, step, 0, RSQRT_OPS)
                return scaled(dst, G, step)

            dve.wait_ge(cst_in, 16)
            v.tensor_copy(ident_bf[:, :], ident).then_inc(consts_ready, 1)
            v.tensor_copy(mask_bf[:, :], const("mask")).then_inc(consts_ready, 1)
            v.memset(x_tok[:, :], 0.0).then_inc(zeroed, 1)
            v.memset(v1[:, :, C:C + 4], 1.0)
            v.memset(kT[:, :, :, :], 0.0).then_inc(zeroed, 1)
            v.memset(wo_pad[0:D, :, 1, :], 0.0)
            v.memset(wo_pad[D:P, :, 0, :], 0.0)
            v.memset(hid[:, 2, :], 0.0)
            v.memset(w2[:, 2, :], 0.0).then_inc(zeroed, 1)
            v.memset(vo[:, 2 * NW - 1, :], 0.0).then_inc(zeroed, 1)
            dve.wait_ge(zeroed, 4)
            dve.wait_ge(x_in, 64)
            dve.wait_ge(w0_in, 128)

            with dve.Fori(0, B) as b:
                for gg in range(2):
                    G = 2 * b + gg
                    src = x_keep[:, bass.ds(G * FT, FT), :]
                    layernorm4(src, xn4[:, :, :], G, f_step, f_xnT_ps).then_inc(f_xn, 1)
                    dve.wait_ge(f_proj, G + 1)
                    dve.wait_ge(f_kv, G)
                    v.tensor_scalar(q0[:, :], q_ps[:, 0:512], bq_col[:, :], None, ALU.add).then_inc(f_min, 1)
                    kv_ps = k_ps.rearrange("p (t c) -> p t c", t=FT)
                    v.tensor_tensor(k0[:, :, :], kv_ps[:, :, 0:C],
                                    bkv_row[:, 0:C].unsqueeze(1).broadcast_to([P, FT, C]), ALU.add).then_inc(f_min, 1)
                    v.tensor_tensor(v1[:, :, 0:C], kv_ps[:, :, C:2 * C],
                                    bkv_row[:, C:2 * C].unsqueeze(1).broadcast_to([P, FT, C]), ALU.add)
                    dve.wait_ge(f_min, 4 * G + 1)
                    v.tensor_scalar(q0e[:, :], q0[:, :], 0.0, None, ALU.min).then_inc(f_min, 1)
                    dve.wait_ge(f_min, 4 * G + 2)
                    v.tensor_scalar(k0e[:, :, :], k0[:, :, :], 0.0, None, ALU.min).then_inc(f_min, 1)
                    dve.wait_ge(f_exp, 2 * G + 1)
                    if gg == 0:
                        dve.wait_ge(f_num, G)
                    v.scalar_tensor_tensor(qfT[:, gg * 512:(gg + 1) * 512], q0[:, :], 0.0, q0e[:, :],
                                           ALU.max, ALU.add)
                    dve.wait_ge(f_exp, 2 * G + 2)
                    v.scalar_tensor_tensor(kf[:, :, :], k0[:, :, :], 0.0, k0e[:, :, :],
                                           ALU.max, ALU.add).then_inc(f_feat, 1)
                dve.wait_ge(f_kv, 2 * b + 2)
                dve.wait_ge(f_num, 2 * b)
                v.tensor_tensor(kv_bd[:, 0:C], s_ps[:, 0, 0:C], const("blocks"), ALU.mult)
                v.tensor_tensor(kv_bd[:, C:C + H0], s_ps[:, 0, C:C + 1].broadcast_to([P, H0]), const("heads"),
                                ALU.mult).then_inc(f_bd, 1)
                for gg in range(2):
                    G = 2 * b + gg
                    tiles = x_keep[:, bass.ds(G * FT, FT), :]
                    dve.wait_ge(f_num, G + 1)
                    halves = [ps.rearrange("p (t c) -> p t c", t=2)
                              for ps in (q_ps[:, 512:512 + 2 * (C + H0)], s_ps[:, 1, 0:2 * (C + H0)])]
                    for n in range(2):
                        v.tensor_scalar(den[:, 2 * n:2 * n + 2, :], halves[n][:, :, C:C + H0], 1e-6, None,
                                        ALU.max).then_inc(f_den, 1)
                    dve.wait_ge(f_den, 3 * G + 2)
                    v.reciprocal(den[:, :, :], den[:, :, :]).then_inc(f_den, 1)
                    dve.wait_ge(f_den, 3 * G + 3)
                    dve.wait_ge(f_oT_ps, G)
                    for n in range(2):
                        for t in range(2):
                            i = 2 * n + t
                            last = v.tensor_tensor(heads(o0[:, i, :], H0), heads(halves[n][:, t, 0:C], H0),
                                                   den[:, i, :].unsqueeze(2).broadcast_to([P, H0, D0]), ALU.mult)
                    last.then_inc(f_o, 1)
                    dve.wait_ge(f_y, G + 1)
                    dve.wait_ge(f_xb, G + 1)
                    y = tiles4(ring[:, 0, :])
                    v.tensor_tensor(xb[:, 1, :, :], y, xb[:, 0, :, :], ALU.add)
                    v.tensor_tensor(tiles, y, xb[:, 0, :, :], ALU.add).then_inc(f_x1, 1)
                    dve.wait_ge(f_x1, G + 1)
                    layernorm4(xb[:, 1, :, :], x_cols(G * FT, FT), G, h_step, f_xnT_ps).then_inc(x_ready, FT)

            with dve.Fori(0, DEPTH) as l:
                dve.wait_ge(tables_ready, l + 1)

                def step(k, par, it):
                    t0, T0 = tile_numbers(l, k, it)

                    def copy(out_, in_):
                        return v.tensor_copy(out_, in_)

                    def k_evacuated(which, half, s):
                        if not there(k, it, s):
                            return
                        t, T, a = t0 - s, T0 - s, (par - s) % 2
                        rows, n = (low_rows, 0) if which == "low" else (high_rows, 1)
                        off = WIN + P * a
                        if a == 1:
                            dve.wait_ge(carried, NT // 2 * l + (t >> 1) + 1)
                        for h in range(2):
                            dve.wait_ge(s_ready[h], done(T - 1))
                        dve.wait_ge(kT_ps[half], done(T))
                        copy(kT[rows, 4 * half:4 * half + 4, n, off:off + P],
                             ring[rows, ring_bank(a, f"kT{half}"), :].rearrange("p (n t) -> p n t", n=4)
                             ).then_inc(kT_ready[which][half], 1)

                    def vo_evacuated(w, s):
                        if not there(k, it, s):
                            return
                        T, a = T0 - s, (par - s) % 2
                        dve.wait_ge(o_ps, done(T - 1 if w == NW - 1 else T - 2))
                        dve.wait_ge(vo_ps[w], done(T))
                        copy(vo[:, NW * a + w, :], ring[:, ring_bank(a, f"vo{w}"), :]).then_inc(vo_ready[w], 1)

                    def p_evacuated(half, s):
                        if not there(k, it, s):
                            return
                        T, a = T0 - s, (par - s) % 2
                        dve.wait_ge(o_ps, done(T - 1))
                        dve.wait_ge(pT_ps[half], done(T))
                        copy(pT[:, 2 * half:2 * half + 2, :, :].rearrange("p a b c -> p (a b c)"),
                             ring[:, ring_bank(a, f"pT{half}"), :]).then_inc(pT_ready[half], 1)

                    def xsT_lower(s):
                        if not there(k, it, s):
                            return
                        T, a = T0 - s, (par - s) % 2
                        dve.wait_ge(xsT_ready, done(T))
                        dve.wait_ge(xsT_hi_ready, done(T))
                        v.tensor_tensor(xsT_lo[:, a, :], xsT[:, a, :], xsT_hi[:, a, :].bitcast(F32),
                                        ALU.subtract).then_inc(xsT_lo_ready, 1)

                    def row_reciprocals(half, s):
                        if not there(k, it, s):
                            return
                        T, h = T0 - s, slice(8 * half, 8 * half + 8)
                        dve.wait_ge(p_normed[half], done(T - 1))
                        dve.wait_ge(exp_done[half], done(T))
                        v.reciprocal(rrow[:, h], psum_row[:, h]).then_inc(rrow_ready[half], 1)

                    def rotate(qk, part, s):
                        if not there(k, it, s):
                            return
                        t, T, n = t0 - s, T0 - s, "qk".index(qk)
                        angles = ahead(dve, (t & (TPB - 1)) * D)
                        if part == 0:
                            dve.wait_ge(added[qk], done(T - 1))
                            dve.wait_ge(squared[qk], done(T))
                        last = v.tensor_tensor(heads((by_sin if part else by_cos)[:, n, :]),
                                               heads(qk_ps[:, :]),
                                               rotary[2 * n + part][:, bass.ds(angles, D)].unsqueeze(1)
                                               .broadcast_to([P, H, D]), ALU.mult)
                        if part == 1:
                            last.then_inc(read[qk], 1)

                    def sum_of_squares(qk, s):
                        if not there(k, it, s):
                            return
                        T, n = T0 - s, "qk".index(qk)
                        dve.wait_ge(squared[qk], done(T))
                        v.tensor_reduce(sumsq[:, n * H:(n + 1) * H],
                                        heads(squares[:, n * INNER:(n + 1) * INNER]), AX,
                                        ALU.add).then_inc(summed[qk], 1)

                    def inverse_norms(i0, i1, s):
                        if not there(k, it, s):
                            return
                        T, a = T0 - s, (par - s) % 2
                        if i0 == 0:
                            dve.wait_ge(summed["q"], done(T))
                            dve.wait_ge(summed["k"], done(T))
                        if i0 <= 2 < i1:
                            dve.wait_ge(k_rotated, done(T - 2))
                        op = rsqrt(rnorm[:, a, :], sumsq[:, :], rs_t[:, :], rs_h[:, :],
                                   lambda: v.tensor_scalar(sumsq[:, :], sumsq[:, :], 1e-24, None, ALU.max),
                                   norm_step, RSQRT_OPS * T, False)
                        for i in range(i0, i1):
                            op(i)

                    def carry(s):
                        if not there(k, it, s) or (par - s) % 2 == 1:
                            return
                        t, T = t0 - s, T0 - s
                        n = ahead(dve, (t >> 1) & (TPB // 2 - 1))
                        for h in range(2):
                            dve.wait_ge(s_ready[h], done(T - 2))
                            dve.wait_ge(kT_ready["low"][h], done(T - 1))
                            dve.wait_ge(kT_ready["high"][h], done(T - 1))
                        keep = const("keep")[:, bass.ds(n, 1)].unsqueeze(2).broadcast_to([P, H, WIN])
                        v.tensor_tensor(kT[:, :, :, 0:WIN].rearrange("p a b c -> p (a b) c"),
                                        kT[:, :, :, RING - WIN:RING].rearrange("p a b c -> p (a b) c"),
                                        keep, ALU.mult).then_inc(carried, 1)

                    def maxima(half, s):
                        if not there(k, it, s):
                            return
                        T = T0 - s
                        dve.wait_ge(s_ready[half], done(T))
                        v.tensor_reduce(smax[:, 8 * half:8 * half + 8], heads(s_ps[:, half, :], 8), AX,
                                        ALU.max).then_inc(max_done[half], 1)

                    def softmax_bias(half, s):
                        if not there(k, it, s):
                            return
                        T, a, h = T0 - s, (par - s) % 2, slice(8 * half, 8 * half + 8)
                        dve.wait_ge(exp_done[half], done(T - 1))
                        dve.wait_ge(norm_step, RSQRT_OPS * T + RSQRT_OPS)
                        dve.wait_ge(max_done[half], done(T))
                        v.scalar_tensor_tensor(nbias[:, h], smax[:, h], -1.0, rnorm[:, a, h], ALU.mult,
                                               ALU.mult).then_inc(bias_ready[half], 1)

                    def residual(s):
                        if not there(k, it, s):
                            return
                        t, T, a = t0 - s, T0 - s, (par - s) % 2
                        x_old = x_tok[:, bass.ds(ahead(dve, slot(t) * C), C)]
                        dve.wait_ge(o_ps, done(T))
                        v.tensor_tensor(x_old, ring[:, ring_bank(a, "o"), 0:C], x_old, ALU.add).then_inc(x_mid, 1)

                    p_evacuated(0, 3)
                    carry(2)
                    k_evacuated("high", 0, 2)
                    row_reciprocals(1, 3)
                    sum_of_squares("q", 1)
                    sum_of_squares("k", 1)
                    inverse_norms(0, 1, 1)
                    maxima(0, 2)
                    inverse_norms(1, 2, 1)
                    rotate("k", 0, 1)
                    inverse_norms(2, 3, 1)
                    softmax_bias(0, 2)
                    inverse_norms(3, 4, 1)
                    rotate("k", 1, 1)
                    inverse_norms(4, 5, 1)
                    xsT_lower(0)
                    inverse_norms(5, 7, 1)
                    residual(3)
                    inverse_norms(7, 8, 1)
                    maxima(1, 2)
                    inverse_norms(8, 10, 1)
                    row_reciprocals(0, 2)
                    inverse_norms(10, 11, 1)
                    softmax_bias(1, 2)
                    inverse_norms(11, 12, 1)
                    vo_evacuated(2, 1)
                    rotate("q", 0, 0)
                    rotate("q", 1, 0)
                    vo_evacuated(1, 1)

                schedule(dve.Fori, step, 3)

                dve.wait_ge(b1_in, 96 * l + 96)

                squares4 = squares[:, 0:FT * C].rearrange("p (t c) -> p t c", t=FT)

                def sums(u):
                    U = NG * l + u
                    dve.wait_ge(g_xs, U + 1)
                    centred(xs4[:, :, :], U, g_step)
                    squared4(squares4, U, g_step)
                    variance(squares4, U, g_step)

                def normalised(u):
                    U = NG * l + u
                    dve.wait_ge(g_xnT_ps, U)
                    scaled(xn4[:, :, :], U, g_step).then_inc(g_xn, 1)

                def hidden(u, i):
                    U = NG * l + u
                    c, n = FB[i]
                    if i == 0:
                        dve.wait_ge(g_down, U)
                    dve.wait_ge(g_up, 6 * U + 2 * i + 2)
                    dve.wait_ge(g_gelu, 3 * U + i + 1)
                    v.scalar_tensor_tensor(hid[0:n, i, :], up_banks[i][0][0:n, :], b1_col[0:n, 0, i:i + 1],
                                           gate[0:n, i, :], ALU.add, ALU.mult).then_inc(g_hid, 1)

                def x_new(u):
                    U = NG * l + u
                    tiles = x_cols(u * FT, FT)
                    dve.wait_ge(g_xb, U + 1)
                    dve.wait_ge(g_down, U + 1)
                    v.tensor_tensor(tiles, ring[:, 1, :].rearrange("p (t c) -> p t c", t=FT),
                                    xb[:, 0, :, :], ALU.add).then_inc(x_ready, FT)

                def step4(u, more, next):
                    if next:
                        inverse_deviation(NG * l + u + 1, g_step, 0, RSQRT_OPS // 2)
                    hidden(u, 0)
                    if next:
                        inverse_deviation(NG * l + u + 1, g_step, RSQRT_OPS // 2, RSQRT_OPS)
                        normalised(u + 1)
                    hidden(u, 1)
                    hidden(u, 2)
                    if more:
                        sums(u + 2)
                    x_new(u)

                sums(0)
                inverse_deviation(NG * l, g_step, 0, RSQRT_OPS)
                normalised(0)
                sums(1)
                with dve.Fori(0, NG - 2) as u:
                    step4(u, True, True)
                step4(NG - 2, False, True)
                step4(NG - 1, False, False)

            dve.wait_ge(x_ready, NT * (DEPTH + 1))
            for b in range(B):
                tiles = x_keep[:, b * TPB:(b + 1) * TPB, :]
                v.tensor_tensor(tiles, tiles, x_cols(b * TPB, TPB), ALU.add).then_inc(final_ready, 1)

        @block.scalar
        def _(act):
            def copy(out_, in_):
                return nc.scalar.activation(out_, in_, ACT.Copy)

            act.wait_ge(w0T_ps_ready, 1)
            copy(w0T[:, :, :].rearrange("p a c -> p (a c)"), ring[:, 0, :]).then_inc(w0T_ready, 1)

            def wvT_evacuated(half, layer):
                act.wait_ge(wvT_ps, 2 * layer + half + 1)
                copy(wvT[:, 4 * half:4 * half + 4, :].rearrange("p a c -> p (a c)"),
                     ring[:, 0, :]).then_inc(wvT_ready, 1)

            def wvo_evacuated(r, layer):
                act.wait_ge(wvo_ps, WVO_ROUNDS * layer + r + 1)
                copy(wvo[:, :, r, :], ring[:, 0, :].rearrange("p (a c) -> p a c", a=4)).then_inc(wvo_ready, 1)

            def wqk_upper(layer):
                act.wait_ge(wqk_in, 16 * layer + 16)
                copy(wqk_hi[:, :], wqk).then_inc(wq_hi_ready, 1)

            for half in range(2):
                wvT_evacuated(half, 0)
            wqk_upper(0)
            for r in range(WVO_ROUNDS):
                wvo_evacuated(r, 0)

            with act.Fori(0, B) as b:
                for gg in range(2):
                    G = 2 * b + gg
                    act.wait_ge(f_xnT_ps, G + 1)
                    act.wait_ge(f_proj, G)
                    copy(xnT[:, :], ring[:, 0, :]).then_inc(f_xnT, 1)
                    act.wait_ge(f_min, 4 * G + 3)
                    nc.scalar.activation(q0e[:, :], q0e[:, :], ACT.Exp).then_inc(f_exp, 1)
                    act.wait_ge(f_min, 4 * G + 4)
                    nc.scalar.activation(k0e[:, :, :], k0e[:, :, :], ACT.Exp).then_inc(f_exp, 1)
                for gg in range(2):
                    G = 2 * b + gg
                    act.wait_ge(f_oT_ps, G + 1)
                    act.wait_ge(f_y, G)
                    copy(o0T[:, :], ring[:, 1, :]).then_inc(f_oT, 1)

            with act.Fori(0, DEPTH) as l:
                def step(k, par, it):
                    t0, T0 = tile_numbers(l, k, it)

                    def xs_written(s):
                        if not there(k, it, s):
                            return
                        t, T, a = t0 - s, T0 - s, (par - s) % 2
                        kept = x_tok[:, bass.ds(ahead(act, slot(t) * C), C // 2)]
                        act.wait_ge(xsT_ps, done(T - 1))
                        act.wait_ge(shift_ps, done(T))
                        copy(xs[:, C // 2:C], ring[:, ring_bank(a, "shift"), C // 2:C])
                        copy(xs[:, 0:C // 2], kept).then_inc(xs_ready, 1)

                    def q_evacuated(half, s):
                        if not there(k, it, s):
                            return
                        T, a = T0 - s, (par - s) % 2
                        act.wait_ge(s_ready[half], done(T - 1))
                        act.wait_ge(qT_ps[half], done(T))
                        copy(qT[:, 4 * half:4 * half + 4, :],
                             ring[:, ring_bank(a, f"qT{half}"), :].rearrange("p (n t) -> p n t", n=4)
                             ).then_inc(qT_ready[half], 1)

                    def k_evacuated(which, half, s):
                        if not there(k, it, s):
                            return
                        t, T, a = t0 - s, T0 - s, (par - s) % 2
                        rows, n = (low_rows, 0) if which == "low" else (high_rows, 1)
                        off = WIN + P * a
                        if a == 1:
                            act.wait_ge(carried, NT // 2 * l + (t >> 1) + 1)
                        for h in range(2):
                            act.wait_ge(s_ready[h], done(T - 1))
                        act.wait_ge(kT_ps[half], done(T))
                        copy(kT[rows, 4 * half:4 * half + 4, n, off:off + P],
                             ring[rows, ring_bank(a, f"kT{half}"), :].rearrange("p (n t) -> p n t", n=4)
                             ).then_inc(kT_ready[which][half], 1)

                    def vo_evacuated(w, s):
                        if not there(k, it, s):
                            return
                        T, a = T0 - s, (par - s) % 2
                        act.wait_ge(o_ps, done(T - 1 if w == NW - 1 else T - 2))
                        act.wait_ge(vo_ps[w], done(T))
                        copy(vo[:, NW * a + w, :], ring[:, ring_bank(a, f"vo{w}"), :]).then_inc(vo_ready[w], 1)

                    def p_evacuated(half, s):
                        if not there(k, it, s):
                            return
                        T, a = T0 - s, (par - s) % 2
                        act.wait_ge(o_ps, done(T - 1))
                        act.wait_ge(pT_ps[half], done(T))
                        copy(pT[:, 2 * half:2 * half + 2, :, :].rearrange("p a b c -> p (a b c)"),
                             ring[:, ring_bank(a, f"pT{half}"), :]).then_inc(pT_ready[half], 1)

                    def xsT_evacuated(s):
                        if not there(k, it, s):
                            return
                        T, a = T0 - s, (par - s) % 2
                        act.wait_ge(xsT_ps, done(T))
                        copy(xsT[:, a, :], ring[:, ring_bank(a, "xsT"), 0:P]).then_inc(xsT_ready, 1)

                    def xsT_upper(s):
                        if not there(k, it, s):
                            return
                        T, a = T0 - s, (par - s) % 2
                        act.wait_ge(xsT_ps, done(T))
                        copy(xsT_hi[:, a, :], ring[:, ring_bank(a, "xsT"), 0:P]).then_inc(xsT_hi_ready, 1)

                    def square(qk, s):
                        if not there(k, it, s):
                            return
                        T, n = T0 - s, "qk".index(qk)
                        act.wait_ge(summed[qk], done(T - 1))
                        act.wait_ge(projected[qk], done(T))
                        nc.scalar.activation(squares[:, n * INNER:(n + 1) * INNER], qk_ps[:, :],
                                             ACT.Square).then_inc(squared[qk], 1)

                    def exponentials(h0, s):
                        if not there(k, it, s):
                            return
                        T, a, half = T0 - s, (par - s) % 2, h0 // 8
                        if h0 % 8 == 0:
                            act.wait_ge(rrow_ready[half], done(T - 1))
                            act.wait_ge(pT_ps[half], done(T - 2))
                            act.wait_ge(bias_ready[half], done(T))
                        for h in (h0, h0 + 1):
                            c = h % 8 * 2 * WIN
                            last = nc.scalar.activation(
                                probs[:, a, h // 4, :, h % 4, :],
                                s_ps[:, half, c:c + 2 * WIN].rearrange("p (s c) -> p s c", s=2), ACT.Exp,
                                scale=rnorm[:, a, h:h + 1], bias=nbias[:, h:h + 1],
                                accum_out=psum_row[:, h:h + 1])
                        if h0 % 8 == 6:
                            last.then_inc(exp_done[half], 1)

                    exponentials(4, 3)
                    exponentials(6, 3)
                    vo_evacuated(3, 3)
                    square("q", 1)
                    exponentials(8, 3)
                    q_evacuated(0, 2)
                    vo_evacuated(0, 2)
                    exponentials(10, 3)
                    exponentials(12, 3)
                    exponentials(14, 3)
                    k_evacuated("low", 0, 2)
                    q_evacuated(1, 2)
                    square("k", 1)
                    k_evacuated("high", 1, 2)
                    k_evacuated("low", 1, 2)
                    p_evacuated(1, 3)
                    xs_written(0)
                    xsT_evacuated(0)
                    exponentials(0, 2)
                    xsT_upper(0)
                    exponentials(2, 2)

                schedule(act.Fori, step, 3)

                act.wait_ge(ln_in, 32 * l + 32)
                act.wait_ge(b1_in, 96 * l + 96)

                def shifted(u):
                    U = NG * l + u
                    kept = x_cols(u * FT, FT, 0, C // 2)
                    act.wait_ge(g_shift, U + 1)
                    act.wait_ge(g_xn, U)
                    bank = ring[:, 0, :].rearrange("p (t c) -> p t c", t=FT)
                    copy(xs4[:, :, C // 2:C], bank[:, :, C // 2:C])
                    copy(xs4[:, :, 0:C // 2], kept).then_inc(g_xs, 1)

                def transposed(u):
                    U = NG * l + u
                    act.wait_ge(g_xnT_ps, U + 1)
                    nc.scalar.activation(xnT[:, :], ring[:, 0, :], ACT.Identity, scale=ln_col[:, 0:1],
                                         bias=ln_col[:, 1:2]).then_inc(g_xnT, 1)

                def gelu(u, i):
                    U = NG * l + u
                    c, n = FB[i]
                    act.wait_ge(g_hid, 3 * U)
                    act.wait_ge(g_up, 6 * U + 2 * i + 1)
                    nc.scalar.activation(gate[0:n, i, :], up_banks[i][1][0:n, :], ACT.Gelu,
                                         bias=b1_col[0:n, 1, i:i + 1]).then_inc(g_gelu, 1)

                shifted(0)
                shifted(1)
                transposed(0)
                wqk_upper(l + 1)
                with act.Fori(0, NG - 2) as u:
                    for i in range(3):
                        gelu(u, i)
                    shifted(u + 2)
                    transposed(u + 1)
                for i in range(3):
                    gelu(NG - 2, i)
                transposed(NG - 1)
                wvT_evacuated(0, l + 1)
                gelu(NG - 1, 0)
                wvT_evacuated(1, l + 1)
                gelu(NG - 1, 1)
                wvo_evacuated(0, l + 1)
                gelu(NG - 1, 2)
                for r in range(1, WVO_ROUNDS):
                    wvo_evacuated(r, l + 1)

        @block.gpsimd
        def _(pool):
            g = nc.gpsimd

            pool.wait_ge(x_in, 64)
            pool.wait_ge(w0_in, 128)
            with pool.Fori(0, NG) as G:
                pool.wait_ge(f_x1, G)
                g.tensor_tensor(xb[:, 0, :, :], x_keep[:, bass.ds(G * FT, FT), :],
                                bo_row[:, :].unsqueeze(1).broadcast_to([P, FT, C]), ALU.add).then_inc(f_xb, 1)

            def tables(layer):
                pool.wait_ge(sc_in, 32 * layer + 32)
                if not isinstance(layer, int):
                    pool.wait_ge(read["k"], done(NT * layer - 1))
                for n in range(4):
                    last = g.tensor_tensor(rotary[n][:, :].rearrange("p (j d) -> p j d", j=TPB), rotary0[:, n],
                                           qk_scales[:, n // 2, :].unsqueeze(1).broadcast_to([P, TPB, D]), ALU.mult)
                last.then_inc(tables_ready, 1)

            def wqk_lower(layer):
                pool.wait_ge(wq_hi_ready, layer + 1)
                g.tensor_tensor(wqk_lo[:, :], wqk, wqk_hi[:, :].bitcast(F32), ALU.subtract).then_inc(wq_ready, 1)

            tables(0)
            wqk_lower(0)
            with pool.Fori(0, DEPTH) as l:
                def step(k, par, it):
                    t0, T0 = tile_numbers(l, k, it)

                    def normalise(half, s):
                        if not there(k, it, s):
                            return
                        T, a = T0 - s, (par - s) % 2
                        pool.wait_ge(rrow_ready[half], done(T))
                        for quad in (2 * half, 2 * half + 1):
                            p = probs[:, a, quad]
                            r = rrow[:, 4 * quad:4 * quad + 4].unsqueeze(1).unsqueeze(3).broadcast_to([P, 2, 4, WIN])
                            last = g.tensor_tensor(p, p, r, ALU.mult)
                        last.then_inc(p_normed[half], 1)

                    def add_rotated(qk, s):
                        if not there(k, it, s):
                            return
                        T, n = T0 - s, "qk".index(qk)
                        for half in range(2):
                            pool.wait_ge((qT_ps, kT_ps)[n][half], done(T - 1))
                        pool.wait_ge(read[qk], done(T))
                        d, cs, sn = heads(qk_rot[:, n, :]), heads(by_cos[:, n, :]), heads(by_sin[:, n, :])
                        lo, hi = slice(0, D // 2), slice(D // 2, D)
                        g.tensor_tensor(d[:, :, lo], cs[:, :, lo], sn[:, :, hi], ALU.add)
                        g.tensor_tensor(d[:, :, hi], cs[:, :, hi], sn[:, :, lo], ALU.add).then_inc(added[qk], 1)

                    def normalise_k(s):
                        if not there(k, it, s):
                            return
                        T, a = T0 - s, (par - s) % 2
                        pool.wait_ge(added["k"], done(T))
                        pool.wait_ge(norm_step, RSQRT_OPS * T + RSQRT_OPS)
                        kk = heads(qk_rot[:, 1, :])
                        g.tensor_tensor(kk, kk, rnorm[:, a, H:2 * H].unsqueeze(2).broadcast_to([P, H, D]),
                                        ALU.mult).then_inc(k_rotated, 1)

                    normalise_k(1)
                    add_rotated("q", 0)
                    normalise(1, 2)
                    add_rotated("k", 0)
                    normalise(0, 1)

                schedule(pool.Fori, step, 2)

                tables(l + 1)
                wqk_lower(l + 1)
                with pool.Fori(0, NG) as u:
                    tiles = x_cols(u * FT, FT)
                    pool.wait_ge(b2_in, 16 * l + 16)
                    pool.wait_ge(x_mid, done(NT * l + FT * u + FT - 1))
                    pool.wait_ge(x_ready, NT * l + FT * u + NT)
                    g.tensor_tensor(xb[:, 0, :, :], tiles,
                                    b2_row[:, :].unsqueeze(1).broadcast_to([P, FT, C]), ALU.add).then_inc(g_xb, 1)

        @block.sync
        def _(sp):
            def load(dst, src, done):
                sp.dma_start(dst, src).then_inc(done, 16)

            def col(ap):
                return ap.rearrange("(p a) -> p a", a=1)

            def row(ap):
                return ap.partition_broadcast(P)

            load(cst[:, :], consts, cst_in)
            for s in counts_tiles:
                sp.sem_inc(s, CREDIT)
            for i, w in enumerate((Wq, Wk, Wv, Wo)):
                load(w0[:, i, :], w, w0_in)
            load(bq_col[:, :], col(bq), w0_in)
            load(bkv_row[:, 0:C], row(bk), w0_in)
            load(bkv_row[:, C:2 * C], row(bv), w0_in)
            load(bo_row[:, :], row(bo), w0_in)
            for b in range(B):
                load(x_keep[:, b * TPB:(b + 1) * TPB, :], x[b].rearrange("(t p) c -> p t c", p=P), x_in)
            sp.wait_ge(zeroed, 4)

            def attention_weights(i):
                layer = bass.ds(i, 1)
                w = Wqkv[layer, :, :].rearrange("l c n -> (l c) n")
                load(wqk, w[:, 0:2 * INNER], wqk_in)
                load(wv[:, :], w[:, 2 * INNER:3 * INNER], wv_in)
                wo = Wout[layer, :, :].rearrange("l (q a d) c -> (l a) d q c", a=2, d=D)
                load(wo_pad[low_rows, :, 0, :], wo[0], wo_in)
                load(wo_pad[high_rows, :, 1, :], wo[1], wo_in)

            def scales(i):
                layer = bass.ds(i, 1)
                load(qk_scales[:, 0, :], row(q_scale[layer, :].rearrange("l d -> (l d)")), sc_in)
                load(qk_scales[:, 1, :], row(k_scale[layer, :].rearrange("l d -> (l d)")), sc_in)

            scales(0)
            attention_weights(0)
            with sp.Fori(0, DEPTH) as l:
                layer = bass.ds(l, 1)
                sp.wait_ge(x_ready, NT * l + NT)
                load(w1[:, :], W1[layer, :, :].rearrange("l c n -> (l c) n"), w1_in)
                wd = W2[layer, :, :].rearrange("l n c -> (l n) c")
                load(w2[:, 0:2, :], wd[0:2 * P, :].rearrange("(i p) c -> p i c", p=P), w2_in)
                load(w2[0:F - 2 * P, 2, :], wd[2 * P:F, :], w2_in)
                bias = b1[layer, :].rearrange("l n -> (l n)")
                for j in range(2):
                    for i, (c, n) in enumerate(FB):
                        load(b1_col[0:n, j, i:i + 1], col(bias[j * F + c:j * F + c + n]), b1_in)
                load(ln_col[:, 0:1], col(ln_g[layer, :].rearrange("l n -> (l n)")), ln_in)
                load(ln_col[:, 1:2], col(ln_b[layer, :].rearrange("l n -> (l n)")), ln_in)
                load(b2_row[:, :], row(b2[layer, :].rearrange("l n -> (l n)")), b2_in)
                after = (l + 1) % DEPTH
                sp.wait_ge(tables_ready, l + 1)
                scales(after)
                for w in range(NW):
                    sp.wait_ge(vo_ps[w], done(NT * l + NT - 1))
                sp.wait_ge(k_rotated, done(NT * l + NT - 1))
                for half in range(2):
                    sp.wait_ge(qT_ps[half], done(NT * l + NT - 1))
                    sp.wait_ge(kT_ps[half], done(NT * l + NT - 1))
                attention_weights(after)
            for b in range(B):
                sp.wait_ge(final_ready, b + 1)
                sp.dma_start(out[b].rearrange("(t p) c -> p t c", p=P),
                             x_keep[:, b * TPB:(b + 1) * TPB, :]).then_inc(out_done, 16)
            sp.wait_ge(out_done, 16 * B)


_INS = ["L0_attn_x", "L0_attn_Wq", "L0_attn_bq", "L0_attn_Wk", "L0_attn_bk", "L0_attn_Wv", "L0_attn_bv",
        "L0_attn_Wo", "L0_attn_bo", "L0_ffn_Wqkv", "L0_ffn_q_scale", "L0_ffn_k_scale", "L0_ffn_Wo",
        "L0_ffn_ln_g", "L0_ffn_ln_b", "L0_ffn_W1", "L0_ffn_b1", "L0_ffn_W2", "L0_ffn_b2"]


def kernel(**inputs):
    import concourse.bacc as bacc
    from concourse.bass_utils import run_bass_kernel_spmd

    nc = bacc.Bacc("TRN2", target_bir_lowering=False, num_devices=1)
    table, at = constants()
    arrays = {"consts": table}
    for name in _INS:
        arrays[name] = np.ascontiguousarray(inputs[name])
    args = [nc.dram_tensor(n, a.shape, mybir.dt.from_np(a.dtype), kind="ExternalInput").ap()
            for n, a in arrays.items()]
    out = nc.dram_tensor("out", (B, N, C), F32, kind="ExternalOutput").ap()
    build(nc, args[0], at, *args[1:], out)
    r = run_bass_kernel_spmd(nc, [arrays], core_ids=[0])
    return r.results[0]["out"]
```

```python
from contextlib import ExitStack

import numpy as np

import concourse.bass as bass
from concourse import mybir

F32 = mybir.dt.float32
F32R = mybir.dt.float32r
I32 = mybir.dt.int32
BF16 = mybir.dt.bfloat16
ACT = mybir.ActivationFunctionType
ALU = mybir.AluOpType
AX = mybir.AxisListType.X

P = 128
B, N, C = 4, 1024, 128
TPB = N // P
NT = B * TPB
DEPTH, H, D, WIN = 6, 16, 64, 32
PAIRS = H // 2
WVO_ROUNDS = PAIRS // 2
QUADS = H // 4
NW = P // WIN
INNER = H * D
F = int(C * 4 * 2 / 3)
FB = [(0, 128), (128, 128), (256, F - 256)]
W1_COLS = F + FB[2][0] + P
FT = 4
NG = NT // FT
H0, D0 = 16, 8
EPS = 1e-5
NEG = -1e30
CREDIT = 3
RING_BANKS = 4
RING = WIN + 2 * P
RSQRT_MAGIC = 1597463007.0
RSQRT_OPS = 11
NEWTON_OPS = 12


def rotary_constants():
    f = np.float32
    half = np.arange(0, D, 2, dtype=f)
    inv_freq = f(1.0) / np.power(f(10000.0), half / f(D), dtype=f)
    t = np.arange(N, dtype=f)
    freqs = np.concatenate([t[:, None] * inv_freq[None]] * 2, -1)
    base = (half + f(0.4 * D)) / f(1.4 * D)
    power = (t - N // 2) / f(WIN // 2)
    scale = np.power(base[None], power[:, None], dtype=f)
    scale = np.concatenate([scale, scale], -1)
    inv = f(1.0) / scale
    sign = np.where(np.arange(D) < D // 2, f(1), f(-1))[None]
    cos, sin = np.cos(freqs), np.sin(freqs) * sign
    qk_scale = f(8.0)
    tab = np.stack([cos * scale * qk_scale, sin * scale * qk_scale, cos * inv, sin * inv])
    return tab.reshape(4, TPB, P, D).transpose(2, 0, 1, 3).reshape(P, -1).astype(f)


def constants():
    f = np.float32
    parts = {"ident": np.eye(P, dtype=f)}
    r, c = np.arange(P)[:, None] % WIN, np.arange(WIN)[None]
    mask = np.concatenate([np.where(r > c, f(NEG), f(0)), np.where(c > r, f(NEG), f(0))], 1)
    first = mask.copy()
    first[0:WIN, 0:WIN] = NEG
    parts["mask"] = np.concatenate([first] + [mask] * (TPB // 2 - 1), 1)
    parts["keep"] = np.tile((np.arange(TPB // 2) > 0).astype(f)[None], (P, 1))
    h = np.arange(P) // D0
    parts["blocks"] = (h[:, None] == h[None]).astype(f)
    parts["heads"] = (h[:, None] == np.arange(H0)[None]).astype(f)
    parts["rotary"] = rotary_constants()
    at, n = {}, 0
    for k, v in parts.items():
        at[k] = (n, v.shape[1])
        n += v.shape[1]
    return np.concatenate(list(parts.values()), 1), at


def build(nc, consts, at, x, Wq, bq, Wk, bk, Wv, bv, Wo, bo, Wqkv, q_scale, k_scale, Wout,
          ln_g, ln_b, W1, b1, W2, b2, out):
    ctx = ExitStack()
    with ctx:
        def sb(name, shape, dt=F32):
            return ctx.enter_context(nc.sbuf_tensor(name, shape, dt))

        def sem(name):
            return ctx.enter_context(nc.semaphore(name))

        qk_ps = ctx.enter_context(nc.psum_tensor("qk_ps", [P, INNER], F32))
        s_ps = ctx.enter_context(nc.psum_tensor("s_ps", [P, 2, 512], F32))
        ring = ctx.enter_context(nc.psum_tensor("ring", [P, RING_BANKS, 512], F32))
        q_ps = qk_ps
        k_ps = ring[:, 2:4, :].rearrange("p a c -> p (a c)")

        cst = sb("cst", [P, consts.shape[1]])

        def const(name):
            a, n = at[name]
            return cst[:, a:a + n]

        ident = const("ident")
        ident_bf = sb("ident_bf", [P, P], BF16)
        mask_bf = sb("mask_bf", [P, at["mask"][1]], BF16)
        rotary0 = const("rotary").rearrange("p (f j d) -> p f j d", f=4, j=TPB)
        x_tok = sb("x_tok", [P, (B * (TPB + 1) + 1) * C])
        x_keep = sb("x_keep", [P, NT, C])

        w0 = sb("w0", [P, 4, C])
        w0T = sb("w0T", [P, 4, C])
        bq_col = sb("bq_col", [P, 1])
        bq_minus = sb("bq_minus", [P, 1])
        bkv_row = sb("bkv_row", [P, 2 * C])
        bo_row = sb("bo_row", [P, C])
        wqk_hi = sb("wqk_hi", [P, 2 * INNER], F32R)
        wqk_lo = sb("wqk_lo", [P, 2 * INNER], F32R)
        wv = sb("wv", [P, INNER])
        wvT = sb("wvT", [P, PAIRS, C])
        wo_pad = sb("wo_pad", [P, PAIRS, 2, C])
        wvo = sb("wvo", [P, 4, QUADS, C])
        qk_scales = sb("qk_scales", [P, 2, D])
        rotary = [sb(f"rotary{n}", [P, TPB * D]) for n in range(4)]
        w1 = sb("w1", [P, W1_COLS])
        w2 = sb("w2", [P, 3, C])
        b1_col = sb("b1_col", [P, 2, 3])
        ln_col = sb("ln_col", [P, 2])
        b2_row = sb("b2_row", [P, C])

        xs = sb("xs", [P, 2, C])
        xsT = sb("xsT", [P, 2, P + 1])
        xsT_hi = sb("xsT_hi", [P, 2, P], F32R)
        xsT_lo = sb("xsT_lo", [P, 2, P], F32R)
        squares = sb("squares", [P, 2 * INNER])
        by_cos = sb("by_cos", [P, 2, INNER])
        by_sin = sb("by_sin", [P, 2, INNER])
        qk_rot = sb("qk_rot", [P, 2, INNER])
        wqk = qk_rot[:, :, :].rearrange("p a n -> p (a n)")
        sumsq = sb("sumsq", [P, 2 * H])
        rs_t = sb("rs_t", [P, 2 * H])
        rs_h = sb("rs_h", [P, 2 * H])
        rnorm = sb("rnorm", [P, 2, 2 * H])
        qT = sb("qT", [P, PAIRS, P])
        kT = sb("kT", [P, PAIRS, 2, RING])
        smax = sb("smax", [P, H])
        nbias = sb("nbias", [P, H])
        probs = sb("probs", [P, 2, QUADS, 2, 4, WIN])
        psum_row = sb("psum_row", [P, H])
        rrow = sb("rrow", [P, H])
        pT = sb("pT", [P, QUADS, 2, P])
        vo = sb("vo", [P, 2 * NW, QUADS * C])
        xn4 = sb("xn4", [P, FT, C])
        ln_rs = sb("ln_rs", [P, 2, 5, FT])
        three_halves = sb("three_halves", [P, FT])
        xnT = sb("xnT", [P, FT * P])
        xb = sb("xb", [P, FT, C])
        gate = by_sin[:, :, :].rearrange("p a n -> p (a n)")[:, 0:3 * FT * P].rearrange("p (a n) -> p a n", a=3)
        hid = sb("hid", [P, 3, FT * P])
        xs4_pair = by_cos[:, :, 0:FT * C].rearrange("p a (t c) -> p a t c", t=FT)
        squares4 = squares[:, 0:FT * C].rearrange("p (t c) -> p t c", t=FT)
        hid_first = [hid[:, 0, :], squares[:, FT * C:2 * FT * C]]
        probs_flat = probs[:, :, :, :, :, :].rearrange("p a b c d e -> p (a b c d e)")
        late = 2 * INNER - W1_COLS - FT * P
        w1_hi, w1_lo = [parts[:, late:late + W1_COLS] for parts in (wqk_hi, wqk_lo)]
        xnT_hi, xnT_lo = [[parts[:, c:c + FT * P] for c in (late - FT * P, late + W1_COLS)]
                          for parts in (wqk_hi, wqk_lo)]
        def tiles4(ap):
            return ap.rearrange("p (t c) -> p t c", t=FT)

        x_centred, x_squares, x1_centred, x1_squares, x1_tok = [tiles4(vo[:, i, :]) for i in range(5)]
        q0_exp, q0_relu = squares[:, 0:512], squares[:, 512:1024]
        k0, k0_exp = tiles4(squares[:, 1024:1536]), tiles4(squares[:, 1536:2048])
        qfT = by_cos[:, 0, :]
        kf, o0 = tiles4(by_cos[:, 1, 0:512]), tiles4(by_cos[:, 1, 512:1024])
        o0T = by_sin[:, 0, 0:512]
        v1 = tiles4(by_sin[:, 1, 0:FT * (C + 4)])
        kv_bd = probs_flat[:, 0:C + H0]
        den = probs_flat[:, C + H0:C + H0 + FT * H0].rearrange("p (t h) -> p t h", t=FT)

        cst_in, rotary_in, x0_in, x_in, w0_in, wqk_in, wv_in, wo_in, sc_in, w1_in, w2_in, b1_in, ln_in, b2_in = [
            sem(n) for n in ("cst_in", "rotary_in", "x0_in", "x_in", "w0_in", "wqk_in", "wv_in", "wo_in", "sc_in", "w1_in",
                             "w2_in", "b1_in", "ln_in", "b2_in")]
        out_done = sem("out_done")
        zeroed = sem("zeroed")
        consts_ready = sem("consts_ready")
        w0T_ps_ready, w0T_ready = sem("w0T_ps_ready"), sem("w0T_ready")
        x_ready = sem("x_ready")
        counts_tiles = []
        xs_in = [sem(f"xs_in{a}") for a in range(2)]

        def tile_sem(name, n=None):
            sems = [sem(name if n is None else f"{name}{i}") for i in range(n or 1)]
            counts_tiles.extend(sems)
            return sems[0] if n is None else sems

        x_mid = tile_sem("x_mid")
        norm_f, norm_h, norm_g = [
            {n: tile_sem(f"{stage}_{n}") for n in ("sums", "centred", "squared", "var", "half_var", "seed", "rsqrt")}
            for stage in "fhg"]
        f_xn, f_xnT_ps, f_xnT, f_proj, f_qmin, f_qexp, f_k0, f_kmin, f_kexp, f_feat, f_kv, f_bd = [
            tile_sem(n) for n in ("f_xn", "f_xnT_ps", "f_xnT", "f_proj", "f_qmin", "f_qexp", "f_k0", "f_kmin",
                                  "f_kexp", "f_feat", "f_kv", "f_bd")]
        f_num, f_den, f_o, f_oT_ps, f_oT, f_y, f_xb, f_x1 = [
            tile_sem(n) for n in ("f_num", "f_den", "f_o", "f_oT_ps", "f_oT", "f_y", "f_xb", "f_x1")]
        wvT_ps, wvT_ready, wvo_ps, wvo_ready = [sem(n) for n in ("wvT_ps", "wvT_ready", "wvo_ps", "wvo_ready")]
        tables_ready = sem("tables_ready")
        wq_hi_ready, wq_ready = sem("wq_hi_ready"), sem("wq_ready")
        xsT_ps, xsT_ready, xsT_hi_ready, xsT_lo_ready = [
            tile_sem(n) for n in ("xsT_ps", "xsT_ready", "xsT_hi_ready", "xsT_lo_ready")]
        projected, squared, summed, read, added = [
            {qk: tile_sem(f"{qk}_{n}") for qk in "qk"} for n in ("projected", "squared", "summed", "read", "added")]
        norm_step = sem("norm_step")
        k_rotated = tile_sem("k_rotated")
        qT_ps, qT_ready, kT_ps = [tile_sem(n, 2) for n in ("qT_ps", "qT_ready", "kT_ps")]
        kT_ready = {rows: tile_sem(f"kT_{rows}", 2) for rows in ("low", "high")}
        carried = sem("carried")
        s_ready, max_done, bias_ready, exp_done, rrow_ready, p_normed = [
            tile_sem(n, 2) for n in ("s_ready", "max_done", "bias_ready", "exp_done", "rrow_ready", "p_normed")]
        pT_ps, pT_ready = [tile_sem(n, 2) for n in ("pT_ps", "pT_ready")]
        vo_ps, vo_ready = [tile_sem(n, NW) for n in ("vo_ps", "vo_ready")]
        o_ps = tile_sem("o_ps")
        w1_hi_ready, w1_ready = sem("w1_hi_ready"), sem("w1_ready")
        g_xs = [sem(f"g_xs{par}") for par in range(2)]
        g_xn, g_xnT_ps, g_xnT, g_xnT_hi, g_xnT_lo, g_xb = [
            tile_sem(n) for n in ("g_xn", "g_xnT_ps", "g_xnT", "g_xnT_hi", "g_xnT_lo", "g_xb")]
        g_up, g_gelu, g_hid, g_down = [tile_sem(n) for n in ("g_up", "g_gelu", "g_hid", "g_down")]
        final_ready = sem("final_ready")

        block = ctx.enter_context(nc.Block())

        def slot(i):
            return i + (i >> 3) + 1

        low_rows, high_rows = slice(0, D), slice(D, P)

        def x_cols(i, tiles=1, lo=0, n=C):
            view = x_tok[:, bass.ds((slot(i)) * C, tiles * C)]
            return view.rearrange("p (t c) -> p t c", c=C)[:, :, lo:lo + n] if tiles > 1 or n < C else view

        up_banks = [(q_ps[:, 0:512], q_ps[:, 512:1024]), (k_ps[:, 0:512], k_ps[:, 512:1024]),
                    (s_ps[:, 0, :], s_ps[:, 1, :])]

        wvo_banks = (0, 0, 2, 3)

        def heads(ap, n=H):
            return ap.rearrange("p (h d) -> p h d", h=n)

        RING_USES = (("kT0", 2), ("kT1", 2), ("pT0", 3), ("vo3", 2), ("pT1", 3), ("xsT", 0),
                     ("o", 3), ("qT0", 1), ("vo1", 1), ("vo0", 1), ("vo2", 1), ("qT1", 1))
        ring_names = [name for name, _ in RING_USES]

        def ring_bank(tile_par, use):
            i = ring_names.index(use)
            return (len(RING_USES) * ((tile_par + RING_USES[i][1]) % 2) + i) % RING_BANKS

        def use_before(i):
            j = i - RING_BANKS
            return *RING_USES[j], int(j < 0)

        def schedule(loop, step, depth, n=NT, after_loop=None, before_last=None):
            turns = (n - depth) // 2
            for k in range(depth):
                step(k, k % 2, None)
            with loop(0, turns) as it:
                for r in range(2):
                    step(depth + r, (depth + r) % 2, it)
            k = depth + 2 * turns
            if after_loop:
                after_loop(k)
            for k in range(k, n + depth):
                if before_last and k == n + depth - 1:
                    before_last()
                step(k, k % 2, None)

        def tile_numbers(l, k, it):
            if it is None:
                return k, NT * l + k
            return 2 * it + k, (NT * l + 2 * it) + k

        def there(k, it, s, n=NT):
            return it is not None or 0 <= k - s < n

        def projection_banks(qk, k, it, s):
            return s_ps[:, :, :].rearrange("p a c -> p (a c)") if it is None and k == s and qk == "k" else qk_ps[:, :]

        def front_group(k, it, s):
            return k - s if it is None else 2 * it + (k - s)

        def done(T):
            return passed(T + 1)

        def passed(n):
            return n + CREDIT

        def ahead(engine, value):
            engine.compute_val(value)
            return value

        @block.tensor
        def _(pe):
            mm = nc.tensor.matmul

            pe.wait_ge(cst_in, 16)
            pe.wait_ge(w0_in, 128)
            for i in range(4):
                last = nc.tensor.transpose(ring[:, 0, i * C:(i + 1) * C], w0[:, i, :], ident)
            last.then_inc(w0T_ps_ready, 1)
            pe.wait_ge(w0T_ready, 1)

            def wv_transposed(half, layer):
                pe.wait_ge(wv_in, 16 * layer + 16)
                for p in range(4 * half, 4 * half + 4):
                    last = nc.tensor.transpose(ring[:, 0, (p % 4) * C:(p % 4 + 1) * C], wv[:, p * C:(p + 1) * C], ident)
                last.then_inc(wvT_ps, 1)

            def wvo_product(r, layer):
                if r == 0:
                    pe.wait_ge(wo_in, 32 * layer + 32)
                    pe.wait_ge(wvT_ready, 2 * layer + 2)
                else:
                    pe.wait_ge(wvo_ready, WVO_ROUNDS * layer + r)
                for p in (2 * r, 2 * r + 1):
                    last = mm(ring[:, wvo_banks[r], (p % 2) * 2 * C:(p % 2 + 1) * 2 * C], wvT[:, p, :], wo_pad[:, p, :, :],
                              start=True, stop=True)
                last.then_inc(wvo_ps, 1)

            def step(k, par, it):
                def numerators(s):
                    if not there(k, it, s, NG):
                        return
                    G, gg = front_group(k, it, s), (par - s) % 2
                    pe.wait_ge(f_bd, done(G >> 1))
                    pe.wait_ge(f_o, done(G - 1))
                    for t in range(FT):
                        bank = q_ps[:, 512:1024] if t < 2 else s_ps[:, 1, :]
                        a = (t % 2) * (C + H0)
                        last = mm(bank[:, a:a + C + H0], qfT[:, (gg * FT + t) * P:(gg * FT + t + 1) * P],
                                  kv_bd[:, :], start=True, stop=True)
                    last.then_inc(f_num, 1)

                def transposed(s):
                    if not there(k, it, s, NG):
                        return
                    G = front_group(k, it, s)
                    pe.wait_ge(f_xnT, done(G - 1))
                    pe.wait_ge(f_xn, done(G))
                    for t in range(FT):
                        last = nc.tensor.transpose(ring[:, 0, t * P:(t + 1) * P], xn4[:, t, :], ident)
                    last.then_inc(f_xnT_ps, 1)

                def projections(s):
                    if not there(k, it, s, NG):
                        return
                    G = front_group(k, it, s)
                    pe.wait_ge(f_xnT, done(G))
                    pe.wait_ge(f_feat, done(G - 1))
                    mm(q_ps[:, 0:512], w0T[:, 0, :], xnT[:, :], start=True, stop=True)
                    for t in range(FT):
                        last = mm(k_ps[:, t * 256:(t + 1) * 256], xnT[:, t * P:(t + 1) * P],
                                  w0T[:, 1:3, :], start=True, stop=True)
                    last.then_inc(f_proj, 1)

                def output(s):
                    if not there(k, it, s, NG):
                        return
                    G = front_group(k, it, s)
                    pe.wait_ge(f_x1, done(G - 1))
                    pe.wait_ge(f_o, done(G))
                    for t in range(FT):
                        last = nc.tensor.transpose(ring[:, 1, t * P:(t + 1) * P], o0[:, t, :], ident)
                    last.then_inc(f_oT_ps, 1)
                    pe.wait_ge(f_oT, done(G))
                    for t in range(FT):
                        last = mm(ring[:, 1, t * C:(t + 1) * C], o0T[:, t * P:(t + 1) * P], w0T[:, 3, :],
                                  start=True, stop=True)
                    last.then_inc(f_y, 1)

                def keys_by_values(s):
                    if not there(k, it, s, NG):
                        return
                    G, gg = front_group(k, it, s), (par - s) % 2
                    if gg == 0:
                        pe.wait_ge(f_bd, done((G >> 1) - 1))
                    pe.wait_ge(f_feat, done(G))
                    for t in range(FT):
                        last = mm(s_ps[:, 0, 0:C + 2], kf[:, t, :], v1[:, t, 0:C + 2],
                                  start=(gg == 0 and t == 0), stop=(gg == 1 and t == FT - 1))
                    last.then_inc(f_kv, 1)

                transposed(1)
                numerators(3)
                projections(1)
                if it is None and k == NG + 2:
                    wvo_product(0, 0)
                    wvo_product(1, 0)
                output(3)
                keys_by_values(1)
                if it is None and k == NG + 1:
                    wv_transposed(0, 0)
                    pe.wait_ge(wvT_ready, 1)
                    wv_transposed(1, 0)

            schedule(pe.Fori, step, 4, n=NG)

            for r in range(2, WVO_ROUNDS):
                wvo_product(r, 0)

            with pe.Fori(0, DEPTH) as l:
                pe.wait_ge(x_ready, NT * l + NT)
                pe.wait_ge(wvo_ready, WVO_ROUNDS * l + WVO_ROUNDS)
                pe.wait_ge(wq_ready, 2 * l + 2)

                def freed(use, T):
                    if use == "xsT":
                        pe.wait_ge(xsT_ready, done(T))
                    elif use == "o":
                        pe.wait_ge(x_mid, done(T))
                    elif use[0] == "q":
                        pe.wait_ge(qT_ready[int(use[2])], done(T))
                    elif use[0] == "k":
                        pe.wait_ge(kT_ready["low"][int(use[2])], done(T))
                        pe.wait_ge(kT_ready["high"][int(use[2])], done(T))
                    elif use[0] == "p":
                        pe.wait_ge(pT_ready[int(use[2])], done(T))
                    else:
                        pe.wait_ge(vo_ready[int(use[2])], done(T))

                last_use = [None] * RING_BANKS

                def after_loop(k):
                    for step_before in (k - 2, k - 1):
                        for name, s in RING_USES:
                            last_use[ring_bank((step_before - s) % 2, name)] = name, NT * l + step_before - s

                def step(k, par, it):
                    t0, T0 = tile_numbers(l, k, it)

                    def bank(use, s):
                        i = ring_names.index(use)
                        b = ring_bank((par - s) % 2, use)
                        if it is not None:
                            name, s2, ago = use_before(i)
                            freed(name, T0 - s2 - ago)
                            if ago and par == 1 and last_use[b][0] != name:
                                freed(*last_use[b])
                        else:
                            if last_use[b]:
                                freed(*last_use[b])
                            last_use[b] = use, T0 - s
                        return ring[:, b, :]

                    def xs_transposed(s):
                        if not there(k, it, s):
                            return
                        t, T, a = t0 - s, T0 - s, (par - s) % 2
                        r = bank("xsT", s)
                        pe.wait_ge(xs_in[a], 8 * NT * l + 16 * (t >> 1) + 16)
                        nc.tensor.transpose(r[:, 0:P], xs[:, a, :], ident).then_inc(xsT_ps, 1)

                    def project(qk, n, s):
                        if not there(k, it, s):
                            return
                        T, a = T0 - s, (par - s) % 2
                        pe.wait_ge(xsT_hi_ready, done(T))
                        pe.wait_ge(xsT_lo_ready, done(T))
                        if it is not None or k > s + 1:
                            pe.wait_ge(read["k" if qk == "q" else "q"], done(T - 1 if qk == "q" else T))
                        elif k == s + 1:
                            pe.wait_ge(read["q"], done(T - 1 if qk == "q" else T))
                        cols = slice(INNER * (qk == "k") + n * 512, INNER * (qk == "k") + (n + 1) * 512)
                        half = projection_banks(qk, k, it, s)[:, n * 512:(n + 1) * 512]
                        mm(half, xsT_hi[:, a, :], wqk_hi[:, cols], start=True, stop=False)
                        mm(half, xsT_hi[:, a, :], wqk_lo[:, cols], start=False, stop=False)
                        last = mm(half, xsT_lo[:, a, :], wqk_hi[:, cols], start=False, stop=True)
                        if n == 1:
                            last.then_inc(projected[qk], 1)

                    def transposed(qk, half, s):
                        if not there(k, it, s):
                            return
                        T = T0 - s
                        r = bank(f"{qk}T{half}", s)
                        pe.wait_ge(k_rotated if qk == "k" else added["q"], done(T))
                        for p in range(4):
                            c = (4 * half + p) * P
                            last = nc.tensor.transpose(r[:, p * P:(p + 1) * P],
                                                       qk_rot[:, 1 if qk == "k" else 0, c:c + P], ident)
                        last.then_inc((kT_ps if qk == "k" else qT_ps)[half], 1)

                    def probs_transposed(half, s):
                        if not there(k, it, s):
                            return
                        T, a = T0 - s, (par - s) % 2
                        r = bank(f"pT{half}", s)
                        pe.wait_ge(p_normed[half], done(T))
                        for n in range(4):
                            quad, side = 2 * half + n // 2, n % 2
                            last = nc.tensor.transpose(r[:, n * P:(n + 1) * P],
                                                       probs[:, a, quad, side, :, :].rearrange("p h c -> p (h c)"),
                                                       ident)
                        last.then_inc(pT_ps[half], 1)

                    def scores(half, s):
                        if not there(k, it, s):
                            return
                        t, T, a = t0 - s, T0 - s, (par - s) % 2
                        if a == 0:
                            variant = (t >> 1) & (TPB // 2 - 1)
                            pe.wait_ge(carried, NT // 2 * l + (t >> 1) + 1)
                        else:
                            variant = 1
                        pe.wait_ge(exp_done[half], done(T - 1))
                        pe.wait_ge(qT_ready[half], done(T))
                        pe.wait_ge(kT_ready["low"][half], done(T))
                        pe.wait_ge(kT_ready["high"][half], done(T))
                        mask = mask_bf[:, bass.ds(variant * 2 * WIN, 2 * WIN)]
                        mm(s_ps[:, half, :], ident_bf[:, :], mask.unsqueeze(1).broadcast_to([P, 8, 2 * WIN]),
                           start=True, stop=False, skip_group_check=True)
                        for p in range(4):
                            for w in range(NW):
                                c = P * a + WIN * w
                                last = mm(s_ps[WIN * w:WIN * (w + 1), half, p * P:(p + 1) * P],
                                          qT[:, 4 * half + p, WIN * w:WIN * (w + 1)],
                                          kT[:, 4 * half + p, :, c:c + 2 * WIN],
                                          start=False, stop=True, skip_group_check=True)
                        last.then_inc(s_ready[half], 1)

                    def values(w, s):
                        if not there(k, it, s):
                            return
                        T, a = T0 - s, (par - s) % 2
                        r = bank(f"vo{w}", s)
                        pe.wait_ge(xsT_ready, done(T))
                        for mh in range(4):
                            last = mm(r[WIN * mh:WIN * (mh + 1), :], xsT[:, a, WIN * w:WIN * (w + 1)],
                                      wvo[:, mh, :, :], start=True, stop=True)
                        last.then_inc(vo_ps[w], 1)

                    def output(s):
                        if not there(k, it, s):
                            return
                        T, a = T0 - s, (par - s) % 2
                        r = bank("o", s)
                        for w in range(NW):
                            pe.wait_ge(vo_ready[w], done(T))
                        for half in range(2):
                            pe.wait_ge(pT_ready[half], done(T))
                        for n in range(2 * QUADS):
                            quad, side = n // 2, n % 2
                            for w in range(NW):
                                at_w = (NW * a + w - 1 + side) % (2 * NW)
                                last = mm(r[WIN * w:WIN * (w + 1), 0:C], pT[:, quad, side, WIN * w:WIN * (w + 1)],
                                          vo[:, at_w, quad * C:(quad + 1) * C],
                                          start=(n == 0), stop=(n == 2 * QUADS - 1))
                        last.then_inc(o_ps, 1)

                    transposed("k", 0, 2)
                    project("k", 0, 1)
                    project("k", 1, 1)
                    transposed("k", 1, 2)
                    probs_transposed(0, 3)
                    scores(0, 2)
                    values(3, 2)
                    probs_transposed(1, 3)
                    scores(1, 2)
                    xs_transposed(0)
                    output(3)
                    project("q", 0, 0)
                    project("q", 1, 0)
                    transposed("q", 0, 1)
                    values(1, 1)
                    values(0, 1)
                    values(2, 1)
                    transposed("q", 1, 1)

                schedule(pe.Fori, step, 3, after_loop=after_loop)

                pe.wait_ge(x_mid, done(NT * l + NT - 1))
                pe.wait_ge(w1_ready, l + 1)
                pe.wait_ge(w2_in, 32 * l + 32)

                def transpose4(u):
                    U = NG * l + u
                    pe.wait_ge(g_xnT, done(U - 1))
                    pe.wait_ge(g_xn, done(U))
                    for t in range(FT):
                        last = nc.tensor.transpose(ring[:, 0, t * P:(t + 1) * P], xn4[:, t, :], ident)
                    last.then_inc(g_xnT_ps, 1)

                def up(u, par, i):
                    U = NG * l + u
                    pe.wait_ge(g_hid, passed(3 * U + i - 2))
                    if i == 0:
                        pe.wait_ge(g_xnT_hi, done(U))
                        pe.wait_ge(g_xnT_lo, done(U))
                    c, n = FB[i]
                    for j, off in ((1, F + c), (0, c)):
                        cols, bank = slice(off, off + P), up_banks[i][j]
                        mm(bank, w1_hi[:, cols], xnT_hi[par], start=True, stop=False)
                        mm(bank, w1_hi[:, cols], xnT_lo[par], start=False, stop=False)
                        mm(bank, w1_lo[:, cols], xnT_hi[par], start=False, stop=True).then_inc(g_up, 1)

                def down(u, par, t0=0, t1=FT):
                    U = NG * l + u
                    if t0 == 0:
                        pe.wait_ge(x_ready, FT * U + NT)
                        pe.wait_ge(g_hid, passed(3 * U + 3))
                    for t in range(t0, t1):
                        for i in range(3):
                            block = hid[:, i, :] if i else hid_first[par]
                            last = mm(ring[:, 1, t * C:(t + 1) * C], block[:, t * P:(t + 1) * P], w2[:, i, :],
                                      start=(i == 0), stop=(i == 2))
                    if t1 == FT:
                        last.then_inc(g_down, 1)

                transpose4(0)
                transpose4(1)
                up(0, 0, 0)
                with pe.Fori(0, (NG - 2) // 2) as it:
                    for par in range(2):
                        u = 2 * it + par
                        up(u, par, 1)
                        up(u, par, 2)
                        up(u + 1, 1 - par, 0)
                        down(u, par, 0, FT // 2)
                        transpose4(u + 2)
                        down(u, par, FT // 2, FT)
                up(NG - 2, 0, 1)
                up(NG - 2, 0, 2)
                up(NG - 1, 1, 0)
                pe.wait_ge(g_xnT, done(NG * l + NG - 1))
                wv_transposed(0, l + 1)
                down(NG - 2, 0)
                up(NG - 1, 1, 1)
                pe.wait_ge(wvT_ready, 2 * l + 3)
                wv_transposed(1, l + 1)
                up(NG - 1, 1, 2)
                wvo_product(0, l + 1)
                down(NG - 1, 1, 0, FT // 2)
                wvo_product(1, l + 1)
                down(NG - 1, 1, FT // 2, FT)
                for r in range(2, WVO_ROUNDS):
                    wvo_product(r, l + 1)

        @block.vector
        def _(dve):
            v = nc.vector

            def rsqrt(y, src, t, h, first, steps, base):
                ops = [
                    first,
                    lambda: v.tensor_scalar(y.bitcast(I32), src.bitcast(I32), -0.5, RSQRT_MAGIC, ALU.mult, ALU.add),
                ]
                for _ in range(3):
                    ops += [
                        lambda: v.tensor_tensor(t, y, y, ALU.mult),
                        lambda: v.scalar_tensor_tensor(h, t, -0.5, src, ALU.mult, ALU.mult),
                        lambda: v.scalar_tensor_tensor(y, h, 1.5, y, ALU.add, ALU.mult),
                    ]
                assert len(ops) == RSQRT_OPS

                def op(i):
                    if i:
                        dve.wait_ge(steps, base + i)
                    ops[i]().then_inc(steps, 1)
                return op

            def wide(ap):
                return ap.unsqueeze(2).broadcast_to([P, FT, C])

            def centred(src, dst, sums, n, norm):
                v.tensor_reduce(sums, src, AX, ALU.add).then_inc(norm["sums"], 1)
                dve.wait_ge(norm["sums"], done(n))
                v.scalar_tensor_tensor(dst, wide(sums), -1.0 / C, src, ALU.mult, ALU.add).then_inc(norm["centred"], 1)

            def deviation(squares, half_var, y, n, norm):
                dve.wait_ge(norm["squared"], done(n))
                v.tensor_reduce(half_var, squares, AX, ALU.add).then_inc(norm["var"], 1)
                dve.wait_ge(norm["var"], done(n))
                v.tensor_scalar(half_var, half_var, 0.5 / C, 0.5 * EPS, ALU.mult, ALU.add).then_inc(norm["half_var"], 1)
                dve.wait_ge(norm["half_var"], done(n))
                v.tensor_scalar(y.bitcast(I32), half_var.bitcast(I32), -0.5, RSQRT_MAGIC - 2 ** 22, ALU.mult,
                                ALU.add).then_inc(norm["seed"], 1)

            def scaled(xc, dst, y, n, norm):
                dve.wait_ge(norm["rsqrt"], passed(NEWTON_OPS * (n + 1)))
                return v.tensor_tensor(dst, xc, wide(y), ALU.mult)

            v.memset(kT[:, :, :, :], 0.0).then_inc(zeroed, 1)
            v.memset(xsT[:, :, P:P + 1], 0.0)
            v.memset(v1[:, :, C:C + 4], 1.0)
            v.memset(wo_pad[0:D, :, 1, :], 0.0)
            v.memset(wo_pad[D:P, :, 0, :], 0.0)
            v.memset(hid[:, 2, :], 0.0)
            v.memset(three_halves[:, :], 1.5)
            v.memset(w1[:, 2 * F:W1_COLS], 0.0)
            v.memset(w2[:, 2, :], 0.0).then_inc(zeroed, 1)
            dve.wait_ge(zeroed, 4)
            dve.wait_ge(cst_in, 16)
            v.tensor_copy(ident_bf[:, :], ident).then_inc(consts_ready, 1)
            v.tensor_copy(mask_bf[:, :], const("mask")).then_inc(consts_ready, 1)
            dve.wait_ge(x0_in, 16)

            def step(k, par, it):
                def block_diagonal(s):
                    if not there(k, it, s, NG) or (par - s) % 2 == 1:
                        return
                    G = front_group(k, it, s)
                    dve.wait_ge(f_kv, done(G + 1))
                    dve.wait_ge(f_num, done(G - 1))
                    v.tensor_tensor(kv_bd[:, 0:C], s_ps[:, 0, 0:C], const("blocks"), ALU.mult)
                    v.tensor_tensor(kv_bd[:, C:C + H0], s_ps[:, 0, C:C + 1].broadcast_to([P, H0]), const("heads"),
                                    ALU.mult).then_inc(f_bd, 1)

                def x_centre(s):
                    if not there(k, it, s, NG):
                        return
                    G = front_group(k, it, s)
                    if it is None and G == TPB // FT:
                        dve.wait_ge(x_in, 16 * (B - 1))
                    centred(x_keep[:, bass.ds(G * FT, FT), :], x_centred, ln_rs[:, 0, 0, :], G, norm_f)

                def x1_centre(s):
                    if not there(k, it, s, NG):
                        return
                    G = front_group(k, it, s)
                    dve.wait_ge(f_x1, done(G))
                    centred(x1_tok, x1_centred, ln_rs[:, 1, 0, :], G, norm_h)

                def biased_keys(s):
                    if not there(k, it, s, NG):
                        return
                    G = front_group(k, it, s)
                    dve.wait_ge(f_proj, done(G))
                    dve.wait_ge(f_kv, done(G - 1))
                    kv_ps = k_ps.rearrange("p (t c) -> p t c", t=FT)
                    v.tensor_tensor(k0, kv_ps[:, :, 0:C],
                                    bkv_row[:, 0:C].unsqueeze(1).broadcast_to([P, FT, C]), ALU.add).then_inc(f_k0, 1)
                    v.tensor_tensor(v1[:, :, 0:C], kv_ps[:, :, C:2 * C],
                                    bkv_row[:, C:2 * C].unsqueeze(1).broadcast_to([P, FT, C]), ALU.add)

                def features(s):
                    if not there(k, it, s, NG):
                        return
                    G, gg = front_group(k, it, s), (par - s) % 2
                    dve.wait_ge(f_num, done(G - 2))
                    dve.wait_ge(f_qexp, done(G))
                    v.scalar_tensor_tensor(qfT[:, gg * 512:(gg + 1) * 512], q0_relu, 0.0, q0_exp, ALU.max, ALU.add)
                    dve.wait_ge(f_kexp, done(G))
                    v.scalar_tensor_tensor(kf, k0, 0.0, k0_exp, ALU.max, ALU.add).then_inc(f_feat, 1)

                def quotients(s):
                    if not there(k, it, s, NG):
                        return
                    G = front_group(k, it, s)
                    dve.wait_ge(f_num, done(G))
                    halves = [ps.rearrange("p (t c) -> p t c", t=2)
                              for ps in (q_ps[:, 512:512 + 2 * (C + H0)], s_ps[:, 1, 0:2 * (C + H0)])]
                    for n in range(2):
                        v.tensor_scalar(den[:, 2 * n:2 * n + 2, :], halves[n][:, :, C:C + H0], 1e-6, None,
                                        ALU.max).then_inc(f_den, 1)
                    dve.wait_ge(f_den, passed(3 * G + 2))
                    v.reciprocal(den[:, :, :], den[:, :, :]).then_inc(f_den, 1)
                    dve.wait_ge(f_oT_ps, done(G - 1))
                    dve.wait_ge(f_den, passed(3 * G + 3))
                    for n in range(2):
                        for t in range(2):
                            i = 2 * n + t
                            last = v.tensor_tensor(heads(o0[:, i, :], H0), heads(halves[n][:, t, 0:C], H0),
                                                   den[:, i, :].unsqueeze(2).broadcast_to([P, H0, D0]), ALU.mult)
                    last.then_inc(f_o, 1)

                def x1(s):
                    if not there(k, it, s, NG):
                        return
                    G = front_group(k, it, s)
                    dve.wait_ge(f_xb, done(G))
                    dve.wait_ge(f_y, done(G))
                    y = tiles4(ring[:, 1, :])
                    v.tensor_tensor(x_keep[:, bass.ds(G * FT, FT), :], y, xb[:, :, :], ALU.add)
                    v.tensor_tensor(x1_tok, y, xb[:, :, :], ALU.add).then_inc(f_x1, 1)

                def x_deviation(s):
                    if there(k, it, s, NG):
                        deviation(x_squares, ln_rs[:, 0, 1, :], ln_rs[:, 0, 2, :], front_group(k, it, s), norm_f)

                def x1_deviation(s):
                    if there(k, it, s, NG):
                        deviation(x1_squares, ln_rs[:, 1, 1, :], ln_rs[:, 1, 2, :], front_group(k, it, s), norm_h)

                def x_normalised(s):
                    if not there(k, it, s, NG):
                        return
                    G = front_group(k, it, s)
                    dve.wait_ge(f_xnT_ps, done(G - 1))
                    scaled(x_centred, xn4[:, :, :], ln_rs[:, 0, 2, :], G, norm_f).then_inc(f_xn, 1)

                def stack_input(s):
                    if not there(k, it, s, NG):
                        return
                    G = front_group(k, it, s)
                    scaled(x1_centred, x_cols(G * FT, FT), ln_rs[:, 1, 2, :], G, norm_h).then_inc(x_ready, FT)

                block_diagonal(4)
                x1_centre(5)
                x_deviation(1)
                x1_deviation(5)
                quotients(4)
                biased_keys(2)
                features(2)
                x_normalised(1)
                x_centre(0)
                x1(4)
                stack_input(5)

            schedule(dve.Fori, step, 6, n=NG)

            with dve.Fori(0, DEPTH) as l:
                dve.wait_ge(tables_ready, l + 1)

                def centre(u, par):
                    x4 = xs4_pair[:, par]
                    dve.wait_ge(g_xs[par], 24 * NG * l + 48 * (u >> 1) + 48)
                    centred(x4, x4, ln_rs[:, par, 0, :], NG * l + u, norm_g)

                def squared_early(u):
                    U = NG * l + u
                    if u:
                        dve.wait_ge(norm_g["var"], done(U - 1))
                    dve.wait_ge(norm_g["centred"], done(U))
                    v.tensor_tensor(squares4, xs4_pair[:, u], xs4_pair[:, u], ALU.mult).then_inc(norm_g["squared"], 1)

                def variance4(u, par):
                    deviation(squares4, ln_rs[:, par, 1, :], ln_rs[:, par, 2, :], NG * l + u, norm_g)

                def normalised(u, par):
                    U = NG * l + u
                    dve.wait_ge(g_xnT_ps, done(U - 1))
                    counted = U + 1 if isinstance(u, int) and u == 0 else U
                    scaled(xs4_pair[:, par], xn4[:, :, :], ln_rs[:, par, 2, :], counted, norm_g).then_inc(g_xn, 1)

                def step(k, par, it):
                    t0, T0 = tile_numbers(l, k, it)

                    def copy(out_, in_):
                        return v.tensor_copy(out_, in_)

                    def k_evacuated(which, half, s):
                        if not there(k, it, s):
                            return
                        t, T, a = t0 - s, T0 - s, (par - s) % 2
                        rows, n = (low_rows, 0) if which == "low" else (high_rows, 1)
                        off = WIN + P * a
                        if a == 1:
                            dve.wait_ge(carried, NT // 2 * l + (t >> 1) + 1)
                        for h in range(2):
                            dve.wait_ge(s_ready[h], done(T - 1))
                        dve.wait_ge(kT_ps[half], done(T))
                        copy(kT[rows, 4 * half:4 * half + 4, n, off:off + P],
                             ring[rows, ring_bank(a, f"kT{half}"), :].rearrange("p (n t) -> p n t", n=4)
                             ).then_inc(kT_ready[which][half], 1)

                    def vo_evacuated(w, s):
                        if not there(k, it, s):
                            return
                        T, a = T0 - s, (par - s) % 2
                        dve.wait_ge(o_ps, done(T - 1 if w == NW - 1 else T - 2))
                        dve.wait_ge(vo_ps[w], done(T))
                        copy(vo[:, NW * a + w, :], ring[:, ring_bank(a, f"vo{w}"), :]).then_inc(vo_ready[w], 1)

                    def xsT_lower(s):
                        if not there(k, it, s):
                            return
                        T, a = T0 - s, (par - s) % 2
                        dve.wait_ge(xsT_ready, done(T))
                        dve.wait_ge(xsT_hi_ready, done(T))
                        v.tensor_tensor(xsT_lo[:, a, :], xsT[:, a, 0:P], xsT_hi[:, a, :].bitcast(F32),
                                        ALU.subtract).then_inc(xsT_lo_ready, 1)

                    def row_reciprocals(half, s):
                        if not there(k, it, s):
                            return
                        T, h = T0 - s, slice(8 * half, 8 * half + 8)
                        dve.wait_ge(p_normed[half], done(T - 1))
                        dve.wait_ge(exp_done[half], done(T))
                        v.reciprocal(rrow[:, h], psum_row[:, h]).then_inc(rrow_ready[half], 1)

                    def rotate(qk, part, s):
                        if not there(k, it, s):
                            return
                        t, T, n = t0 - s, T0 - s, "qk".index(qk)
                        angles = ahead(dve, (t & (TPB - 1)) * D)
                        if part == 0:
                            dve.wait_ge(added[qk], done(T - 1))
                            dve.wait_ge(squared[qk], done(T))
                        last = v.tensor_tensor(heads((by_sin if part else by_cos)[:, n, :]),
                                               heads(projection_banks(qk, k, it, s)),
                                               rotary[2 * n + part][:, bass.ds(angles, D)].unsqueeze(1)
                                               .broadcast_to([P, H, D]), ALU.mult)
                        if part == 1:
                            last.then_inc(read[qk], 1)

                    def sum_of_squares(qk, s):
                        if not there(k, it, s):
                            return
                        T, n = T0 - s, "qk".index(qk)
                        dve.wait_ge(squared[qk], done(T))
                        v.tensor_reduce(sumsq[:, n * H:(n + 1) * H],
                                        heads(squares[:, n * INNER:(n + 1) * INNER]), AX,
                                        ALU.add).then_inc(summed[qk], 1)

                    def inverse_norms(i0, i1, s):
                        if not there(k, it, s):
                            return
                        T, a = T0 - s, (par - s) % 2
                        if i0 == 0:
                            dve.wait_ge(summed["q"], done(T))
                            dve.wait_ge(summed["k"], done(T))
                        if i0 <= 1 < i1:
                            dve.wait_ge(k_rotated, done(T - 2))
                        op = rsqrt(rnorm[:, a, :], sumsq[:, :], rs_t[:, :], rs_h[:, :],
                                   lambda: v.tensor_scalar(sumsq[:, :], sumsq[:, :], 1e-24, None, ALU.max),
                                   norm_step, RSQRT_OPS * T)
                        for i in range(i0, i1):
                            op(i)

                    def carry(s):
                        if not there(k, it, s) or (par - s) % 2 == 1:
                            return
                        t, T = t0 - s, T0 - s
                        n = ahead(dve, (t >> 1) & (TPB // 2 - 1))
                        for h in range(2):
                            dve.wait_ge(s_ready[h], done(T - 2))
                            dve.wait_ge(kT_ready["low"][h], done(T - 1))
                            dve.wait_ge(kT_ready["high"][h], done(T - 1))
                        keep = const("keep")[:, bass.ds(n, 1)].unsqueeze(2).broadcast_to([P, H, WIN])
                        v.tensor_tensor(kT[:, :, :, 0:WIN].rearrange("p a b c -> p (a b) c"),
                                        kT[:, :, :, RING - WIN:RING].rearrange("p a b c -> p (a b) c"),
                                        keep, ALU.mult).then_inc(carried, 1)

                    def maxima(half, s):
                        if not there(k, it, s):
                            return
                        T = T0 - s
                        dve.wait_ge(s_ready[half], done(T))
                        v.tensor_reduce(smax[:, 8 * half:8 * half + 8], heads(s_ps[:, half, :], 8), AX,
                                        ALU.max).then_inc(max_done[half], 1)

                    def softmax_bias(half, s):
                        if not there(k, it, s):
                            return
                        T, a, h = T0 - s, (par - s) % 2, slice(8 * half, 8 * half + 8)
                        dve.wait_ge(exp_done[half], done(T - 1))
                        dve.wait_ge(norm_step, RSQRT_OPS * T + RSQRT_OPS)
                        dve.wait_ge(max_done[half], done(T))
                        v.scalar_tensor_tensor(nbias[:, h], smax[:, h], -1.0, rnorm[:, a, h], ALU.mult,
                                               ALU.mult).then_inc(bias_ready[half], 1)

                    def residual(s):
                        if not there(k, it, s):
                            return
                        t, T, a = t0 - s, T0 - s, (par - s) % 2
                        x_old = x_tok[:, bass.ds(ahead(dve, slot(t) * C), C)]
                        dve.wait_ge(o_ps, done(T))
                        v.tensor_tensor(x_old, ring[:, ring_bank(a, "o"), 0:C], x_old, ALU.add).then_inc(x_mid, 1)

                    inverse_norms(3, 4, 1)
                    if it is not None or k != 1:
                        xsT_lower(0)
                    inverse_norms(4, 5, 1)
                    maxima(1, 2)
                    inverse_norms(5, 6, 1)
                    residual(3)
                    inverse_norms(6, 8, 1)
                    softmax_bias(1, 2)
                    inverse_norms(8, 9, 1)
                    row_reciprocals(0, 2)
                    inverse_norms(9, 11, 1)
                    rotate("q", 0, 0)
                    rotate("q", 1, 0)
                    if it is None and k == 0:
                        xsT_lower(-1)
                    vo_evacuated(2, 1)
                    carry(1)
                    k_evacuated("low", 0, 1)
                    sum_of_squares("q", 0)
                    if it is None and k == NT + 1:
                        centre(0, 0)
                        squared_early(0)
                        variance4(0, 0)
                    row_reciprocals(1, 2)
                    if it is None and k == NT + 1:
                        centre(1, 1)
                        squared_early(1)
                        variance4(1, 1)
                    sum_of_squares("k", 0)
                    maxima(0, 1)
                    inverse_norms(0, 1, 0)
                    softmax_bias(0, 1)
                    inverse_norms(1, 2, 0)
                    rotate("k", 0, 0)
                    inverse_norms(2, 3, 0)
                    rotate("k", 1, 0)

                def lower(u, par):
                    U = NG * l + u
                    dve.wait_ge(g_xnT_hi, done(U))
                    v.tensor_tensor(xnT_lo[par], xnT[:, :], xnT_hi[par].bitcast(F32),
                                    ALU.subtract).then_inc(g_xnT_lo, 1)

                def hidden(u, par, i):
                    U = NG * l + u
                    c, n = FB[i]
                    dve.wait_ge(g_down, done(U - 1 if i else U - 2))
                    dve.wait_ge(g_up, passed(6 * U + 2 * i + 2))
                    dve.wait_ge(g_gelu, passed(3 * U + i + 1))
                    v.scalar_tensor_tensor((hid[:, i, :] if i else hid_first[par])[0:n, :], up_banks[i][0][0:n, :], b1_col[0:n, 0, i:i + 1],
                                           gate[0:n, i, :], ALU.add, ALU.mult).then_inc(g_hid, 1)

                def x_new(u):
                    U = NG * l + u
                    tiles = x_cols(u * FT, FT)
                    dve.wait_ge(g_xb, done(U))
                    dve.wait_ge(g_down, done(U))
                    v.tensor_tensor(tiles, ring[:, 1, :].rearrange("p (t c) -> p t c", t=FT),
                                    xb[:, :, :], ALU.add).then_inc(x_ready, FT)

                def step4(u, par, ahead1, ahead2, ahead3):
                    hidden(u, par, 1)
                    hidden(u, par, 2)
                    if ahead2:
                        normalised(u + 2, par)
                    if ahead3:
                        centre(u + 3, 1 - par)
                        variance4(u + 3, 1 - par)
                    if ahead2:
                        lower(u + 2, par)
                    if ahead1:
                        hidden(u + 1, 1 - par, 0)
                    x_new(u)

                schedule(dve.Fori, step, 3, before_last=lambda: normalised(0, 0))

                dve.wait_ge(b1_in, 96 * l + 96)
                normalised(1, 1)
                lower(0, 0)
                lower(1, 1)
                centre(2, 0)
                variance4(2, 0)
                hidden(0, 0, 0)
                with dve.Fori(0, (NG - 4) // 2) as it:
                    for par in range(2):
                        step4(2 * it + par, par, True, True, True)
                for u in range(NG - 4, NG):
                    step4(u, u % 2, u + 1 < NG, u + 2 < NG, u + 3 < NG)

            dve.wait_ge(x_ready, NT * (DEPTH + 1))
            for b in range(B):
                tiles = x_keep[:, b * TPB:(b + 1) * TPB, :]
                v.tensor_tensor(tiles, tiles, x_cols(b * TPB, TPB), ALU.add).then_inc(final_ready, 1)

        @block.scalar
        def _(act):
            def copy(out_, in_):
                return nc.scalar.activation(out_, in_, ACT.Copy)

            act.wait_ge(w0T_ps_ready, 1)
            copy(w0T[:, :, :].rearrange("p a c -> p (a c)"), ring[:, 0, :]).then_inc(w0T_ready, 1)

            def wvT_evacuated(half, layer):
                act.wait_ge(wvT_ps, 2 * layer + half + 1)
                copy(wvT[:, 4 * half:4 * half + 4, :].rearrange("p a c -> p (a c)"),
                     ring[:, 0, :]).then_inc(wvT_ready, 1)

            def wvo_evacuated(r, layer):
                act.wait_ge(wvo_ps, WVO_ROUNDS * layer + r + 1)
                copy(wvo[:, :, r, :], ring[:, wvo_banks[r], :].rearrange("p (a c) -> p a c", a=4)).then_inc(wvo_ready, 1)

            def wqk_upper(layer, part):
                cols = slice(late, 2 * INNER) if part else slice(0, late)
                act.wait_ge(wqk_in, 16 * layer + 16)
                copy(wqk_hi[:, cols], wqk[:, cols]).then_inc(wq_hi_ready, 1)

            act.wait_ge(w0_in, 128)
            nc.scalar.activation(bq_minus[:, :], bq_col[:, :], ACT.Copy, scale=-1.0)

            def step(k, par, it):
                def normalised_evacuated(s):
                    if not there(k, it, s, NG):
                        return
                    G = front_group(k, it, s)
                    act.wait_ge(f_proj, done(G - 1))
                    act.wait_ge(f_xnT_ps, done(G))
                    copy(xnT[:, :], ring[:, 0, :]).then_inc(f_xnT, 1)

                def squared(src, dst, norm, s):
                    if not there(k, it, s, NG):
                        return
                    G = front_group(k, it, s)
                    act.wait_ge(norm["var"], done(G - 1))
                    act.wait_ge(norm["centred"], done(G))
                    nc.scalar.activation(dst, src, ACT.Square).then_inc(norm["squared"], 1)

                def q_parts(s):
                    if not there(k, it, s, NG):
                        return
                    G = front_group(k, it, s)
                    act.wait_ge(f_feat, done(G - 1))
                    act.wait_ge(f_proj, done(G))
                    nc.scalar.activation(q0_exp, q_ps[:, 0:512], ACT.Relu, scale=-1.0,
                                         bias=bq_minus[:, :]).then_inc(f_qmin, 1)
                    nc.scalar.activation(q0_relu, q_ps[:, 0:512], ACT.Relu, bias=bq_col[:, :])
                    act.wait_ge(f_qmin, done(G))
                    nc.scalar.activation(q0_exp, q0_exp, ACT.Exp, scale=-1.0).then_inc(f_qexp, 1)

                def k_parts(s):
                    if not there(k, it, s, NG):
                        return
                    G = front_group(k, it, s)
                    act.wait_ge(f_k0, done(G))
                    nc.scalar.activation(k0_exp, k0, ACT.Relu, scale=-1.0).then_inc(f_kmin, 1)
                    act.wait_ge(f_kmin, done(G))
                    nc.scalar.activation(k0_exp, k0_exp, ACT.Exp, scale=-1.0).then_inc(f_kexp, 1)

                def output_evacuated(s):
                    if not there(k, it, s, NG):
                        return
                    G = front_group(k, it, s)
                    act.wait_ge(f_y, done(G - 1))
                    act.wait_ge(f_oT_ps, done(G))
                    copy(o0T[:, :], ring[:, 1, :]).then_inc(f_oT, 1)

                normalised_evacuated(1)
                squared(x_centred, x_squares, norm_f, 0)
                squared(x1_centred, x1_squares, norm_h, 4)
                q_parts(1)
                k_parts(1)
                if it is None and k == NG + 2:
                    wvo_evacuated(0, 0)
                    wvo_evacuated(1, 0)
                output_evacuated(3)
                if it is None and k == NG + 1:
                    for half in range(2):
                        wvT_evacuated(half, 0)

            def first_wqk_upper(k):
                for part in range(2):
                    wqk_upper(0, part)

            schedule(act.Fori, step, 4, n=NG, after_loop=first_wqk_upper)
            for r in range(2, WVO_ROUNDS):
                wvo_evacuated(r, 0)

            with act.Fori(0, DEPTH) as l:
                def step(k, par, it):
                    t0, T0 = tile_numbers(l, k, it)

                    def scaled_copy(out_, in_, by):
                        return nc.scalar.activation(out_, in_, ACT.Copy, scale=by)

                    def q_evacuated(half, s):
                        if not there(k, it, s):
                            return
                        T, a = T0 - s, (par - s) % 2
                        act.wait_ge(s_ready[half], done(T - 1))
                        act.wait_ge(qT_ps[half], done(T))
                        copy(qT[:, 4 * half:4 * half + 4, :],
                             ring[:, ring_bank(a, f"qT{half}"), :].rearrange("p (n t) -> p n t", n=4)
                             ).then_inc(qT_ready[half], 1)

                    def k_evacuated(which, half, s):
                        if not there(k, it, s):
                            return
                        t, T, a = t0 - s, T0 - s, (par - s) % 2
                        rows, n = (low_rows, 0) if which == "low" else (high_rows, 1)
                        off = WIN + P * a
                        if a == 1:
                            act.wait_ge(carried, NT // 2 * l + (t >> 1) + 1)
                        for h in range(2):
                            act.wait_ge(s_ready[h], done(T - 1))
                        act.wait_ge(kT_ps[half], done(T))
                        copy(kT[rows, 4 * half:4 * half + 4, n, off:off + P],
                             ring[rows, ring_bank(a, f"kT{half}"), :].rearrange("p (n t) -> p n t", n=4)
                             ).then_inc(kT_ready[which][half], 1)

                    def vo_evacuated(w, s):
                        if not there(k, it, s):
                            return
                        T, a = T0 - s, (par - s) % 2
                        act.wait_ge(o_ps, done(T - 1 if w == NW - 1 else T - 2))
                        act.wait_ge(vo_ps[w], done(T))
                        copy(vo[:, NW * a + w, :], ring[:, ring_bank(a, f"vo{w}"), :]).then_inc(vo_ready[w], 1)

                    def p_evacuated(half, s):
                        if not there(k, it, s):
                            return
                        T, a = T0 - s, (par - s) % 2
                        act.wait_ge(o_ps, done(T - 1))
                        act.wait_ge(pT_ps[half], done(T))
                        copy(pT[:, 2 * half:2 * half + 2, :, :].rearrange("p a b c -> p (a b c)"),
                             ring[:, ring_bank(a, f"pT{half}"), :]).then_inc(pT_ready[half], 1)

                    def xsT_evacuated(s):
                        if not there(k, it, s):
                            return
                        t, T, a = t0 - s, T0 - s, (par - s) % 2
                        act.wait_ge(xsT_ps, done(T))
                        act.wait_ge(xsT_ready, done(T - 1))
                        r = ring[:, ring_bank(a, "xsT"), 0:P]
                        copy(xsT[low_rows, a, 0:P], r[low_rows, :])
                        copy(xsT[high_rows, a, 1:P + 1], r[high_rows, :])
                        before, first = xsT[high_rows, 1 - a, P:P + 1], xsT[high_rows, a, 0:1]
                        if a == 1:
                            copy(first, before).then_inc(xsT_ready, 1)
                        else:
                            n = (t >> 1) & (TPB // 2 - 1)
                            scaled_copy(first, before, const("keep")[high_rows, bass.ds(n, 1)]).then_inc(xsT_ready, 1)

                    def xsT_upper(s):
                        if not there(k, it, s):
                            return
                        T, a = T0 - s, (par - s) % 2
                        act.wait_ge(xsT_ready, done(T))
                        copy(xsT_hi[:, a, :], xsT[:, a, 0:P]).then_inc(xsT_hi_ready, 1)

                    def square(qk, s):
                        if not there(k, it, s):
                            return
                        T, n = T0 - s, "qk".index(qk)
                        act.wait_ge(summed[qk], done(T - 1))
                        act.wait_ge(projected[qk], done(T))
                        nc.scalar.activation(squares[:, n * INNER:(n + 1) * INNER], projection_banks(qk, k, it, s),
                                             ACT.Square).then_inc(squared[qk], 1)

                    def exponentials(h0, s):
                        if not there(k, it, s):
                            return
                        T, a, half = T0 - s, (par - s) % 2, h0 // 8
                        if h0 % 8 == 0:
                            act.wait_ge(rrow_ready[half], done(T - 1))
                            act.wait_ge(pT_ps[half], done(T - 2))
                            act.wait_ge(bias_ready[half], done(T))
                        for h in (h0, h0 + 1):
                            c = h % 8 * 2 * WIN
                            last = nc.scalar.activation(
                                probs[:, a, h // 4, :, h % 4, :],
                                s_ps[:, half, c:c + 2 * WIN].rearrange("p (s c) -> p s c", s=2), ACT.Exp,
                                scale=rnorm[:, a, h:h + 1], bias=nbias[:, h:h + 1],
                                accum_out=psum_row[:, h:h + 1])
                        if h0 % 8 == 6:
                            last.then_inc(exp_done[half], 1)

                    xsT_evacuated(0)
                    xsT_upper(0)
                    exponentials(4, 2)
                    exponentials(6, 2)
                    vo_evacuated(3, 2)
                    square("q", 0)
                    q_evacuated(0, 1)
                    exponentials(8, 2)
                    vo_evacuated(1, 1)
                    vo_evacuated(0, 1)
                    exponentials(10, 2)
                    exponentials(12, 2)
                    k_evacuated("high", 0, 1)
                    exponentials(14, 2)
                    square("k", 0)
                    q_evacuated(1, 1)
                    k_evacuated("low", 1, 1)
                    k_evacuated("high", 1, 1)
                    p_evacuated(0, 2)
                    p_evacuated(1, 2)
                    exponentials(0, 1)
                    exponentials(2, 1)

                def squared4(u, par):
                    U = NG * l + u
                    act.wait_ge(norm_g["var"], done(U - 1))
                    act.wait_ge(norm_g["centred"], done(U))
                    nc.scalar.activation(squares4, xs4_pair[:, par], ACT.Square).then_inc(norm_g["squared"], 1)

                def transposed(u):
                    U = NG * l + u
                    act.wait_ge(g_xnT_lo, done(U - 1))
                    act.wait_ge(g_xnT_ps, done(U))
                    nc.scalar.activation(xnT[:, :], ring[:, 0, :], ACT.Identity, scale=ln_col[:, 0:1],
                                         bias=ln_col[:, 1:2]).then_inc(g_xnT, 1)

                def upper(u, par):
                    act.wait_ge(g_xnT, done(NG * l + u))
                    copy(xnT_hi[par], xnT[:, :]).then_inc(g_xnT_hi, 1)

                def gelu(u, i):
                    U = NG * l + u
                    c, n = FB[i]
                    act.wait_ge(g_hid, passed(3 * U + i - 2))
                    act.wait_ge(g_up, passed(6 * U + 2 * i + 1))
                    nc.scalar.activation(gate[0:n, i, :], up_banks[i][1][0:n, :], ACT.Gelu,
                                         bias=b1_col[0:n, 1, i:i + 1]).then_inc(g_gelu, 1)

                def w1_upper():
                    act.wait_ge(w1_in, 16 * l + 16)
                    act.wait_ge(projected["k"], done(NT * l + NT - 1))
                    copy(w1_hi, w1[:, :]).then_inc(w1_hi_ready, 1)

                schedule(act.Fori, step, 2, before_last=w1_upper)

                act.wait_ge(ln_in, 32 * l + 32)
                act.wait_ge(b1_in, 96 * l + 96)
                transposed(0)
                upper(0, 0)
                transposed(1)
                upper(1, 1)
                squared4(2, 0)
                gelu(0, 0)

                def step4(u, par, ahead2, ahead3):
                    gelu(u, 1)
                    gelu(u, 2)
                    gelu(u + 1, 0)
                    if ahead3:
                        squared4(u + 3, 1 - par)
                    if ahead2:
                        transposed(u + 2)
                        upper(u + 2, par)

                with act.Fori(0, (NG - 4) // 2) as it:
                    for par in range(2):
                        step4(2 * it + par, par, True, True)
                for u in range(NG - 4, NG - 1):
                    step4(u, u % 2, u + 2 < NG, u + 3 < NG)
                wvT_evacuated(0, l + 1)
                act.wait_ge(g_up, passed(6 * (NG * l + NG - 1)))
                wqk_upper(l + 1, 0)
                gelu(NG - 1, 1)
                wvT_evacuated(1, l + 1)
                gelu(NG - 1, 2)
                wvo_evacuated(0, l + 1)
                act.wait_ge(g_up, passed(6 * (NG * l + NG)))
                wqk_upper(l + 1, 1)
                for r in range(1, WVO_ROUNDS):
                    wvo_evacuated(r, l + 1)

        @block.gpsimd
        def _(pool):
            g = nc.gpsimd

            g.memset(x_tok[:, :], 0.0).then_inc(zeroed, 1)
            g.memset(vo[:, 2 * NW - 1, :], 0.0).then_inc(zeroed, 1)

            def newton(rs, three_halves=three_halves[:, :]):
                _, half_var, y, t, _ = (rs[:, i, :] for i in range(5))
                ops = [
                    lambda: g.tensor_tensor(t, y, y, ALU.mult),
                    lambda: g.tensor_tensor(t, t, half_var, ALU.mult),
                    lambda: g.tensor_tensor(t, three_halves, t, ALU.subtract),
                    lambda: g.tensor_tensor(y, y, t, ALU.mult),
                ] * 3
                assert len(ops) == NEWTON_OPS
                return ops

            def inverse_deviations(*norms):
                for i in range(NEWTON_OPS):
                    for rs, n, norm in norms:
                        if i == 0:
                            pool.wait_ge(norm["seed"], done(n))
                        else:
                            pool.wait_ge(norm["rsqrt"], passed(NEWTON_OPS * n + i))
                        newton(rs)[i]().then_inc(norm["rsqrt"], 1)

            def step(k, par, it):
                def x_and_bias(s):
                    if not there(k, it, s, NG):
                        return
                    G = front_group(k, it, s)
                    pool.wait_ge(f_x1, done(G - 1))
                    g.tensor_tensor(xb[:, :, :], x_keep[:, bass.ds(G * FT, FT), :],
                                    bo_row[:, :].unsqueeze(1).broadcast_to([P, FT, C]), ALU.add).then_inc(f_xb, 1)

                def rsqrts(s, s1):
                    inverse_deviations(*[(ln_rs[:, n], front_group(k, it, stage), norm)
                                         for n, stage, norm in ((0, s, norm_f), (1, s1, norm_h))
                                         if there(k, it, stage, NG)])

                x_and_bias(3)
                rsqrts(0, 4)

            def tables(layer):
                pool.wait_ge(sc_in, 32 * layer + 32)
                if not isinstance(layer, int):
                    pool.wait_ge(read["k"], done(NT * layer - 1))
                for n in range(4):
                    last = g.tensor_tensor(rotary[n][:, :].rearrange("p (j d) -> p j d", j=TPB), rotary0[:, n],
                                           qk_scales[:, n // 2, :].unsqueeze(1).broadcast_to([P, TPB, D]), ALU.mult)
                last.then_inc(tables_ready, 1)

            def wqk_lower(layer, part):
                cols = slice(late, 2 * INNER) if part else slice(0, late)
                pool.wait_ge(wq_hi_ready, 2 * layer + part + 1)
                g.tensor_tensor(wqk_lo[:, cols], wqk[:, cols], wqk_hi[:, cols].bitcast(F32),
                                ALU.subtract).then_inc(wq_ready, 1)

            def first_weights(k):
                pool.wait_ge(rotary_in, 16)
                tables(0)
                for part in range(2):
                    wqk_lower(0, part)

            pool.wait_ge(w0_in, 128)
            schedule(pool.Fori, step, 4, n=NG, after_loop=first_weights)
            step(NG + 4, 0, None)

            with pool.Fori(0, DEPTH) as l:
                def step(k, par, it):
                    t0, T0 = tile_numbers(l, k, it)

                    def normalise(half, s):
                        if not there(k, it, s):
                            return
                        T, a = T0 - s, (par - s) % 2
                        pool.wait_ge(rrow_ready[half], done(T))
                        for quad in (2 * half, 2 * half + 1):
                            p = probs[:, a, quad]
                            r = rrow[:, 4 * quad:4 * quad + 4].unsqueeze(1).unsqueeze(3).broadcast_to([P, 2, 4, WIN])
                            last = g.tensor_tensor(p, p, r, ALU.mult)
                        last.then_inc(p_normed[half], 1)

                    def add_rotated(qk, s):
                        if not there(k, it, s):
                            return
                        T, n = T0 - s, "qk".index(qk)
                        for half in range(2):
                            pool.wait_ge((qT_ps, kT_ps)[n][half], done(T - 1))
                        pool.wait_ge(read[qk], done(T))
                        d, cs, sn = heads(qk_rot[:, n, :]), heads(by_cos[:, n, :]), heads(by_sin[:, n, :])
                        lo, hi = slice(0, D // 2), slice(D // 2, D)
                        g.tensor_tensor(d[:, :, lo], cs[:, :, lo], sn[:, :, hi], ALU.add)
                        g.tensor_tensor(d[:, :, hi], cs[:, :, hi], sn[:, :, lo], ALU.add).then_inc(added[qk], 1)

                    def normalise_k(s):
                        if not there(k, it, s):
                            return
                        T, a = T0 - s, (par - s) % 2
                        pool.wait_ge(added["k"], done(T))
                        pool.wait_ge(norm_step, RSQRT_OPS * T + RSQRT_OPS)
                        kk = heads(qk_rot[:, 1, :])
                        g.tensor_tensor(kk, kk, rnorm[:, a, H:2 * H].unsqueeze(2).broadcast_to([P, H, D]),
                                        ALU.mult).then_inc(k_rotated, 1)

                    normalise_k(1)
                    normalise(0, 2)
                    normalise(1, 2)
                    add_rotated("q", 0)
                    add_rotated("k", 0)

                schedule(pool.Fori, step, 2)

                def group_rsqrt(u, par):
                    inverse_deviations((ln_rs[:, par], NG * l + u, norm_g))

                def x_and_bias(u):
                    pool.wait_ge(x_ready, NT * l + FT * u + NT)
                    g.tensor_tensor(xb[:, :, :], x_cols(u * FT, FT),
                                    b2_row[:, :].unsqueeze(1).broadcast_to([P, FT, C]), ALU.add).then_inc(g_xb, 1)

                pool.wait_ge(norm_g["seed"], done(NG * l + 1))
                both = newton(ln_rs[:, :, :, :].rearrange("p a i t -> p i a t"),
                              three_halves[:, :].unsqueeze(1).broadcast_to([P, 2, FT]))
                for i, op in enumerate(both):
                    if i:
                        pool.wait_ge(norm_g["rsqrt"], passed(NEWTON_OPS * NG * l + 2 * i))
                    op().then_inc(norm_g["rsqrt"], 2)
                pool.wait_ge(w1_hi_ready, l + 1)
                g.tensor_tensor(w1_lo, w1[:, :], w1_hi.bitcast(F32), ALU.subtract).then_inc(w1_ready, 1)
                pool.wait_ge(b2_in, 16 * l + 16)
                pool.wait_ge(x_mid, done(NT * l + NT - 1))
                group_rsqrt(2, 0)
                with pool.Fori(0, (NG - 4) // 2) as it:
                    for par in range(2):
                        x_and_bias(2 * it + par)
                        group_rsqrt(2 * it + par + 3, 1 - par)
                x_and_bias(NG - 4)
                group_rsqrt(NG - 1, 1)
                x_and_bias(NG - 3)
                tables(l + 1)
                x_and_bias(NG - 2)
                x_and_bias(NG - 1)
                for part in range(2):
                    wqk_lower(l + 1, part)

        @block.sync
        def _(sp):
            def load(dst, src, done):
                sp.dma_start(dst, src).then_inc(done, 16)

            def col(ap):
                return ap.rearrange("(p a) -> p a", a=1)

            def row(ap):
                return ap.partition_broadcast(P)

            def batch(b, done):
                load(x_keep[:, b * TPB:(b + 1) * TPB, :], x[b].rearrange("(t p) c -> p t c", p=P), done)

            rotary_at = at["rotary"][0]
            batch(0, x0_in)
            load(cst[:, 0:rotary_at], consts[:, 0:rotary_at], cst_in)
            for i, w in enumerate((Wq, Wk, Wv, Wo)):
                load(w0[:, i, :], w, w0_in)
            load(bq_col[:, :], col(bq), w0_in)
            load(bkv_row[:, 0:C], row(bk), w0_in)
            load(bkv_row[:, C:2 * C], row(bv), w0_in)
            load(bo_row[:, :], row(bo), w0_in)
            for s in counts_tiles:
                sp.sem_inc(s, CREDIT)
            for b in range(1, B):
                batch(b, x_in)
            load(cst[:, rotary_at:], consts[:, rotary_at:], rotary_in)
            sp.wait_ge(zeroed, 4)

            def attention_weights(i):
                layer = bass.ds(i, 1)
                w = Wqkv[layer, :, :].rearrange("l c n -> (l c) n")
                load(wqk, w[:, 0:2 * INNER], wqk_in)
                load(wv[:, :], w[:, 2 * INNER:3 * INNER], wv_in)
                wo = Wout[layer, :, :].rearrange("l (q a d) c -> (l a) d q c", a=2, d=D)
                load(wo_pad[low_rows, :, 0, :], wo[0], wo_in)
                load(wo_pad[high_rows, :, 1, :], wo[1], wo_in)

            def scales(i):
                layer = bass.ds(i, 1)
                load(qk_scales[:, 0, :], row(q_scale[layer, :].rearrange("l d -> (l d)")), sc_in)
                load(qk_scales[:, 1, :], row(k_scale[layer, :].rearrange("l d -> (l d)")), sc_in)

            scales(0)
            attention_weights(0)

            def attention_tokens(l, t, a, written=None):
                tokens, before = x_cols(t), ahead(sp, done(NT * l + t - 2))
                if written is not None:
                    written = ahead(sp, written)
                    sp.wait_ge(x_ready, written)
                sp.wait_ge(xsT_ps, before)
                sp.dma_start(xs[:, a, :], tokens).then_inc(xs_in[a], 16)

            for a in range(2):
                attention_tokens(0, a, a, FT)
            with sp.Fori(0, DEPTH) as l:
                layer = bass.ds(l, 1)
                sp.wait_ge(x_ready, NT * l + NT)
                load(w1[:, 0:2 * F], W1[layer, :, :].rearrange("l c n -> (l c) n"), w1_in)
                wd = W2[layer, :, :].rearrange("l n c -> (l n) c")
                load(w2[:, 0:2, :], wd[0:2 * P, :].rearrange("(i p) c -> p i c", p=P), w2_in)
                load(w2[0:F - 2 * P, 2, :], wd[2 * P:F, :], w2_in)
                bias = b1[layer, :].rearrange("l n -> (l n)")
                for j in range(2):
                    for i, (c, n) in enumerate(FB):
                        load(b1_col[0:n, j, i:i + 1], col(bias[j * F + c:j * F + c + n]), b1_in)
                load(ln_col[:, 0:1], col(ln_g[layer, :].rearrange("l n -> (l n)")), ln_in)
                load(ln_col[:, 1:2], col(ln_b[layer, :].rearrange("l n -> (l n)")), ln_in)
                load(b2_row[:, :], row(b2[layer, :].rearrange("l n -> (l n)")), b2_in)
                after = (l + 1) % DEPTH
                sp.wait_ge(tables_ready, l + 1)
                scales(after)
                with sp.Fori(0, NT // 2 - 1) as it:
                    for a in range(2):
                        attention_tokens(l, (2 * it + 2) + a, a)

                def ffn_tokens(u, par):
                    here, before = x_cols(u * FT, FT), x_tok[:, bass.ds((slot(u * FT) - 1) * C, FT * C)]
                    before = before.rearrange("p (t c) -> p t c", c=C)
                    x4, lo, hi = xs4_pair[:, par], slice(0, C // 2), slice(C // 2, C)
                    tokens = ahead(sp, done(NT * l + FT * u + FT - 1))
                    group_before_last = ahead(sp, done(NG * l + u - 2))
                    sp.wait_ge(x_mid, tokens)
                    sp.wait_ge(g_xn, group_before_last)
                    load(x4[:, :, lo], here[:, :, lo], g_xs[par])
                    load(x4[1:P, :, hi], here[0:P - 1, :, hi], g_xs[par])
                    load(x4[0:1, :, hi], before[P - 1:P, :, hi], g_xs[par])

                last_tile = done(NT * l + NT - 1)
                sp.wait_ge(k_rotated, last_tile)
                for u in range(2):
                    ffn_tokens(u, u)
                for half in range(2):
                    sp.wait_ge(qT_ps[half], last_tile)
                    sp.wait_ge(kT_ps[half], last_tile)
                for w in range(NW):
                    sp.wait_ge(vo_ps[w], last_tile)
                attention_weights(after)
                with sp.Fori(0, NG // 2 - 1) as it:
                    for par in range(2):
                        ffn_tokens((2 * it + 2) + par, par)
                for a in range(2):
                    attention_tokens(l + 1, a, a, NT * l + NT + FT)
            for a in range(2):
                sp.wait_ge(xs_in[a], 8 * NT * DEPTH + 16)
            for b in range(B):
                sp.wait_ge(final_ready, b + 1)
                sp.dma_start(out[b].rearrange("(t p) c -> p t c", p=P),
                             x_keep[:, b * TPB:(b + 1) * TPB, :]).then_inc(out_done, 16)
            sp.wait_ge(out_done, 16 * B)


_INS = ["L0_attn_x", "L0_attn_Wq", "L0_attn_bq", "L0_attn_Wk", "L0_attn_bk", "L0_attn_Wv", "L0_attn_bv",
        "L0_attn_Wo", "L0_attn_bo", "L0_ffn_Wqkv", "L0_ffn_q_scale", "L0_ffn_k_scale", "L0_ffn_Wo",
        "L0_ffn_ln_g", "L0_ffn_ln_b", "L0_ffn_W1", "L0_ffn_b1", "L0_ffn_W2", "L0_ffn_b2"]


def kernel(**inputs):
    import concourse.bacc as bacc
    from concourse.bass_utils import run_bass_kernel_spmd

    nc = bacc.Bacc("TRN2", target_bir_lowering=False, num_devices=1)
    table, at = constants()
    arrays = {"consts": table}
    for name in _INS:
        arrays[name] = np.ascontiguousarray(inputs[name])
    args = [nc.dram_tensor(n, a.shape, mybir.dt.from_np(a.dtype), kind="ExternalInput").ap()
            for n, a in arrays.items()]
    out = nc.dram_tensor("out", (B, N, C), F32, kind="ExternalOutput").ap()
    build(nc, args[0], at, *args[1:], out)
    r = run_bass_kernel_spmd(nc, [arrays], core_ids=[0])
    return r.results[0]["out"]
```
